# Optimizing a Trainium2 kernel written in Bass

```python
import numpy as np
import jax
import jax.numpy as jnp

def _softmax(x, axis=-1):
    return jax.nn.softmax(x, axis=axis)

def _gelu(x):
    return jax.nn.gelu(x, approximate=True)

def _silu(x):
    return jax.nn.silu(x)

def _sigmoid(x):
    return jax.nn.sigmoid(x)

def _layernorm(x, axis=-1, eps=1e-05):
    m = jnp.mean(x, axis=axis, keepdims=True)
    v = jnp.var(x, axis=axis, keepdims=True)
    return (x - m) / jnp.sqrt(v + eps)

def _scatter_add(tgt, idx, src, axis=0):
    return tgt.at[idx].add(src)

def _segment_sum(src, seg, n):
    return jax.ops.segment_sum(src, seg, n)
kernel_name = 'mk_gnn_resnorm_d4_gnn_r32_55a423'

def setup_inputs(seed: int=0):
    np.random.seed(seed)
    _w = jnp.asarray

    def _rec_inputs():
        import jax
        import jax.numpy as jnp
        _gk = jax.random.key(seed)
        x = -0.000202 + 1 * jax.random.normal(jax.random.fold_in(_gk, 1), (3125, 128), jnp.float32)
        _s = jax.random.randint(jax.random.fold_in(_gk, 2), (50000,), 0, 3125, jnp.int32)
        _d = jax.random.randint(jax.random.fold_in(_gk, 3), (50000,), 0, 3125, jnp.int32)
        _loop = jnp.arange(3125, dtype=jnp.int32)
        src = jnp.concatenate([_s, _d, _loop])
        dst = jnp.concatenate([_d, _s, _loop])
        _o = jnp.argsort(dst, stable=True)
        src = src[_o]
        dst = dst[_o]
        edge_type_64 = jax.random.randint(jax.random.fold_in(_gk, 12), (103125,), 0, 64, jnp.int32)
        return (x, src, dst, edge_type_64)
    x, src, dst, edge_type_64 = _rec_inputs()

    def _L0_gnn_setup():
        import jax, jax.numpy as jnp
        import numpy as np
        N = 50000
        E = 18750
        IN = 128
        H = 4
        C = 32
        B = 3
        NEG_SLOPE = 0.2
        key = jax.random.key(seed)
        ks = jax.random.split(key, 6)
        x = jax.random.normal(ks[0], (N, IN), dtype=jnp.float32)
        edge_index = jax.random.randint(ks[1], (2, E), 0, N)
        coeffs_t = jnp.array([0.25, 0.5, 0.25], dtype=jnp.float32)
        glorot_w = float(np.sqrt(2.0) * np.sqrt(6.0 / (H * C + IN)))
        glorot_a = float(np.sqrt(2.0) * np.sqrt(6.0 / (1 + C)))
        lin_weight = jax.random.uniform(ks[2], (B, H * C, IN), jnp.float32, -glorot_w, glorot_w)
        lin_bias = jnp.zeros((B, H * C), dtype=jnp.float32)
        att_src = jax.random.uniform(ks[3], (B, 1, H, C), jnp.float32, -glorot_a, glorot_a)
        att_dst = jax.random.uniform(ks[4], (B, 1, H, C), jnp.float32, -glorot_a, glorot_a)
        return {'x': x, 'edge_index': edge_index, 'coeffs_t': coeffs_t, 'lin_weight': lin_weight, 'lin_bias': lin_bias, 'att_src': att_src, 'att_dst': att_dst}
    _L0_gnn_all = _L0_gnn_setup()
    _L0_gnn_in = {k: v for k, v in _L0_gnn_all.items() if k in ('coeffs_t', 'lin_weight', 'lin_bias', 'att_src', 'att_dst')}
    del _L0_gnn_all

    def _L1_gnn_setup():
        import jax, jax.numpy as jnp
        import numpy as np
        N = 3125
        E = 25000
        D = 128
        OUT = 128
        key = jax.random.key(seed)
        k = jax.random.split(key, 6)
        x = jax.random.normal(k[0], (N, D), dtype=jnp.float32)
        edge_index = jax.random.randint(k[1], (2, E), 0, N, dtype=jnp.int64)
        Wl = jax.random.normal(k[2], (D, OUT), dtype=jnp.float32) / np.sqrt(D)
        bl = jax.random.normal(k[3], (OUT,), dtype=jnp.float32) * 0.01
        Wr = jax.random.normal(k[4], (D, OUT), dtype=jnp.float32) / np.sqrt(D)
        br = jax.random.normal(k[5], (OUT,), dtype=jnp.float32) * 0.01
        return {'x': x, 'edge_index': edge_index, 'Wl': Wl, 'bl': bl, 'Wr': Wr, 'br': br}
    _L1_gnn_all = _L1_gnn_setup()
    _L1_gnn_in = {k: v for k, v in _L1_gnn_all.items() if k in ('Wl', 'bl', 'Wr', 'br')}
    del _L1_gnn_all

    def _L2_gnn_setup():
        import jax, jax.numpy as jnp
        import numpy as np
        N, D, E, L = (50000, 128, 25000, 3)
        key = jax.random.key(seed)
        ks = jax.random.split(key, 4)
        scale = 1.0 / np.sqrt(D)
        x = jax.random.normal(ks[0], (N, D), dtype=jnp.float32)
        edge_index = jax.random.randint(ks[1], (2, E), 0, N, dtype=jnp.int64)
        W1 = jax.random.normal(ks[2], (L, D, D), dtype=jnp.float32) * scale
        W2 = jax.random.normal(ks[3], (L, D, D), dtype=jnp.float32) * scale
        b1 = jnp.zeros((L, D), dtype=jnp.float32)
        b2 = jnp.zeros((L, D), dtype=jnp.float32)
        return {'x': x, 'edge_index': edge_index, 'W1': W1, 'b1': b1, 'W2': W2, 'b2': b2}
    _L2_gnn_all = _L2_gnn_setup()
    _L2_gnn_in = {k: v for k, v in _L2_gnn_all.items() if k in ('W1', 'b1', 'W2', 'b2')}
    del _L2_gnn_all

    def _L3_gnn_setup():
        import jax, jax.numpy as jnp
        import numpy as np
        N_HOPS = 3
        N_ENTITIES = 3125
        EMB = 128
        N_EDGES = 18750
        N_REL = 64
        key = jax.random.key(seed)
        k1, k2, k3, k4, k5, k6 = jax.random.split(key, 6)
        entity_emb = jax.random.normal(k1, (N_ENTITIES, EMB), dtype=jnp.float32)
        edge_emb = jax.random.normal(k2, (N_REL, EMB), dtype=jnp.float32)
        q_w = jax.random.normal(k3, (EMB, EMB), dtype=jnp.float32) * (1.0 / np.sqrt(EMB))
        k_w = jax.random.normal(k4, (EMB, EMB), dtype=jnp.float32) * (1.0 / np.sqrt(EMB))
        edge_index = jax.random.randint(k5, (2, N_EDGES), 0, N_ENTITIES, dtype=jnp.int64)
        edge_type = jax.random.randint(k6, (N_EDGES,), 0, N_REL, dtype=jnp.int64)
        return {'entity_emb': entity_emb, 'edge_emb': edge_emb, 'q_w': q_w, 'k_w': k_w, 'edge_index': edge_index, 'edge_type': edge_type, 'mess_dropout': 0}
    _L3_gnn_all = _L3_gnn_setup()
    _L3_gnn_in = {k: v for k, v in _L3_gnn_all.items() if k in ('edge_emb', 'q_w', 'k_w')}
    del _L3_gnn_all
    return {'x': x, 'src': src, 'dst': dst, 'edge_type_64': edge_type_64, 'L0_gnn_coeffs_t': _L0_gnn_in['coeffs_t'], 'L0_gnn_lin_weight': _L0_gnn_in['lin_weight'], 'L0_gnn_lin_bias': _L0_gnn_in['lin_bias'], 'L0_gnn_att_src': _L0_gnn_in['att_src'], 'L0_gnn_att_dst': _L0_gnn_in['att_dst'], 'L1_gnn_Wl': _L1_gnn_in['Wl'], 'L1_gnn_bl': _L1_gnn_in['bl'], 'L1_gnn_Wr': _L1_gnn_in['Wr'], 'L1_gnn_br': _L1_gnn_in['br'], 'L2_gnn_W1': _L2_gnn_in['W1'], 'L2_gnn_b1': _L2_gnn_in['b1'], 'L2_gnn_W2': _L2_gnn_in['W2'], 'L2_gnn_b2': _L2_gnn_in['b2'], 'L3_gnn_edge_emb': _L3_gnn_in['edge_emb'], 'L3_gnn_q_w': _L3_gnn_in['q_w'], 'L3_gnn_k_w': _L3_gnn_in['k_w']}

def reference(x, src, dst, edge_type_64, L0_gnn_coeffs_t, L0_gnn_lin_weight, L0_gnn_lin_bias, L0_gnn_att_src, L0_gnn_att_dst, L1_gnn_Wl, L1_gnn_bl, L1_gnn_Wr, L1_gnn_br, L2_gnn_W1, L2_gnn_b1, L2_gnn_W2, L2_gnn_b2, L3_gnn_edge_emb, L3_gnn_q_w, L3_gnn_k_w):
    import jax
    import jax.numpy as jnp

    def _L0_gnn_ref(x, edge_index, coeffs_t, lin_weight, lin_bias, att_src, att_dst):
        import jax, jax.numpy as jnp
        import numpy as np
        N = 50000
        E = 18750
        IN = 128
        H = 4
        C = 32
        B = 3
        NEG_SLOPE = 0.2
        W = jnp.einsum('b,boi->oi', coeffs_t, lin_weight)
        bias = jnp.einsum('b,bo->o', coeffs_t, lin_bias)
        a_src = jnp.einsum('b,bqhc->qhc', coeffs_t, att_src)
        a_dst = jnp.einsum('b,bqhc->qhc', coeffs_t, att_dst)
        n = x.shape[0]
        xt = (x @ W.T + bias).reshape(n, H, C)
        alpha_src = jnp.sum(xt * a_src, axis=-1)
        alpha_dst = jnp.sum(xt * a_dst, axis=-1)
        row, col = (edge_index[0], edge_index[1])
        alpha = alpha_src[row] + alpha_dst[col]
        alpha = jax.nn.leaky_relu(alpha, NEG_SLOPE)
        amax = jax.ops.segment_max(alpha, col, num_segments=n)
        ex = jnp.exp(alpha - amax[col])
        denom = jax.ops.segment_sum(ex, col, num_segments=n)
        alpha = ex / (denom[col] + 1e-16)
        msg = xt[row] * alpha[..., None]
        out = jax.ops.segment_sum(msg, col, num_segments=n)
        return out.reshape(n, H * C)

    def _L1_gnn_ref(x, edge_index, Wl, bl, Wr, br):
        import jax, jax.numpy as jnp
        import numpy as np
        N = 3125
        E = 25000
        D = 128
        OUT = 128
        n = x.shape[0]
        tgt = edge_index[0]
        nbr = edge_index[1]
        agg_sum = jax.ops.segment_sum(x[nbr], tgt, num_segments=n)
        deg = jax.ops.segment_sum(jnp.ones((edge_index.shape[1],), x.dtype), tgt, num_segments=n)
        agg = agg_sum / jnp.maximum(deg, 1.0)[:, None]
        out = jax.nn.relu(x @ Wl + bl + agg @ Wr + br)
        norm = jnp.linalg.norm(out, axis=1, keepdims=True) + 1e-06
        return out / norm

    def _L2_gnn_ref(x, edge_index, W1, b1, W2, b2):
        import jax, jax.numpy as jnp
        import numpy as np
        N, D, E, L = (50000, 128, 25000, 3)
        src = edge_index[0]
        dst = edge_index[1]
        n = x.shape[0]
        for l in range(W1.shape[0]):
            agg = x + jax.ops.segment_sum(x[src], dst, num_segments=n)
            h = jnp.maximum(agg @ W1[l] + b1[l], 0.0)
            x = jnp.maximum(h @ W2[l] + b2[l], 0.0)
        return x

    def _L3_gnn_ref(entity_emb, edge_emb, q_w, k_w, edge_index, edge_type, mess_dropout):
        import jax, jax.numpy as jnp
        import numpy as np
        N_HOPS = 3
        N_ENTITIES = 3125
        EMB = 128
        N_EDGES = 18750
        N_REL = 64
        head = edge_index[0]
        tail = edge_index[1]
        rel = edge_emb[edge_type]
        n = entity_emb.shape[0]
        agg = entity_emb
        out = jnp.zeros_like(entity_emb)
        for _ in range(N_HOPS):
            h = agg[head]
            t = agg[tail]
            left = h @ q_w
            right = jnp.tanh(rel * t @ k_w)
            att = jnp.sum(left * right, axis=1)
            seg_max = jax.ops.segment_max(att, head, num_segments=n)
            e = jnp.exp(att - seg_max[head])
            seg_sum = jax.ops.segment_sum(e, head, num_segments=n)
            w = e / seg_sum[head]
            msg = w[:, None] * rel * t
            summed = jax.ops.segment_sum(msg, head, num_segments=n)
            cnt = jax.ops.segment_sum(jnp.ones_like(att), head, num_segments=n)
            agg = summed / jnp.maximum(cnt, 1.0)[:, None]
            norm = jnp.linalg.norm(agg, axis=1, keepdims=True)
            agg = agg / jnp.maximum(norm, 1e-12)
            out = out + agg + entity_emb
        return out
    edge_index = jnp.stack([src, dst])
    x = _layernorm(x + _L0_gnn_ref(x, edge_index, L0_gnn_coeffs_t, L0_gnn_lin_weight, L0_gnn_lin_bias, L0_gnn_att_src, L0_gnn_att_dst), axis=-1)
    x = _layernorm(x + _L1_gnn_ref(x, edge_index, L1_gnn_Wl, L1_gnn_bl, L1_gnn_Wr, L1_gnn_br), axis=-1)
    x = _layernorm(x + _L2_gnn_ref(x, edge_index, L2_gnn_W1, L2_gnn_b1, L2_gnn_W2, L2_gnn_b2), axis=-1)
    x = _layernorm(x + _L3_gnn_ref(x, L3_gnn_edge_emb, L3_gnn_q_w, L3_gnn_k_w, edge_index, edge_type_64, 0), axis=-1)
    return x

_drawn_inputs = setup_inputs


def setup_inputs(seed=0):
    import zlib

    import numpy as np

    out = dict(_drawn_inputs(seed))
    spreads = {'L0_gnn_lin_bias': (0.0, 0.1), 'L2_gnn_b1': (0.0, 0.8), 'L2_gnn_b2': (0.0, 0.1)}
    factors = {'L0_gnn_att_dst': 3.943, 'L1_gnn_bl': 8.0, 'L1_gnn_br': 8.0}
    for name, (base, spread) in spreads.items():
        noise = np.random.default_rng([zlib.crc32(name.encode()), seed]).standard_normal(out[name].shape)
        drawn = base * np.exp(spread * noise) if base else spread * noise
        out[name] = jnp.asarray(drawn.astype(out[name].dtype))
    for name, factor in factors.items():
        out[name] = (out[name] * factor).astype(out[name].dtype)
    return out
```

```python
import concourse.bass as bass
from concourse import mybir
from contextlib import ExitStack, contextmanager

F32 = mybir.dt.float32
BF16 = mybir.dt.bfloat16
F16 = mybir.dt.float16
I32 = mybir.dt.int32
ALU = mybir.AluOpType
ACT = mybir.ActivationFunctionType
AX = mybir.AxisListType

P = 128
N, D, E = 3125, 128, 103125
W = -(-N // P)
NP = W * P
TAIL = N - (W - 1) * P
EP = 125
EC = E // EP
S = 512
J = S // P
NST = (E + W + W * (S - 1)) // S
CH = 400
NCH = NP // CH
MID = 1600
SHIFT = 9
H, C = 4, 32
BIG = 2.0 ** 100
REL = 64
SCAT_BUFS, SCAT_COLS = 3, 11


class Chain:

    def __init__(self, eng, sem):
        self.eng, self.sem, self.base, self.n = eng, sem, 0, 0

    def link(self, ins):
        ins.then_inc(self.sem, 1)
        self.n += 1
        self.eng.wait_ge(self.sem, self.base + self.n)

    @contextmanager
    def loop(self, start, end, links):
        before = self.base + self.n
        with self.eng.Fori(start, end) as i:
            self.base, self.n = i * links + (before - start * links), 0
            yield i
            assert self.n == links, self.n
        self.base, self.n = 0, before + (end - start) * links


def ring(eng, count, bufs, body, chain=None, links=0):
    for t in range(bufs):
        body(t, t, 0)
    full = count // bufs
    if full > 1:
        if chain:
            with chain.loop(1, full, links) as k:
                for b in range(bufs):
                    body(k * bufs + b, b, k)
        else:
            with eng.Fori(1, full) as k:
                for b in range(bufs):
                    body(k * bufs + b, b, k)
    for b in range(count - full * bufs):
        body(full * bufs + b, b, full)


def used(k):
    return not (isinstance(k, int) and k == 0)


class Core:
    stages = 0
    kept = {}

    def __init__(self, nc, ctx, tag, again=None):
        Core.stages += 1
        self.nc, self.ctx, self.tag, self.again = nc, ctx, f"{tag}{Core.stages}", again
        self.mine = []
        if again:
            ctx.callback(self.clear)

    def sb(self, name, shape, dt=F32):
        return self.ctx.enter_context(self.nc.sbuf_tensor(f"{self.tag}_{name}", shape, dt))

    def ps(self, name, shape, dt=F32):
        return self.ctx.enter_context(self.nc.psum_tensor(f"{self.tag}_{name}", shape, dt))

    def sem(self, name, fresh=False):
        if self.again and not fresh:
            key = (id(self.nc), self.again, name)
            if key not in Core.kept:
                Core.kept[key] = self.nc.alloc_semaphore(f"{self.again}_{name}")
            self.mine.append(Core.kept[key])
            return Core.kept[key]
        return self.nc.alloc_semaphore(f"{self.tag}_{name}")

    def clear(self):
        with self.nc.Block() as block:
            @block.sync
            def _(sp):
                for s in self.mine:
                    sp.sem_clear(s)


def build_constants(nc, k):
    with ExitStack() as ctx:
        m = Core(nc, ctx, "const")
        diff = m.sb("diff", [P, P], I32)
        node = m.sb("node", [P, P], I32)
        steps = m.sb("steps", [P, NST + 1], I32)
        part = m.sb("part", [P, 1], I32)
        iotas_written = m.sem("iotas_written")
        dve_step = m.sem("dve_step")
        block = ctx.enter_context(nc.Block())

        @block.gpsimd
        def _(pool):
            nc.gpsimd.iota(diff[:, :], [[1, P]], base=0, channel_multiplier=-1).then_inc(iotas_written, 1)
            nc.gpsimd.iota(node[:, :], [[1, P]], base=0, channel_multiplier=0).then_inc(iotas_written, 1)
            nc.gpsimd.iota(steps[:, :], [[1, NST + 1]], base=0, channel_multiplier=0).then_inc(iotas_written, 1)
            nc.gpsimd.iota(part[:, :], [[0, 1]], base=0, channel_multiplier=1).then_inc(iotas_written, 1)

        @block.vector
        def _(dve):
            c = Chain(dve, dve_step)
            dve.wait_ge(iotas_written, 4)
            nc.vector.tensor_scalar(k.ident[:, :], diff[:, :], 0, None, ALU.is_equal).then_inc(dve_step, 1)
            nc.vector.tensor_scalar(k.identb[:, :], diff[:, :], 0, None, ALU.is_equal).then_inc(dve_step, 1)
            nc.vector.tensor_scalar(k.ident_neg[:, :], diff[:, :], 0, -BIG, ALU.is_equal, ALU.mult).then_inc(dve_step, 1)
            nc.vector.tensor_scalar(k.tri[:, :], diff[:, :], 0, None, ALU.is_gt).then_inc(dve_step, 1)
            nc.vector.tensor_copy(k.node[:, :], node[:, :]).then_inc(dve_step, 1)
            nc.vector.tensor_copy(k.steps[:, :], steps[:, :]).then_inc(dve_step, 1)
            nc.vector.tensor_copy(k.part[:, :], part[:, :]).then_inc(dve_step, 1)
            nc.vector.memset(k.ones[:, :], 1.0).then_inc(dve_step, 1)


def sort_edges(nc, p, d, k):
    with ExitStack() as ctx:
        m = Core(nc, ctx, "sort")
        src = m.sb("src", [EP, EC], I32)
        dst = m.sb("dst", [EP, EC], I32)
        typ = m.sb("typ", [EP, EC], I32)
        tmp_i = m.sb("tmp_i", [EP, EC], I32)
        rec = m.sb("rec", [EP, EC, 4])
        win = m.sb("win", [EP, EC])
        mask = m.sb("mask", [EP, EC])
        run = m.sb("run", [EP, EC])
        zero = m.sb("zero", [EP, EC])
        pos = m.sb("pos", [EP, EC])
        pos_i = m.sb("pos_i", [EP, EC], I32)
        cur = m.sb("cur", [P, 1])
        off_a = m.sb("off_a", [P, 1])
        tot = m.sb("tot", [EP, W])
        nst = m.sb("nst", [P, W])
        nst_i = m.sb("nst_i", [P, W], I32)
        ends = m.sb("ends", [P, W])
        off = m.sb("off", [P, W])
        wst = m.sb("wst", [P, NST + 1])
        empty = m.sb("empty", [P, NST * J, 4])
        st_rec = [m.sb(f"st_rec{b}", [EP, SCAT_COLS, 4], I32) for b in range(SCAT_BUFS)]
        st_pos = [m.sb(f"st_pos{b}", [EP, SCAT_COLS], I32) for b in range(SCAT_BUFS)]
        before_ps = m.ps("before_ps", [P, W])
        total_ps = m.ps("total_ps", [P, W])
        edges_in = m.sem("edges_in")
        empties_set = m.sem("empties_set")
        empties_out = m.sem("empties_out")
        dve_step = m.sem("dve_step")
        totals_ready = m.sem("totals_ready")
        prefix_ready = m.sem("prefix_ready")
        staged = m.sem("staged")
        issue_step = m.sem("issue_step")
        scattered = [m.sem(f"scattered{b}") for b in range(SCAT_BUFS)]
        rounds = EC // (SCAT_BUFS * SCAT_COLS)
        block = ctx.enter_context(nc.Block())

        @block.sync
        def _(sp):
            for name, to in (("src", src), ("dst", dst), ("edge_type_64", typ)):
                sp.dma_start(to[:, :], p[name].rearrange("(p t) -> p t", p=EP)).then_inc(edges_in, 16)
            sp.wait_ge(empties_set, 2)
            sp.dma_start(d.slots.rearrange("(p t) f -> p t f", p=P), empty[:, :, :].bitcast(I32)).then_inc(empties_out, 16)
            sp.wait_ge(empties_out, 16)

        @block.gpsimd
        def _(pool):
            nc.gpsimd.memset(empty[:, :, :], 0.0).then_inc(empties_set, 1)
            pool.wait_ge(empties_set, 1)
            nc.gpsimd.memset(empty[:, :, 0:1], -1.0).then_inc(empties_set, 1)
            pool.wait_ge(empties_out, 16)

            def scatter(t, b, kk):
                pool.wait_ge(staged, (t + 1) * 2)
                pool.sem_inc(issue_step, 1)
                for j in range(SCAT_COLS):
                    pool.indirect_dma_start(d.slots, bass.IndirectOffsetOnAxis(ap=st_pos[b][:, j:j + 1], axis=0),
                                            st_rec[b][:, j, :], None).then_inc(scattered[b], 16)
            ring(pool, rounds * SCAT_BUFS, SCAT_BUFS, scatter)
            for b in range(SCAT_BUFS):
                pool.wait_ge(scattered[b], 16 * SCAT_COLS * rounds)

        @block.tensor
        def _(pe):
            pe.wait_ge(totals_ready, 1)
            nc.tensor.matmul(before_ps[0:EP, :], k.tri[0:EP, 0:EP], tot[:, :], start=True, stop=True).then_inc(prefix_ready, 1)
            nc.tensor.matmul(total_ps[:, :], k.ones[0:EP, :], tot[:, :], start=True, stop=True).then_inc(prefix_ready, 1)

        @block.vector
        def _(dve):
            c = Chain(dve, dve_step)
            c.link(nc.vector.memset(cur[:, :], 0.0))
            c.link(nc.vector.memset(zero[:, :], 0.0))
            c.link(nc.vector.memset(pos[:, :], 0.0))
            c.link(nc.vector.memset(wst[:, :], 0.0))
            dve.wait_ge(edges_in, 48)
            c.link(nc.vector.tensor_scalar(tmp_i[:, :], src[:, :], P - 1, None, ALU.bitwise_and))
            c.link(nc.vector.tensor_copy(rec[:, :, 0], tmp_i[:, :]))
            c.link(nc.vector.tensor_scalar(rec[:, :, 1], dst[:, :], -float(MID), None, ALU.add))
            c.link(nc.vector.tensor_copy(rec[:, :, 2], typ[:, :]))
            c.link(nc.vector.tensor_copy(rec[:, :, 3].bitcast(I32), dst[:, :]))
            c.link(nc.vector.tensor_scalar(tmp_i[:, :], src[:, :], 7, None, ALU.logical_shift_right))
            c.link(nc.vector.tensor_copy(win[:, :], tmp_i[:, :]))
            with c.loop(0, W, 3) as a:
                c.link(nc.vector.tensor_scalar(mask[:, :], win[:, :], cur[0:EP, :], None, ALU.is_equal))
                c.link(nc.vector.tensor_reduce(tot[:, bass.ds(a, 1)], mask[:, :], AX.X, ALU.add))
                c.link(nc.vector.tensor_scalar(cur[:, :], cur[:, :], 1.0, None, ALU.add))
            c.link(nc.vector.memset(cur[:, :], 0.0))
            nc.vector.memset(nst[:, :], 0.0).then_inc(totals_ready, 1)
            dve.wait_ge(prefix_ready, 2)
            c.link(nc.vector.tensor_scalar(nst_i[:, :], total_ps[:, :], 1.0, S - 1.0, ALU.max, ALU.add))
            c.link(nc.vector.tensor_scalar(nst_i[:, :], nst_i[:, :], SHIFT, None, ALU.logical_shift_right))
            c.link(nc.vector.tensor_copy(nst[:, :], nst_i[:, :]))
            c.link(nc.vector.tensor_tensor_scan(ends[:, :], nst[:, :], zero_row(k), 0.0, ALU.add, ALU.add))
            c.link(nc.vector.tensor_tensor(off[:, :], ends[:, :], nst[:, :], ALU.subtract))
            c.link(nc.vector.tensor_scalar(off[:, :], off[:, :], float(S), -1.0, ALU.mult, ALU.add))
            c.link(nc.vector.tensor_tensor(off[0:EP, :], off[0:EP, :], before_ps[0:EP, :], ALU.add))
            with c.loop(0, W, 6) as a:
                c.link(nc.vector.tensor_scalar(mask[:, :], win[:, :], cur[0:EP, :], None, ALU.is_equal))
                c.link(nc.vector.tensor_copy(off_a[0:EP, :], off[0:EP, bass.ds(a, 1)]))
                c.link(nc.vector.tensor_tensor_scan(run[:, :], mask[:, :], zero[:, :], off_a[0:EP, :], ALU.add, ALU.add))
                c.link(nc.vector.tensor_tensor(run[:, :], run[:, :], mask[:, :], ALU.mult))
                c.link(nc.vector.tensor_tensor(pos[:, :], pos[:, :], run[:, :], ALU.add))
                c.link(nc.vector.tensor_scalar(cur[:, :], cur[:, :], 1.0, None, ALU.add))
            c.link(nc.vector.tensor_copy(pos_i[:, :], pos[:, :]))

            def stage(t, b, kk):
                if used(kk):
                    dve.wait_ge(scattered[b], kk * 16 * SCAT_COLS)
                nc.vector.tensor_scalar(st_pos[b][:, :], pos_i[:, bass.ds(t * SCAT_COLS, SCAT_COLS)], 0, None,
                                        ALU.bitwise_or).then_inc(staged, 1)
                nc.vector.tensor_scalar(st_rec[b][:, :, :], rec[:, bass.ds(t * SCAT_COLS, SCAT_COLS), :].bitcast(I32), 0,
                                        None, ALU.bitwise_or).then_inc(staged, 1)
            ring(dve, rounds * SCAT_BUFS, SCAT_BUFS, stage)
            with c.loop(0, W, 2) as a:
                c.link(nc.vector.tensor_copy(off_a[:, :], ends[:, bass.ds(a, 1)]))
                c.link(nc.vector.scalar_tensor_tensor(wst[:, :], k.steps[:, :], off_a[:, :], wst[:, :], ALU.is_ge, ALU.add))
            c.link(nc.vector.tensor_copy(k.window_of[:, :], wst[:, 0:NST]))
            c.link(nc.vector.tensor_tensor(k.last_of[:, :], wst[:, 0:NST], wst[:, 1:NST + 1], ALU.not_equal))
            c.link(nc.vector.memset(k.keep[:, :, :], 0.0))
            c.link(nc.vector.tensor_tensor(k.keep[:, 1:NST, 0], wst[:, 0:NST - 1], wst[:, 1:NST], ALU.is_equal))
            c.link(nc.vector.tensor_scalar(k.keep[:, :, 1], k.keep[:, :, 0], 1.5 * BIG, -0.5 * BIG, ALU.mult, ALU.add))


def zero_row(k):
    return k.zeros[:, 0:W]


def count_pairs(nc, d, k):
    with ExitStack() as ctx:
        m = Core(nc, ctx, "count")
        tail_i = m.sb("tail_i", [P, NP], I32)
        tail = m.sb("tail", [P, NP], F16)
        iota_written = m.sem("iota_written")
        tail_set = m.sem("tail_set")
        rec = [m.sb(f"rec{b}", [P, J, 4]) for b in range(2)]
        head_hot = [m.sb(f"head_hot{b}", [P, J, P], BF16) for b in range(2)]
        tail_hot = [m.sb(f"tail_hot{b}", [P, J, NP], BF16) for b in range(2)]
        cum = [m.sb(f"cum{b}", [P, NP]) for b in range(2)]
        acc = m.ps("acc", [P, NCH, 512])
        rec_in = [m.sem(f"rec_in{b}") for b in range(2)]
        hot_ready = m.sem("hot_ready")
        counted = m.sem("counted")
        cleared = m.sem("cleared")
        copied = m.sem("copied")
        cum_out = [m.sem(f"cum_out{b}") for b in range(2)]
        block = ctx.enter_context(nc.Block())
        slots = d.slots.rearrange("(s p j) f -> s p (j f)", p=P, j=J)

        @block.sync
        def _(sp):
            def step(t, b, kk):
                if used(kk):
                    sp.wait_ge(hot_ready, (t - 1) * 2 * J)
                sp.dma_start(rec[b][:, :, :].rearrange("p j f -> p (j f)").bitcast(I32), slots[bass.ds(t, 1), :, :].rearrange("s p f -> p (s f)")).then_inc(rec_in[b], 16)
            ring(sp, NST, 2, step)

        @block.gpsimd
        def _(pool):
            nc.gpsimd.iota(tail_i[:, :], [[1, NP]], base=-MID, channel_multiplier=0).then_inc(iota_written, 1)

            def step(t, b, kk):
                w = pool.value_load(k.window_of[0:1, bass.ds(t, 1)], min_val=0, max_val=W)
                last = pool.value_load(k.last_of[0:1, bass.ds(t, 1)], min_val=0, max_val=1)
                pool.wait_ge(copied, (t + 1) * NCH)
                pool.sem_inc(k.issue, 1)
                pool.dma_start(d.cum[bass.ds(w, 1), :, :].rearrange("s p f -> p (s f)"), cum[b][:, :], cond=last).then_inc(cum_out[b], 16)
            ring(pool, NST, 2, step)
            for b in range(2):
                pool.wait_ge(cum_out[b], 16 * (NST // 2))

        @block.vector
        def _(dve):
            dve.wait_ge(iota_written, 1)
            nc.vector.tensor_copy(tail[:, :], tail_i[:, :]).then_inc(tail_set, 1)
            dve.wait_ge(tail_set, 1)

            def step(t, b, kk):
                dve.wait_ge(rec_in[b], (kk + 1) * 16)
                if used(kk):
                    dve.wait_ge(counted, (t - 1) * NCH)
                for j in range(J):
                    nc.vector.tensor_scalar(head_hot[b][:, j, :], k.node[:, :], rec[b][:, j, 0:1], None,
                                            ALU.is_equal).then_inc(hot_ready, 1)
                for j in range(J):
                    nc.vector.tensor_scalar(tail_hot[b][:, j, :], tail[:, :], rec[b][:, j, 1:2], None,
                                            ALU.is_equal).then_inc(hot_ready, 1)
            ring(dve, NST, 2, step)

        @block.tensor
        def _(pe):
            for c in range(NCH):
                nc.tensor.matmul(acc[:, c, 0:CH], k.zerosb[:, 0:P], k.zerosb[:, 0:CH], start=True, stop=False,
                                 skip_group_check=True).then_inc(cleared, 1)

            def step(t, b, kk):
                pe.wait_ge(hot_ready, (t + 1) * 2 * J)
                for c in range(NCH):
                    if used(kk) or b:
                        pe.wait_ge(copied, (t - 1) * NCH + c + 1)
                    for j in range(J):
                        mm = nc.tensor.matmul(acc[:, c, 0:CH], head_hot[b][:, j, :], tail_hot[b][:, j, c * CH:(c + 1) * CH],
                                              start=False, stop=False, skip_group_check=True)
                    mm.then_inc(counted, 1)
            ring(pe, NST, 2, step)

        @block.scalar
        def _(act):
            def step(t, b, kk):
                if used(kk):
                    act.wait_ge(cum_out[b], kk * 16)
                for c in range(NCH):
                    act.wait_ge(counted, t * NCH + c + 1)
                    nc.scalar.copy(cum[b][:, c * CH:(c + 1) * CH], acc[:, c, 0:CH]).then_inc(copied, 1)
            ring(act, NST, 2, step)


def split_counts(nc, d, k):
    B = 3
    G = -(-W // 4)
    with ExitStack() as ctx:
        m = Core(nc, ctx, "split")
        cum = [m.sb(f"cum{b}", [P, NP]) for b in range(B)]
        cnt = [m.sb(f"cnt{b}", [P, NP]) for b in range(B)]
        cntT = [m.sb(f"cntT{b}", [P, NP]) for b in range(B)]
        ps = m.ps("ps", [P, G, 512])
        cum_in = [m.sem(f"cum_in{b}") for b in range(B)]
        cnt_ready = m.sem("cnt_ready")
        turned = m.sem("turned")
        turned_copied = m.sem("turned_copied")
        degree_ready = m.sem("degree_ready")
        cnt_out = [m.sem(f"cnt_out{b}") for b in range(B)]
        cntT_out = [m.sem(f"cntT_out{b}") for b in range(B)]
        block = ctx.enter_context(nc.Block())
        cntT_cols = d.cntT.rearrange("j p (w n) -> p j w n", n=P)

        @block.sync
        def _(sp):
            def load(t, b, kk):
                if used(kk):
                    sp.wait_ge(cnt_ready, t - 1)
                sp.dma_start(cum[b][:, :], d.cum[bass.ds(t, 1), :, :].rearrange("s p f -> p (s f)")).then_inc(cum_in[b], 16)
            ring(sp, W, B, load)

        @block.gpsimd
        def _(pool):
            def store(t, b, kk):
                pool.wait_ge(cnt_ready, t + 1)
                pool.sem_inc(k.issue, 1)
                pool.dma_start(d.cnt[bass.ds(t, 1), :, :].rearrange("s p f -> p (s f)"), cnt[b][:, :]).then_inc(cnt_out[b], 16)
                pool.wait_ge(turned_copied, (t + 1) * G)
                pool.sem_inc(k.issue, 1)
                pool.dma_start(cntT_cols[:, :, bass.ds(t, 1), :].rearrange("p j w n -> p (j w) n"),
                               cntT[b][:, :].rearrange("p (j n) -> p j n", n=P)).then_inc(cntT_out[b], 16)
            ring(pool, W, B, store)
            for b in range(B):
                pool.wait_ge(cnt_out[b], 16 * ((W + B - 1 - b) // B))
                pool.wait_ge(cntT_out[b], 16 * ((W + B - 1 - b) // B))

        @block.vector
        def _(dve):
            def step(t, b, kk):
                dve.wait_ge(cum_in[b], (kk + 1) * 16)
                if used(kk):
                    dve.wait_ge(cnt_out[b], kk * 16)
                    dve.wait_ge(turned, (t - B + 1) * G)
                    dve.wait_ge(degree_ready, t - B + 1)
                if used(kk) or b:
                    nc.vector.tensor_tensor(cnt[b][:, :], cum[b][:, :], cum[(b - 1) % B][:, :], ALU.subtract).then_inc(cnt_ready, 1)
                else:
                    nc.vector.tensor_copy(cnt[b][:, :], cum[b][:, :]).then_inc(cnt_ready, 1)
                dve.wait_ge(cnt_ready, t + 1)
                nc.vector.tensor_reduce(k.degree[:, bass.ds(t, 1)], cnt[b][:, :], AX.X, ALU.add).then_inc(degree_ready, 1)
            ring(dve, W, B, step)

        @block.tensor
        def _(pe):
            def step(t, b, kk):
                pe.wait_ge(cnt_ready, t + 1)
                for g in range(G):
                    if used(kk) or b:
                        pe.wait_ge(turned_copied, (t - 1) * G + g + 1)
                    for j in range(4 * g, min(4 * g + 4, W)):
                        mm = nc.tensor.transpose(ps[:, g, (j % 4) * P:(j % 4 + 1) * P], cnt[b][:, j * P:(j + 1) * P], k.ident[:, :])
                    mm.then_inc(turned, 1)
            ring(pe, W, B, step)

        @block.scalar
        def _(act):
            def step(t, b, kk):
                if used(kk):
                    act.wait_ge(cntT_out[b], kk * 16)
                for g in range(G):
                    n = min(4, W - 4 * g) * P
                    act.wait_ge(turned, t * G + g + 1)
                    nc.scalar.copy(cntT[b][:, g * 512:g * 512 + n], ps[:, g, 0:n]).then_inc(turned_copied, 1)
            ring(act, W, B, step)


def bc(ap, shape):
    return ap.broadcast_to(shape)


def turn(nc, k, nodes, cols, tag):
    G = -(-W // 4)
    with ExitStack() as ctx:
        m = Core(nc, ctx, tag, again="turn")
        ps = m.ps("ps", [P, G, 512])
        turned = m.sem("turned")
        block = ctx.enter_context(nc.Block())

        @block.tensor
        def _(pe):
            for w in range(W):
                mm = nc.tensor.transpose(ps[:, w // 4, (w % 4) * P:(w % 4 + 1) * P], nodes[:, w * P:(w + 1) * P], k.ident[:, :])
                if w % 4 == 3 or w == W - 1:
                    mm.then_inc(turned, 1)

        @block.scalar
        def _(act):
            for g in range(G):
                n = min(4, W - 4 * g) * P
                act.wait_ge(turned, g + 1)
                nc.scalar.copy(cols[:, g * 512:g * 512 + n], ps[:, g, 0:n])


def load_inputs(nc, p, k):
    with ExitStack() as ctx:
        m = Core(nc, ctx, "load")
        cleared = m.sem("cleared")
        x_in = m.sem("x_in")
        block = ctx.enter_context(nc.Block())

        @block.vector
        def _(dve):
            nc.vector.memset(k.x[:, :], 0.0).then_inc(cleared, 1)

        @block.sync
        def _(sp):
            sp.wait_ge(cleared, 1)
            x = k.x[:, :].rearrange("p (w d) -> p w d", d=D)
            sp.dma_start(x[:, 0:W - 1, :], p['x'][0:(W - 1) * P, :].rearrange("(w p) d -> p w d", p=P)).then_inc(x_in, 16)
            sp.dma_start(x[0:TAIL, W - 1, :], p['x'][(W - 1) * P:N, :]).then_inc(x_in, 16)
            sp.wait_ge(x_in, 32)


def attention_project(nc, p, d, k, xT, row_s, row_d):
    G = -(-W // 4)
    with ExitStack() as ctx:
        m = Core(nc, ctx, "proj")
        coef = m.sb("coef", [P, 3])
        lw = m.sb("lw", [P, 3, D])
        raw = {n: m.sb(n, [P, 3, D]) for n in ("bias", "att_src", "att_dst")}
        mixed = {n: m.sb(n + "_mix", [P, D]) for n in ("weight", "bias", "att_src", "att_dst")}
        names = ["weight", "bias", "att_src", "att_dst"]
        flipped = {n: m.sb(n + "_T", [P, D]) for n in names}
        ge = m.sb("ge", [P, H + 1])
        head_s = m.sb("head_s", [P, H, P])
        head_d = m.sb("head_d", [P, H, P])
        xt = m.sb("xt", [P, NP])
        xtT = m.sb("xtT", [P, NP])
        tmp = xT
        flag = m.sb("flag", [P, 1])
        lhs = m.sb("lhs", [P, W, k.LHS])
        ps = m.ps("ps", [P, NCH, 512])
        params_in = m.sem("params_in")
        mixes_ready = m.sem("mixes_ready")
        flips = m.sem("flips")
        flips_ready = m.sem("flips_ready")
        xt_summed = m.sem("xt_summed")
        xt_ready = m.sem("xt_ready")
        xtT_summed = m.sem("xtT_summed")
        xtT_ready = m.sem("xtT_ready")
        row_summed = m.sem("row_summed")
        row_ready = m.sem("row_ready")
        dve_step = m.sem("dve_step")
        lhs_ready = m.sem("lhs_ready")
        lhs_out = m.sem("lhs_out")
        block = ctx.enter_context(nc.Block())

        @block.sync
        def _(sp):
            sp.dma_start(coef[:, :], p['L0_gnn_coeffs_t'].partition_broadcast(P)).then_inc(params_in, 16)
            sp.dma_start(lw[:, :, :], p['L0_gnn_lin_weight'].rearrange("b o i -> o b i")).then_inc(params_in, 16)
            sp.dma_start(raw["bias"][:, :, :], p['L0_gnn_lin_bias'].partition_broadcast(P)).then_inc(params_in, 16)
            for n in ("att_src", "att_dst"):
                sp.dma_start(raw[n][:, :, :], p['L0_gnn_' + n].rearrange("b q h c -> (b q) (h c)").partition_broadcast(P)).then_inc(params_in, 16)
            sp.wait_ge(lhs_ready, 1)
            sp.dma_start(d.lhs.rearrange("w p f -> p w f"), lhs[:, :, :]).then_inc(lhs_out, 16)
            sp.wait_ge(lhs_out, 16)

        @block.tensor
        def _(pe):
            pe.wait_ge(mixes_ready, 1)
            for n, name in enumerate(names):
                mm = nc.tensor.transpose(ps[:, 7, n * P:(n + 1) * P], mixed[name][:, :], k.ident[:, :])
            mm.then_inc(flips, 1)
            pe.wait_ge(flips_ready, 1)
            for w in range(W):
                mm = nc.tensor.matmul(ps[:, w // 4, (w % 4) * P:(w % 4 + 1) * P], xT[:, w * P:(w + 1) * P],
                                      flipped["weight"][:, :], start=True, stop=True)
                if w % 4 == 3 or w == W - 1:
                    mm.then_inc(xt_summed, 1)
            for c in range(NCH):
                if c < G:
                    pe.wait_ge(xt_ready, c + 1)
                nc.tensor.matmul(ps[:, c, 0:CH], flipped["weight"][:, :], xT[:, c * CH:(c + 1) * CH], start=True,
                                 stop=True).then_inc(xtT_summed, 1)
            pe.wait_ge(xtT_ready, NCH)
            for r in range(2 * H):
                for c in range(NCH):
                    if r:
                        pe.wait_ge(row_ready, (r - 1) * NCH + c + 1)
                    nc.tensor.matmul(ps[:, c, 0:CH], (head_s if r < H else head_d)[:, r % H, :],
                                     xtT[:, c * CH:(c + 1) * CH], start=True, stop=True).then_inc(row_summed, 1)

        @block.scalar
        def _(act):
            act.wait_ge(flips_ready, 1)
            for c in range(NCH):
                act.wait_ge(xtT_summed, c + 1)
                nc.scalar.activation(xtT[:, c * CH:(c + 1) * CH], ps[:, c, 0:CH], ACT.Identity,
                                     bias=flipped["bias"][:, 0:1]).then_inc(xtT_ready, 1)
            for r in range(2 * H):
                for c in range(NCH):
                    act.wait_ge(row_summed, r * NCH + c + 1)
                    nc.scalar.copy((row_s if r < H else row_d)[:, r % H, c * CH:(c + 1) * CH], ps[:, c, 0:CH]).then_inc(row_ready, 1)

        @block.vector
        def _(dve):
            c = Chain(dve, dve_step)
            c.link(nc.vector.memset(lhs[:, :, :], 0.0))
            dve.wait_ge(params_in, 5 * 16)
            for name in names:
                r = lw if name == "weight" else raw[name]
                c.link(nc.vector.tensor_scalar(mixed[name][:, :], r[:, 0, :], coef[:, 0:1], None, ALU.mult))
                for b in (1, 2):
                    c.link(nc.vector.scalar_tensor_tensor(mixed[name][:, :], r[:, b, :], coef[:, b:b + 1],
                                                          mixed[name][:, :], ALU.mult, ALU.add))
            c.link(nc.vector.tensor_scalar(ge[:, :], k.steps[:, 0:H + 1], float(C), k.part[:, 0:1], ALU.mult, ALU.is_le))
            c.link(nc.vector.tensor_tensor(ge[:, 0:H], ge[:, 0:H], ge[:, 1:H + 1], ALU.subtract))
            nc.vector.tensor_copy(flag[:, :], ge[:, 0:1]).then_inc(mixes_ready, 1)
            dve.wait_ge(flips, 1)
            for n, name in enumerate(names):
                c.link(nc.vector.tensor_copy(flipped[name][:, :], ps[:, 7, n * P:(n + 1) * P]))
            for h in range(H):
                c.link(nc.vector.tensor_scalar(head_s[:, h, :], flipped["att_src"][:, :], ge[:, h:h + 1], None, ALU.mult))
                c.link(nc.vector.tensor_scalar(head_d[:, h, :], flipped["att_dst"][:, :], ge[:, h:h + 1], None, ALU.mult))
            nc.vector.tensor_copy(flag[:, :], ge[:, 0:1]).then_inc(flips_ready, 1)
            for g in range(G):
                n = min(4, W - 4 * g)
                dve.wait_ge(xt_summed, g + 1)
                nc.vector.tensor_tensor(xt[:, g * 512:g * 512 + n * P].rearrange("p (w f) -> p w f", f=P),
                                        ps[:, g, 0:n * P].rearrange("p (w f) -> p w f", f=P),
                                        bc(mixed["bias"][:, None, :], [P, n, P]), ALU.add).then_inc(xt_ready, 1)
            dve.wait_ge(xt_ready, G)
            dve.wait_ge(xtT_summed, NCH)
            xt3 = xt[:, :].rearrange("p (w f) -> p w f", f=P)
            tmp3 = tmp[:, :].rearrange("p (w f) -> p w f", f=P)
            for name, to in (("att_src", k.col_s), ("att_dst", k.col_d)):
                c.link(nc.vector.tensor_tensor(tmp3, xt3, bc(mixed[name][:, None, :], [P, W, P]), ALU.mult))
                c.link(nc.vector.tensor_reduce(to[:, :], tmp[:, :].rearrange("p (w c) -> p w c", c=C), AX.X, ALU.add))
            HW = C + 1
            for h in range(H):
                at = h * 3 * HW + h * HW if h < 3 else 9 * HW
                c.link(nc.vector.tensor_copy(lhs[:, :, at:at + C], xt3[:, :, h * C:(h + 1) * C]))
                c.link(nc.vector.memset(lhs[:, :, at + C:at + HW], 1.0))
            cs = k.col_s[:, :].rearrange("p (w h) -> p w h", h=H)
            c.link(nc.vector.tensor_copy(lhs[:, :, 10 * HW:10 * HW + H], cs))
            nc.vector.tensor_scalar(lhs[:, :, 10 * HW + H:10 * HW + 2 * H], cs, 0.2, None, ALU.mult).then_inc(lhs_ready, 1)


def attention_max(nc, d, k, row_s):
    with ExitStack() as ctx:
        m = Core(nc, ctx, "amax")
        cnt = [m.sb(f"cnt{b}", [P, NP]) for b in range(2)]
        masked = m.sb("masked", [P, NP])
        spare = m.sb("spare", [P, NP])
        z = m.sb("z", [P, W * H])
        cnt_in = [m.sem(f"cnt_in{b}") for b in range(2)]
        masks_made = m.sem("masks_made")
        dve_step = m.sem("dve_step")
        block = ctx.enter_context(nc.Block())

        @block.sync
        def _(sp):
            def load(t, b, kk):
                if used(kk):
                    sp.wait_ge(masks_made, t - 1)
                sp.dma_start(cnt[b][:, :], d.cntT[bass.ds(t, 1), :, :].rearrange("s p f -> p (s f)")).then_inc(cnt_in[b], 16)
            ring(sp, W, 2, load)

        @block.vector
        def _(dve):
            c = Chain(dve, dve_step)

            def step(t, b, kk):
                dve.wait_ge(cnt_in[b], (kk + 1) * 16)
                nc.vector.tensor_scalar(masked[:, :], cnt[b][:, :], 0.0, -BIG, ALU.is_equal, ALU.mult).then_inc(masks_made, 1)
                dve.wait_ge(masks_made, t + 1)
                for h in range(H):
                    c.link(nc.vector.tensor_tensor(spare[:, :], masked[:, :], row_s[:, h, :], ALU.add))
                    c.link(nc.vector.tensor_reduce(k.amax[:, bass.ds(t * H + h, 1)], spare[:, :], AX.X, ALU.max))
            ring(dve, W, 2, step, c, 2 * 2 * H)
            c.link(nc.vector.tensor_tensor(z[:, :], k.amax[:, :], k.col_d[:, :], ALU.add))
            c.link(nc.vector.scalar_tensor_tensor(k.amax[:, :], z[:, :], 0.2, z[:, :], ALU.mult, ALU.max))


def attention_rows(nc, k, row_d, pos_row, neg_row, w0, n):
    with ExitStack() as ctx:
        m = Core(nc, ctx, "rows", again="rows")
        ps = m.ps("ps", [P, 8, 512])
        spread = m.sem("spread")
        rows_made = m.sem("rows_made")
        block = ctx.enter_context(nc.Block())
        groups = [(h, g) for h in range(H) for g in range(0, n, 4)]

        @block.tensor
        def _(pe):
            for i, (h, g) in enumerate(groups):
                if i >= 8:
                    pe.wait_ge(rows_made, 2 * (i - 7))
                for j in range(g, min(g + 4, n)):
                    col = k.amax[:, (w0 + j) * H + h:(w0 + j) * H + h + 1]
                    mm = nc.tensor.matmul(ps[:, i % 8, (j - g) * P:(j - g + 1) * P], bc(col, [P, P]), k.ident[:, :],
                                          start=True, stop=True)
                mm.then_inc(spread, 1)

        @block.vector
        def _(dve):
            for i, (h, g) in enumerate(groups):
                q = min(4, n - g) * P
                dve.wait_ge(spread, i + 1)
                r = row_d[:, h, (w0 + g) * P:(w0 + g) * P + q]
                nc.vector.tensor_tensor(pos_row[:, h, g * P:g * P + q], r, ps[:, i % 8, 0:q], ALU.subtract).then_inc(rows_made, 1)
                nc.vector.scalar_tensor_tensor(neg_row[:, h, g * P:g * P + q], r, 0.2, ps[:, i % 8, 0:q], ALU.mult,
                                               ALU.subtract).then_inc(rows_made, 1)


def attention_sum(nc, d, k, pos_row, neg_row, w0, n):
    HW = C + 1
    NT = n * P
    QC = NT // 4
    with ExitStack() as ctx:
        m = Core(nc, ctx, "asum", again="asum")
        cnt = [m.sb(f"cnt{b}", [P, NT]) for b in range(2)]
        lhs = [m.sb(f"lhs{b}", [P, k.LHS]) for b in range(2)]
        low = [m.sb(f"low{b}", [P, NT]) for b in range(2)]
        e = [m.sb(f"e{b}", [P, NT]) for b in range(2)]
        wt = [m.sb(f"wt{b}", [P, NT]) for b in range(2)]
        sums = m.sb("sums", [P, NT])
        sums3 = m.sb("sums3", [P, NT])
        o = m.sb("o", [P, n, H, HW])
        den = m.sb("den", [P, n * H])
        ps = m.ps("ps", [P, 8, 512])
        in_ = [m.sem(f"in{b}") for b in range(2)]
        low_ready = m.sem("low_ready")
        raised = m.sem("raised")
        logit_ready = m.sem("logit_ready")
        exp_ready = m.sem("exp_ready")
        weight_ready = m.sem("weight_ready")
        weight_used = m.sem("weight_used")
        sums_copied = m.sem("sums_copied")
        turned = m.sem("turned")
        o_copied = m.sem("o_copied")
        dve_step = m.sem("dve_step")
        block = ctx.enter_context(nc.Block())
        NG = -(-n // 3)

        @block.sync
        def _(sp):
            def load(t, b, kk):
                if used(kk):
                    sp.wait_ge(weight_used, (t - 1) * H)
                sp.dma_start(cnt[b][:, :], d.cnt[bass.ds(t, 1), :, w0 * P:w0 * P + NT].rearrange("s p f -> p (s f)")).then_inc(in_[b], 16)
                sp.dma_start(lhs[b][:, :], d.lhs[bass.ds(t, 1), :, :].rearrange("s p f -> p (s f)")).then_inc(in_[b], 16)
            ring(sp, W, 2, load)

        @block.scalar
        def _(act):
            def exp(q, s, wait_value):
                act.wait_ge(logit_ready, wait_value)
                nc.scalar.activation(e[s][:, :], e[s][:, :], ACT.Exp).then_inc(exp_ready, 1)

            def step(t, b, kk):
                act.wait_ge(in_[b], (kk + 1) * 32)
                for h in range(H):
                    s = h % 2
                    if used(kk) or b or h >= 2:
                        act.wait_ge(raised, t * H + h - 1)
                    nc.scalar.activation(low[s][:, :], neg_row[:, h, :], ACT.Identity,
                                         bias=lhs[b][:, 10 * HW + H + h:10 * HW + H + h + 1]).then_inc(low_ready, 1)
                    if used(kk) or b or h:
                        exp(None, 1 - s, t * H + h)
            ring(act, W, 2, step)
            exp(None, (H - 1) % 2, W * H)
            act.wait_ge(weight_used, W * H)
            for c in range(4):
                nc.scalar.copy(sums[0:3 * HW, c * QC:(c + 1) * QC], ps[0:3 * HW, c, 0:QC]).then_inc(sums_copied, 1)
                nc.scalar.copy(sums3[0:HW, c * QC:(c + 1) * QC], ps[0:HW, 4 + c, 0:QC]).then_inc(sums_copied, 1)
            for g in range(NG):
                r = min(3, n - 3 * g)
                act.wait_ge(turned, g + 1)
                nc.scalar.copy(o[:, 3 * g:3 * g + r, :, :].rearrange("p w h c -> p (w h c)"), ps[:, g, 0:r * H * HW]).then_inc(o_copied, 1)

        @block.vector
        def _(dve):
            c = Chain(dve, dve_step)

            def weight(s, b, wait_value, used_value):
                dve.wait_ge(exp_ready, wait_value)
                if used_value is not None:
                    dve.wait_ge(weight_used, used_value)
                nc.vector.tensor_tensor(wt[s][:, :], e[s][:, :], cnt[b][:, :], ALU.mult).then_inc(weight_ready, 1)

            def step(t, b, kk):
                dve.wait_ge(in_[b], (kk + 1) * 32)
                for h in range(H):
                    s = h % 2
                    dve.wait_ge(low_ready, t * H + h + 1)
                    if used(kk) or b or h >= 2:
                        dve.wait_ge(weight_ready, t * H + h - 1)
                    nc.vector.scalar_tensor_tensor(e[s][:, :], pos_row[:, h, :], lhs[b][:, 10 * HW + h:10 * HW + h + 1],
                                                   low[s][:, :], ALU.add, ALU.max).then_inc(raised, 1)
                    dve.wait_ge(raised, t * H + h + 1)
                    nc.vector.tensor_scalar(e[s][:, :], e[s][:, :], 1.0, None, ALU.min).then_inc(logit_ready, 1)
                    if used(kk) or b or h:
                        before = used(kk) or b or h >= 3
                        weight(1 - s, b if h else 1 - b, t * H + h, t * H + h - 2 if before else None)
            ring(dve, W, 2, step)
            weight((H - 1) % 2, (W - 1) % 2, W * H, W * H - 2)
            dve.wait_ge(o_copied, NG)
            c.link(nc.vector.tensor_scalar(den[:, :], o[:, :, :, C].rearrange("p w h -> p (w h)"), 1e-16, None, ALU.add))
            c.link(nc.vector.reciprocal(den[:, :], den[:, :]))
            x = k.x[:, w0 * P:w0 * P + NT].rearrange("p (w c) -> p w c", c=C)
            o3 = o[:, :, :, :].rearrange("p w h c -> p (w h) c")[:, :, 0:C]
            c.link(nc.vector.tensor_tensor(o3, o3, bc(den[:, :, None], [P, n * H, C]), ALU.mult))
            c.link(nc.vector.tensor_tensor(x, x, o3, ALU.add))

        @block.tensor
        def _(pe):
            def step(t, b, kk):
                pe.wait_ge(in_[b], (kk + 1) * 32)
                first, last = isinstance(t, int) and t == 0, isinstance(t, int) and t == W - 1
                for h in range(H):
                    pe.wait_ge(weight_ready, t * H + h + 1)
                    rows = 3 * HW if h < 3 else HW
                    at = h * 3 * HW
                    for c in range(4):
                        mm = nc.tensor.matmul(ps[0:rows, (0 if h < 3 else 4) + c, 0:QC], lhs[b][:, at:at + rows],
                                              wt[h % 2][:, c * QC:(c + 1) * QC], start=first and h in (0, 3),
                                              stop=last and h in (2, 3), skip_group_check=True)
                    mm.then_inc(weight_used, 1)
            ring(pe, W, 2, step)
            pe.wait_ge(sums_copied, 8)
            for j in range(n):
                g, r = j // 3, (j % 3) * H * HW
                nc.tensor.transpose(ps[:, g, r:r + 3 * HW], sums[0:3 * HW, j * P:(j + 1) * P], k.ident[0:3 * HW, 0:3 * HW])
                mm = nc.tensor.transpose(ps[:, g, r + 3 * HW:r + 4 * HW], sums3[0:HW, j * P:(j + 1) * P], k.ident[0:HW, 0:HW])
                if j % 3 == 2 or j == n - 1:
                    mm.then_inc(turned, 1)


def layer_norm(nc, k, tag, table=None, out=None):
    with ExitStack() as ctx:
        m = Core(nc, ctx, tag, again="norm")
        sq = m.sb("sq", [P, NP])
        s = m.sb("s", [P, W])
        v = m.sb("v", [P, W])
        dve_step = m.sem("dve_step")
        var_ready = m.sem("var_ready")
        root_ready = m.sem("root_ready")
        norm_ready = m.sem("norm_ready")
        stored = m.sem("stored")
        block = ctx.enter_context(nc.Block())
        x = k.x[:, :].rearrange("p (w f) -> p w f", f=D)

        @block.vector
        def _(dve):
            c = Chain(dve, dve_step)
            c.link(nc.vector.tensor_reduce(s[:, :], x, AX.X, ALU.add))
            c.link(nc.vector.tensor_scalar(s[:, :], s[:, :], 1.0 / D, None, ALU.mult))
            c.link(nc.vector.tensor_tensor(x, x, bc(s[:, :, None], [P, W, D]), ALU.subtract))
            c.link(nc.vector.tensor_tensor(sq[:, :], k.x[:, :], k.x[:, :], ALU.mult))
            c.link(nc.vector.tensor_reduce(v[:, :], sq[:, :].rearrange("p (w f) -> p w f", f=D), AX.X, ALU.add))
            nc.vector.tensor_scalar(v[:, :], v[:, :], 1.0 / D, 1e-5, ALU.mult, ALU.add).then_inc(var_ready, 1)
            dve.wait_ge(root_ready, 1)
            c.link(nc.vector.reciprocal(v[:, :], v[:, :]))
            nc.vector.tensor_tensor(x, x, bc(v[:, :, None], [P, W, D]), ALU.mult).then_inc(norm_ready, 1)

        @block.scalar
        def _(act):
            act.wait_ge(var_ready, 1)
            nc.scalar.activation(v[:, :], v[:, :], ACT.Sqrt).then_inc(root_ready, 1)

        @block.sync
        def _(sp):
            sp.wait_ge(norm_ready, 1)
            if table is not None:
                sp.dma_start(table.rearrange("w p f -> p w f"), x).then_inc(stored, 16)
                sp.wait_ge(stored, 16)
            if out is not None:
                sp.dma_start(out[0:(W - 1) * P, :].rearrange("(w p) d -> p w d", p=P), x[:, 0:W - 1, :]).then_inc(stored, 16)
                sp.dma_start(out[(W - 1) * P:N, :], x[0:TAIL, W - 1, :]).then_inc(stored, 16)
                sp.wait_ge(stored, 32)


def aggregate(nc, table, counts, total, tag, add=None):
    B = 3
    with ExitStack() as ctx:
        m = Core(nc, ctx, tag, again="aggregate")
        rows = [m.sb(f"rows{b}", [P, D]) for b in range(B)]
        cnt = [m.sb(f"cnt{b}", [P, NP]) for b in range(B)]
        ps = m.ps("ps", [P, NCH, 512])
        in_ = [m.sem(f"in{b}") for b in range(B)]
        summed = m.sem("summed")
        block = ctx.enter_context(nc.Block())

        @block.sync
        def _(sp):
            def load(t, b, kk):
                if used(kk):
                    sp.wait_ge(summed, (t - B + 1) * NCH)
                sp.dma_start(rows[b][:, :], table[bass.ds(t, 1), :, :].rearrange("s p f -> p (s f)")).then_inc(in_[b], 16)
                sp.dma_start(cnt[b][:, :], counts[bass.ds(t, 1), :, :].rearrange("s p f -> p (s f)")).then_inc(in_[b], 16)
            ring(sp, W, B, load)

        @block.tensor
        def _(pe):
            def step(t, b, kk):
                pe.wait_ge(in_[b], (kk + 1) * 32)
                first, last = isinstance(t, int) and t == 0, isinstance(t, int) and t == W - 1
                for c in range(NCH):
                    nc.tensor.matmul(ps[:, c, 0:CH], rows[b][:, :], cnt[b][:, c * CH:(c + 1) * CH], start=first,
                                     stop=last, skip_group_check=True).then_inc(summed, 1)
            ring(pe, W, B, step)

        @block.vector
        def _(dve):
            for c in range(NCH):
                dve.wait_ge(summed, (W - 1) * NCH + c + 1)
                at = slice(c * CH, (c + 1) * CH)
                if add is None:
                    nc.vector.tensor_copy(total[:, at], ps[:, c, 0:CH])
                else:
                    nc.vector.tensor_tensor(total[:, at], ps[:, c, 0:CH], add[:, at], ALU.add)


def mean_layer(nc, p, k, xT, aggT):
    G = -(-W // 4)
    with ExitStack() as ctx:
        m = Core(nc, ctx, "mean")
        wl = m.sb("wl", [D, D])
        wr = m.sb("wr", [D, D])
        bl = m.sb("bl", [P, D])
        br = m.sb("br", [P, D])
        rdeg = m.sb("rdeg", [P, W])
        y = m.sb("y", [P, NP])
        sq = m.sb("sq", [P, NP])
        s = m.sb("s", [P, W])
        ps = m.ps("ps", [P, 8, 512])
        params_in = m.sem("params_in")
        rdeg_ready = m.sem("rdeg_ready")
        multiplied = m.sem("multiplied")
        mean_ready = m.sem("mean_ready")
        group_ready = m.sem("group_ready")
        squares_ready = m.sem("squares_ready")
        root_ready = m.sem("root_ready")
        dve_step = m.sem("dve_step")
        block = ctx.enter_context(nc.Block())

        @block.sync
        def _(sp):
            sp.dma_start(wl[:, :], p['L1_gnn_Wl']).then_inc(params_in, 16)
            sp.dma_start(wr[:, :], p['L1_gnn_Wr']).then_inc(params_in, 16)
            sp.dma_start(bl[:, :], p['L1_gnn_bl'].partition_broadcast(P)).then_inc(params_in, 16)
            sp.dma_start(br[:, :], p['L1_gnn_br'].partition_broadcast(P)).then_inc(params_in, 16)

        @block.tensor
        def _(pe):
            pe.wait_ge(params_in, 64)
            for g in range(G):
                if g >= 4:
                    pe.wait_ge(group_ready, g - 3)
                for w in range(4 * g, min(4 * g + 4, W)):
                    at = slice((w % 4) * P, (w % 4 + 1) * P)
                    nc.tensor.matmul(ps[:, 2 * (g % 4), at], xT[:, w * P:(w + 1) * P], wl[:, :], start=True, stop=True)
                    mm = nc.tensor.matmul(ps[:, 2 * (g % 4) + 1, at], aggT[:, w * P:(w + 1) * P], wr[:, :], start=True, stop=True)
                mm.then_inc(multiplied, 1)

        @block.scalar
        def _(act):
            act.wait_ge(rdeg_ready, 1)
            for w in range(W):
                g = w // 4
                if w % 4 == 0:
                    act.wait_ge(multiplied, g + 1)
                nc.scalar.activation(y[:, w * P:(w + 1) * P], ps[:, 2 * (g % 4) + 1, (w % 4) * P:(w % 4 + 1) * P],
                                     ACT.Copy, scale=rdeg[:, w:w + 1]).then_inc(mean_ready, 1)
            act.wait_ge(squares_ready, 1)
            nc.scalar.activation(s[:, :], s[:, :], ACT.Sqrt).then_inc(root_ready, 1)

        @block.vector
        def _(dve):
            c = Chain(dve, dve_step)
            c.link(nc.vector.tensor_scalar(rdeg[:, :], k.degree[:, :], 1.0, None, ALU.max))
            nc.vector.reciprocal(rdeg[:, :], rdeg[:, :]).then_inc(rdeg_ready, 1)
            dve.wait_ge(params_in, 64)
            c.link(nc.vector.tensor_tensor(bl[:, :], bl[:, :], br[:, :], ALU.add))
            for g in range(G):
                n = min(4, W - 4 * g) * P
                dve.wait_ge(mean_ready, min(4 * g + 4, W))
                nc.vector.tensor_tensor(y[:, g * 512:g * 512 + n], y[:, g * 512:g * 512 + n], ps[:, 2 * (g % 4), 0:n],
                                        ALU.add).then_inc(group_ready, 1)
            dve.wait_ge(group_ready, G)
            y3 = y[:, :].rearrange("p (w f) -> p w f", f=D)
            c.link(nc.vector.tensor_tensor(y3, y3, bc(bl[:, None, :], [P, W, D]), ALU.add))
            c.link(nc.vector.tensor_scalar(y[:, :], y[:, :], 0.0, None, ALU.max))
            c.link(nc.vector.tensor_tensor(sq[:, :], y[:, :], y[:, :], ALU.mult))
            nc.vector.tensor_reduce(s[:, :], sq[:, :].rearrange("p (w f) -> p w f", f=D), AX.X, ALU.add).then_inc(squares_ready, 1)
            dve.wait_ge(root_ready, 1)
            c.link(nc.vector.tensor_scalar(s[:, :], s[:, :], 1e-6, None, ALU.add))
            c.link(nc.vector.reciprocal(s[:, :], s[:, :]))
            c.link(nc.vector.tensor_tensor(y3, y3, bc(s[:, :, None], [P, W, D]), ALU.mult))
            c.link(nc.vector.tensor_tensor(k.x[:, :], k.x[:, :], y[:, :], ALU.add))


def mlp(nc, p, k, layer, aggT, outT, nodes, table):
    G = -(-W // 4)
    with ExitStack() as ctx:
        m = Core(nc, ctx, f"mlp{layer}", again="mlp")
        w1 = m.sb("w1", [D, D])
        w2 = m.sb("w2", [D, D])
        b1 = m.sb("b1", [D, 1])
        b2 = m.sb("b2", [D, 1])
        hT = m.sb("hT", [P, NP])
        ps = m.ps("ps", [P, NCH, 512])
        params_in = m.sem("params_in")
        hidden_summed = m.sem("hidden_summed")
        hidden_ready = m.sem("hidden_ready")
        out_summed = m.sem("out_summed")
        out_ready = m.sem("out_ready")
        turned = m.sem("turned")
        nodes_ready = m.sem("nodes_ready")
        stored = m.sem("stored")
        block = ctx.enter_context(nc.Block())

        @block.sync
        def _(sp):
            sp.dma_start(w1[:, :], p['L2_gnn_W1'][layer, :, :]).then_inc(params_in, 16)
            sp.dma_start(w2[:, :], p['L2_gnn_W2'][layer, :, :]).then_inc(params_in, 16)
            sp.dma_start(b1[:, :], p['L2_gnn_b1'][layer, :].rearrange("(d a) -> d a", a=1)).then_inc(params_in, 16)
            sp.dma_start(b2[:, :], p['L2_gnn_b2'][layer, :].rearrange("(d a) -> d a", a=1)).then_inc(params_in, 16)
            if table is not None:
                sp.wait_ge(nodes_ready, G)
                sp.dma_start(table.rearrange("w p f -> p w f"), nodes[:, :].rearrange("p (w f) -> p w f", f=D)).then_inc(stored, 16)
                sp.wait_ge(stored, 16)

        @block.tensor
        def _(pe):
            pe.wait_ge(params_in, 64)
            for c in range(NCH):
                nc.tensor.matmul(ps[:, c, 0:CH], w1[:, :], aggT[:, c * CH:(c + 1) * CH], start=True, stop=True).then_inc(hidden_summed, 1)
            for c in range(NCH):
                pe.wait_ge(hidden_ready, c + 1)
                nc.tensor.matmul(ps[:, c, 0:CH], w2[:, :], hT[:, c * CH:(c + 1) * CH], start=True, stop=True).then_inc(out_summed, 1)
            pe.wait_ge(out_ready, NCH)
            for w in range(W):
                mm = nc.tensor.transpose(ps[:, w // 4, (w % 4) * P:(w % 4 + 1) * P], outT[:, w * P:(w + 1) * P], k.ident[:, :])
                if w % 4 == 3 or w == W - 1:
                    mm.then_inc(turned, 1)

        @block.scalar
        def _(act):
            act.wait_ge(params_in, 64)
            for c in range(NCH):
                act.wait_ge(hidden_summed, c + 1)
                nc.scalar.activation(hT[:, c * CH:(c + 1) * CH], ps[:, c, 0:CH], ACT.Relu, bias=b1[:, :]).then_inc(hidden_ready, 1)
            for c in range(NCH):
                act.wait_ge(out_summed, c + 1)
                nc.scalar.activation(outT[:, c * CH:(c + 1) * CH], ps[:, c, 0:CH], ACT.Relu, bias=b2[:, :]).then_inc(out_ready, 1)
            for g in range(G):
                n = min(4, W - 4 * g) * P
                act.wait_ge(turned, g + 1)
                nc.scalar.copy(nodes[:, g * 512:g * 512 + n], ps[:, g, 0:n]).then_inc(nodes_ready, 1)


def add_to_x(nc, k, y, tag, scale=1.0):
    with nc.Block() as block:
        @block.vector
        def _(dve):
            nc.vector.scalar_tensor_tensor(k.x[:, :], k.x[:, :], scale, y[:, :], ALU.mult, ALU.add)


def hop_left(nc, k, d, qw, aggT):
    with ExitStack() as ctx:
        m = Core(nc, ctx, "left", again="left")
        leftT = m.sb("leftT", [P, NP])
        ps = m.ps("ps", [P, NCH, 512])
        summed = m.sem("summed")
        ready = m.sem("ready")
        stored = m.sem("stored")
        block = ctx.enter_context(nc.Block())

        @block.tensor
        def _(pe):
            for c in range(NCH):
                nc.tensor.matmul(ps[:, c, 0:CH], qw[:, :], aggT[:, c * CH:(c + 1) * CH], start=True, stop=True).then_inc(summed, 1)

        @block.scalar
        def _(act):
            for c in range(NCH):
                act.wait_ge(summed, c + 1)
                nc.scalar.copy(leftT[:, c * CH:(c + 1) * CH], ps[:, c, 0:CH]).then_inc(ready, 1)

        @block.sync
        def _(sp):
            sp.wait_ge(ready, NCH)
            sp.dma_start(d.left[0:W, :, :].rearrange("w f n -> f w n"), leftT[:, :].rearrange("f (w n) -> f w n", n=P)).then_inc(stored, 16)
            sp.dma_start(d.left[W, :, :], k.zeros[:, :]).then_inc(stored, 16)
            sp.wait_ge(stored, 32)


def relation_parts(nc, p, k, rel_hi_mid, rel_lo):
    with ExitStack() as ctx:
        m = Core(nc, ctx, "rel")
        t = m.sb("t", [P, D])
        hi = m.sb("hi", [P, D], BF16)
        r1 = m.sb("r1", [P, D])
        mid = m.sb("mid", [P, D], BF16)
        rel_in = m.sem("rel_in")
        dve_step = m.sem("dve_step")
        block = ctx.enter_context(nc.Block())

        @block.sync
        def _(sp):
            sp.dma_start(t[0:REL, :], p['L3_gnn_edge_emb']).then_inc(rel_in, 16)
            sp.dma_start(t[REL:P, :], p['L3_gnn_edge_emb']).then_inc(rel_in, 16)

        @block.vector
        def _(dve):
            c = Chain(dve, dve_step)
            dve.wait_ge(rel_in, 32)
            c.link(nc.vector.tensor_copy(hi[:, :], t[:, :]))
            c.link(nc.vector.tensor_tensor(r1[:, :], t[:, :], hi[:, :], ALU.subtract))
            c.link(nc.vector.tensor_copy(mid[:, :], r1[:, :]))
            c.link(nc.vector.tensor_copy(rel_hi_mid[0:REL, :], hi[0:REL, :]))
            c.link(nc.vector.tensor_copy(rel_hi_mid[REL:P, :], mid[REL:P, :]))
            c.link(nc.vector.tensor_tensor(r1[:, :], r1[:, :], mid[:, :], ALU.subtract))
            c.link(nc.vector.tensor_copy(rel_lo[:, :], r1[0:REL, :]))


def relation_masks(nc, d, k):
    with ExitStack() as ctx:
        m = Core(nc, ctx, "types")
        rec = [m.sb(f"rec{b}", [P, J, 4]) for b in range(2)]
        typ = m.sb("typ", [P, P], BF16)
        hot = [m.sb(f"hot{b}", [P, J, P], BF16) for b in range(2)]
        hotT = [m.sb(f"hotT{b}", [P, S], BF16) for b in range(2)]
        ps = [m.ps(f"ps{b}", [P, S]) for b in range(2)]
        typ_ready = m.sem("typ_ready")
        rec_in = [m.sem(f"rec_in{b}") for b in range(2)]
        hot_ready = m.sem("hot_ready")
        turned = m.sem("turned")
        copied = m.sem("copied")
        stored = [m.sem(f"stored{b}") for b in range(2)]
        block = ctx.enter_context(nc.Block())
        slots = d.slots.rearrange("(s p j) f -> s p (j f)", p=P, j=J)

        @block.sync
        def _(sp):
            def step(t, b, kk):
                if used(kk):
                    sp.wait_ge(hot_ready, (t - 1) * J)
                sp.dma_start(rec[b][:, :, :].rearrange("p j f -> p (j f)").bitcast(I32), slots[bass.ds(t, 1), :, :].rearrange("s p f -> p (s f)")).then_inc(rec_in[b], 16)
            ring(sp, NST, 2, step)

        @block.vector
        def _(dve):
            nc.vector.tensor_copy(typ[:, 0:REL], k.node[:, 0:REL]).then_inc(typ_ready, 1)
            nc.vector.tensor_copy(typ[:, REL:P], k.node[:, 0:REL]).then_inc(typ_ready, 1)
            dve.wait_ge(typ_ready, 2)

            def step(t, b, kk):
                dve.wait_ge(rec_in[b], (kk + 1) * 16)
                if used(kk):
                    dve.wait_ge(turned, t - 1)
                for j in range(J):
                    nc.vector.tensor_scalar(hot[b][:, j, :], typ[:, :], rec[b][:, j, 2:3], None, ALU.is_equal).then_inc(hot_ready, 1)
            ring(dve, NST, 2, step)

        @block.tensor
        def _(pe):
            def step(t, b, kk):
                pe.wait_ge(hot_ready, (t + 1) * J)
                if used(kk):
                    pe.wait_ge(copied, t - 1)
                for j in range(J):
                    mm = nc.tensor.matmul(ps[b][:, j * P:(j + 1) * P], hot[b][:, j, :], k.identb[:, :], start=True, stop=True)
                mm.then_inc(turned, 1)
            ring(pe, NST, 2, step)

        @block.scalar
        def _(act):
            def step(t, b, kk):
                act.wait_ge(turned, t + 1)
                if used(kk):
                    act.wait_ge(stored[b], kk * 16)
                nc.scalar.copy(hotT[b][:, :], ps[b][:, :]).then_inc(copied, 1)
            ring(act, NST, 2, step)

        @block.gpsimd
        def _(pool):
            def step(t, b, kk):
                pool.wait_ge(copied, t + 1)
                pool.sem_inc(k.issue, 1)
                pool.dma_start(d.type_hots[bass.ds(t, 1), :, :].rearrange("s p f -> p (s f)"), hotT[b][:, :]).then_inc(stored[b], 16)
            ring(pool, NST, 2, step)
            for b in range(2):
                pool.wait_ge(stored[b], 16 * (NST // 2))


def hop_edges(nc, d, k, kw, rel_hi_mid, rel_lo, table, result):
    MW = D + 1
    with ExitStack() as ctx:
        m = Core(nc, ctx, "hop", again="hop")
        rec = [m.sb(f"rec{b}", [P, J, 4]) for b in range(2)]
        tail_rows = [m.sb(f"tail_rows{b}", [P, J, D]) for b in range(2)]
        hotT = [m.sb(f"hotT{b}", [P, S], BF16) for b in range(2)]
        left = [m.sb(f"left{b}", [P, P]) for b in range(2)]
        other = [m.sb(f"other{b}", [P, J, P], BF16) for b in range(2)]
        rt = [m.sb(f"rt{b}", [P, J, MW]) for b in range(2)]
        rtT = [m.sb(f"rtT{b}", [P, S]) for b in range(2)]
        right = [m.sb(f"right{b}", [P, S]) for b in range(2)]
        ex = [m.sb(f"ex{b}", [P, S]) for b in range(2)]
        exT = [m.sb(f"exT{b}", [P, S]) for b in range(2)]
        tile_max = m.sb("tile_max", [P, 1])
        run_max = m.sb("run_max", [P, 1])
        new_max = [m.sb(f"new_max{b}", [P, 1]) for b in range(2)]
        neg_max = [m.sb(f"neg_max{b}", [P, 1]) for b in range(2)]
        scale = [m.sb(f"scale{b}", [P, 1]) for b in range(2)]
        keep = [m.sb(f"keep{b}", [P, 2]) for b in range(2)]
        state = [m.sb(f"state{b}", [P, MW]) for b in range(2)]
        ps_rel = m.ps("ps_rel", [P, S])
        ps_rtT = m.ps("ps_rtT", [P, S])
        ps_right = m.ps("ps_right", [P, S])
        ps_logit = [m.ps(f"ps_logit{b}", [P, S]) for b in range(2)]
        ps_exT = m.ps("ps_exT", [P, S])
        ps_sum = [m.ps(f"ps_sum{b}", [P, S]) for b in range(2)]
        rec_in = [m.sem(f"rec_in{b}") for b in range(2)]
        hotT_in = [m.sem(f"hotT_in{b}") for b in range(2)]
        left_in = [m.sem(f"left_in{b}") for b in range(2)]
        rows_in = [m.sem(f"rows_in{b}", fresh=True) for b in range(2)]
        issue = m.sem("issue")
        other_ready = m.sem("other_ready")
        rel_ready = m.sem("rel_ready")
        rt_ready = m.sem("rt_ready")
        rt_turned = m.sem("rt_turned")
        rtT_ready = m.sem("rtT_ready")
        right_summed = m.sem("right_summed")
        right_ready = m.sem("right_ready")
        logits_ready = m.sem("logits_ready")
        max_ready = m.sem("max_ready")
        ex_ready = m.sem("ex_ready")
        ex_turned = m.sem("ex_turned")
        exT_ready = m.sem("exT_ready")
        messages_summed = m.sem("messages_summed")
        state_ready = m.sem("state_ready")
        state_out = [m.sem(f"state_out{b}", fresh=True) for b in range(2)]
        ones_set = m.sem("ones_set")
        dve_step = m.sem("dve_step")
        block = ctx.enter_context(nc.Block())
        slots = d.slots.rearrange("(s p j) f -> s p (j f)", p=P, j=J)
        table_rows = table.rearrange("w p f -> (w p) f")

        @block.sync
        def _(sp):
            def step(t, b, kk):
                if used(kk):
                    sp.wait_ge(other_ready, t - 1)
                    sp.wait_ge(rows_in[b], kk * 16 * J)
                sp.dma_start(rec[b][:, :, :].rearrange("p j f -> p (j f)").bitcast(I32), slots[bass.ds(t, 1), :, :].rearrange("s p f -> p (s f)")).then_inc(rec_in[b], 16)
                if used(kk):
                    sp.wait_ge(rel_ready, t - 1)
                sp.dma_start(hotT[b][:, :], d.type_hots[bass.ds(t, 1), :, :].rearrange("s p f -> p (s f)")).then_inc(hotT_in[b], 16)
                if used(kk):
                    sp.wait_ge(logits_ready, t - 1)
                w = sp.value_load(k.window_of[0:1, bass.ds(t, 1)], min_val=0, max_val=W)
                sp.dma_start(left[b][:, :], d.left[bass.ds(w, 1), :, :].rearrange("s p f -> p (s f)")).then_inc(left_in[b], 16)
            ring(sp, NST, 2, step)

        @block.gpsimd
        def _(pool):
            def store(t, b):
                w = pool.value_load(k.window_of[0:1, bass.ds(t, 1)], min_val=0, max_val=W)
                last = pool.value_load(k.last_of[0:1, bass.ds(t, 1)], min_val=0, max_val=1)
                pool.wait_ge(state_ready, t + 1)
                pool.sem_inc(issue, 1)
                pool.dma_start(d.state[bass.ds(w, 1), :, :].rearrange("s p f -> p (s f)"), state[b][:, :], cond=last).then_inc(state_out[b], 16)

            def step(t, b, kk):
                if used(kk):
                    pool.wait_ge(rt_ready, t - 1)
                    pool.sem_inc(issue, 1)
                pool.wait_ge(rec_in[b], (kk + 1) * 16)
                pool.sem_inc(issue, 1)
                for j in range(J):
                    pool.indirect_dma_start(tail_rows[b][:, j, :], None, table_rows,
                                            bass.IndirectOffsetOnAxis(ap=rec[b][:, j, 3:4].bitcast(I32), axis=0)).then_inc(rows_in[b], 16)
                if used(kk):
                    store(t - 2, b)
            ring(pool, NST, 2, step)
            for t in range(NST - 2, NST):
                store(t, t % 2)
            for b in range(2):
                pool.wait_ge(state_out[b], 16 * (NST // 2))

        @block.tensor
        def _(pe):
            def front(t, b, kk, prev):
                pe.wait_ge(hotT_in[b], (kk + 1) * 16)
                if prev:
                    pe.wait_ge(rt_ready, t)
                for j in range(J):
                    nc.tensor.matmul(ps_rel[:, j * P:(j + 1) * P], hotT[b][:, j * P:(j + 1) * P], rel_hi_mid[:, :], start=True, stop=False)
                    mm = nc.tensor.matmul(ps_rel[:, j * P:(j + 1) * P], hotT[b][0:REL, j * P:(j + 1) * P], rel_lo[:, :], start=False, stop=True)
                mm.then_inc(rel_ready, 1)
                pe.wait_ge(rt_ready, t + 1)
                if prev:
                    pe.wait_ge(rtT_ready, t)
                for j in range(J):
                    mm = nc.tensor.transpose(ps_rtT[:, j * P:(j + 1) * P], rt[b][:, j, 0:D], k.ident[:, :])
                mm.then_inc(rt_turned, 1)
                pe.wait_ge(rtT_ready, t + 1)
                if prev:
                    pe.wait_ge(right_ready, t)
                nc.tensor.matmul(ps_right[:, :], kw[:, :], rtT[b][:, :], start=True, stop=True).then_inc(right_summed, 1)
                pe.wait_ge(other_ready, t + 1)
                pe.wait_ge(left_in[b], (kk + 1) * 16)
                if used(kk):
                    pe.wait_ge(ex_ready, t - 1)
                pe.wait_ge(right_ready, t + 1)
                nc.tensor.matmul(ps_logit[b][:, :], left[b][:, :], right[b][:, :], start=True, stop=False,
                                 skip_group_check=True)
                for j in range(J):
                    mm = nc.tensor.matmul(ps_logit[b][:, j * P:(j + 1) * P], other[b][:, j, :], k.ident_neg[:, :], start=False,
                                          stop=(j == J - 1), skip_group_check=True)
                mm.then_inc(logits_ready, 1)

            def back(t, b, prev):
                pe.wait_ge(ex_ready, t + 1)
                if prev:
                    pe.wait_ge(exT_ready, t)
                for j in range(J):
                    mm = nc.tensor.transpose(ps_exT[:, j * P:(j + 1) * P], ex[b][:, j * P:(j + 1) * P], k.ident[:, :])
                mm.then_inc(ex_turned, 1)
                pe.wait_ge(exT_ready, t + 1)
                for j in range(J):
                    mm = nc.tensor.matmul(ps_sum[b][:, 0:MW], exT[b][:, j * P:(j + 1) * P], rt[b][:, j, :], start=(j == 0), stop=(j == J - 1))
                mm.then_inc(messages_summed, 1)

            def step(t, b, kk):
                front(t, b, kk, used(kk) or b)
                if used(kk) or b:
                    if used(kk):
                        pe.wait_ge(state_ready, t - 2)  if not (isinstance(t, int) and t <= 2) else None
                    back(t - 1, 1 - b, used(kk))
            ring(pe, NST, 2, step)
            back(NST - 1, (NST - 1) % 2, True)

        @block.scalar
        def _(act):
            def front(t, b, kk):
                act.wait_ge(rt_turned, t + 1)
                if used(kk):
                    act.wait_ge(right_summed, t - 1)
                nc.scalar.copy(rtT[b][:, :], ps_rtT[:, :]).then_inc(rtT_ready, 1)
                act.wait_ge(right_summed, t + 1)
                if used(kk):
                    act.wait_ge(logits_ready, t - 1)
                nc.scalar.activation(right[b][:, :], ps_right[:, :], ACT.Tanh).then_inc(right_ready, 1)

            def middle(t, b, kk):
                act.wait_ge(max_ready, t + 1)
                if used(kk):
                    act.wait_ge(ex_turned, t - 1)
                nc.scalar.activation(ex[b][:, :], ps_logit[b][:, :], ACT.Exp, bias=neg_max[b][:, :])
                act.wait_ge(logits_ready, t + 1)
                nc.scalar.activation(scale[b][:, :], run_max[:, :], ACT.Exp, bias=neg_max[b][:, :]).then_inc(ex_ready, 1)

            def back(t, b, prev2):
                act.wait_ge(ex_turned, t + 1)
                if prev2:
                    act.wait_ge(messages_summed, t - 1)
                nc.scalar.copy(exT[b][:, :], ps_exT[:, :]).then_inc(exT_ready, 1)

            def step(t, b, kk):
                front(t, b, kk)
                if used(kk) or b:
                    back(t - 1, 1 - b, used(kk) and not (isinstance(t, int) and t <= 2))
                middle(t, b, kk)
            ring(act, NST, 2, step)
            back(NST - 1, (NST - 1) % 2, True)

        @block.vector
        def _(dve):
            c = Chain(dve, dve_step)
            for b in range(2):
                nc.vector.memset(rt[b][:, :, D:MW], 1.0).then_inc(ones_set, 1)
                nc.vector.memset(state[b][:, :], 0.0).then_inc(ones_set, 1)
                nc.vector.memset(new_max[b][:, :], -BIG / 2).then_inc(ones_set, 1)
            dve.wait_ge(ones_set, 6)

            def front(t, b, kk):
                dve.wait_ge(rec_in[b], (kk + 1) * 16)
                if used(kk):
                    dve.wait_ge(logits_ready, t - 1)
                nc.vector.tensor_tensor(other[b][:, :, :], bc(k.node[:, None, :], [P, J, P]), bc(rec[b][:, :, 0:1], [P, J, P]),
                                        ALU.not_equal).then_inc(other_ready, 1)
                dve.wait_ge(rows_in[b], (kk + 1) * 16 * J)
                dve.wait_ge(rel_ready, t + 1)
                if used(kk):
                    dve.wait_ge(messages_summed, t - 1)
                nc.vector.tensor_tensor(rt[b][:, :, 0:D], tail_rows[b][:, :, :], ps_rel[:, :].rearrange("p (j f) -> p j f", f=D),
                                        ALU.mult).then_inc(rt_ready, 1)

            def middle(t, b, first):
                dve.wait_ge(logits_ready, t + 1)
                c.link(nc.vector.tensor_reduce(tile_max[:, :], ps_logit[b][:, :], AX.X, ALU.max))
                if not first:
                    dve.wait_ge(ex_ready, t)
                c.link(nc.vector.tensor_copy(keep[b][:, :], k.keep[:, bass.ds(t, 1), :].rearrange("p s a -> p (s a)")))
                c.link(nc.vector.tensor_tensor(run_max[:, :], new_max[1 - b][:, :], keep[b][:, 1:2], ALU.min))
                c.link(nc.vector.tensor_tensor(new_max[b][:, :], run_max[:, :], tile_max[:, :], ALU.max))
                nc.vector.tensor_scalar(neg_max[b][:, :], new_max[b][:, :], -1.0, None, ALU.mult).then_inc(max_ready, 1)

            def back(t, b, prev2):
                dve.wait_ge(ex_ready, t + 1)
                c.link(nc.vector.tensor_tensor(scale[b][:, :], scale[b][:, :], keep[b][:, 0:1], ALU.mult))
                dve.wait_ge(messages_summed, t + 1)
                if prev2 is not None:
                    dve.wait_ge(state_out[b], prev2)
                nc.vector.scalar_tensor_tensor(state[b][:, :], state[1 - b][:, :], scale[b][:, :], ps_sum[b][:, 0:MW], ALU.mult,
                                               ALU.add).then_inc(state_ready, 1)
                dve.wait_ge(state_ready, t + 1)

            def step(t, b, kk):
                front(t, b, kk)
                if used(kk) or b:
                    n = None
                    if used(kk) and not (isinstance(t, int) and t <= 2):
                        n = (kk - 1) * 16 if not b else kk * 16
                    back(t - 1, 1 - b, n)
                middle(t, b, not used(kk) and b == 0)
            return_links = 2 * 5
            ring(dve, NST, 2, step, c, return_links)
            back(NST - 1, (NST - 1) % 2, (NST // 2 - 1) * 16)

    with ExitStack() as ctx:
        m = Core(nc, ctx, "hop_end", again="hop_end")
        st = m.sb("st", [P, W, MW])
        r = m.sb("r", [P, W])
        cn = m.sb("cn", [P, W])
        sq = m.sb("sq", [P, NP])
        st_in = m.sem("st_in")
        dve_step = m.sem("dve_step")
        squares_ready = m.sem("squares_ready")
        root_ready = m.sem("root_ready")
        unit_ready = m.sem("unit_ready")
        stored = m.sem("stored")
        block = ctx.enter_context(nc.Block())
        y3 = result[:, :].rearrange("p (w f) -> p w f", f=D)

        @block.sync
        def _(sp):
            sp.dma_start(st[:, :, :], d.state[0:W, :, :].rearrange("w p f -> p w f")).then_inc(st_in, 16)
            sp.wait_ge(unit_ready, 1)
            sp.dma_start(table.rearrange("w p f -> p w f"), y3).then_inc(stored, 16)
            sp.wait_ge(stored, 16)

        @block.scalar
        def _(act):
            act.wait_ge(squares_ready, 1)
            nc.scalar.activation(r[:, :], r[:, :], ACT.Sqrt).then_inc(root_ready, 1)

        @block.vector
        def _(dve):
            c = Chain(dve, dve_step)
            dve.wait_ge(st_in, 16)
            c.link(nc.vector.tensor_scalar(r[:, :], st[:, :, D], 1e-30, None, ALU.max))
            c.link(nc.vector.tensor_scalar(cn[:, :], k.degree[:, :], 1.0, None, ALU.max))
            c.link(nc.vector.tensor_tensor(r[:, :], r[:, :], cn[:, :], ALU.mult))
            c.link(nc.vector.reciprocal(r[:, :], r[:, :]))
            c.link(nc.vector.tensor_tensor(y3, st[:, :, 0:D], bc(r[:, :, None], [P, W, D]), ALU.mult))
            c.link(nc.vector.tensor_tensor(sq[:, :], result[:, :], result[:, :], ALU.mult))
            nc.vector.tensor_reduce(r[:, :], sq[:, :].rearrange("p (w f) -> p w f", f=D), AX.X, ALU.add).then_inc(squares_ready, 1)
            dve.wait_ge(root_ready, 1)
            c.link(nc.vector.tensor_scalar(r[:, :], r[:, :], 1e-12, None, ALU.max))
            c.link(nc.vector.reciprocal(r[:, :], r[:, :]))
            nc.vector.tensor_tensor(y3, y3, bc(r[:, :, None], [P, W, D]), ALU.mult).then_inc(unit_ready, 1)


class Space:
    pass


def build(nc, p, out, debug=None):
    with ExitStack() as ctx:
        m = Core(nc, ctx, "all")
        k, d = Space(), Space()
        k.ident = m.sb("ident", [P, P])
        k.identb = m.sb("identb", [P, P], BF16)
        k.ident_neg = m.sb("ident_neg", [P, P], BF16)
        k.tri = m.sb("tri", [P, P])
        k.node = m.sb("node", [P, P], BF16)
        k.steps = m.sb("steps", [P, NST + 1])
        k.part = m.sb("part", [P, 1])
        k.ones = m.sb("ones", [P, P])
        k.zeros = m.sb("zeros", [P, P])
        k.zerosb = m.sb("zerosb", [P, CH], BF16)
        k.window_of = m.sb("window_of", [P, NST], I32)
        k.last_of = m.sb("last_of", [P, NST], I32)
        k.keep = m.sb("keep", [P, NST, 2])
        k.degree = m.sb("degree", [P, W])
        k.issue = m.sem("issue")
        d.slots = nc.dram_tensor("slots", (NST * S, 4), I32).ap()
        d.cum = nc.dram_tensor("cum", (W + 1, P, NP), F32).ap()
        d.cnt = nc.dram_tensor("cnt", (W, P, NP), F32).ap()
        d.cntT = nc.dram_tensor("cntT", (W, P, NP), F32).ap()
        zeros_set = m.sem("zeros_set")
        with nc.Block() as block:
            @block.vector
            def _(dve):
                nc.vector.memset(k.zeros[:, :], 0.0).then_inc(zeros_set, 1)
                nc.vector.memset(k.zerosb[:, :], 0.0).then_inc(zeros_set, 1)
        build_constants(nc, k)
        sort_edges(nc, p, d, k)
        count_pairs(nc, d, k)
        split_counts(nc, d, k)
        k.x = m.sb("x", [P, NP])
        k.LHS = 10 * (C + 1) + 2 * H
        k.col_s = m.sb("col_s", [P, W * H])
        k.col_d = m.sb("col_d", [P, W * H])
        k.amax = m.sb("amax", [P, W * H])
        d.lhs = nc.dram_tensor("lhs", (W, P, k.LHS), F32).ap()
        d.nodes = nc.dram_tensor("nodes", (W, P, D), F32).ap()
        d.left = nc.dram_tensor("left", (W + 1, P, P), F32).ap()
        d.type_hots = nc.dram_tensor("types", (NST, P, S), BF16).ap()
        d.state = nc.dram_tensor("state", (W + 1, P, D + 1), F32).ap()
        load_inputs(nc, p, k)
        with ExitStack() as inner:
            mm = Core(nc, inner, "att")
            row_d = mm.sb("row_d", [P, H, NP])
            with ExitStack() as deep:
                mm = Core(nc, deep, "att")
                row_s = mm.sb("row_s", [P, H, NP])
                with ExitStack() as deeper:
                    xT = Core(nc, deeper, "att").sb("xT", [P, NP])
                    turn(nc, k, k.x, xT, "turn_x")
                    attention_project(nc, p, d, k, xT, row_s, row_d)
                attention_max(nc, d, k, row_s)
            with ExitStack() as deep:
                mm = Core(nc, deep, "att")
                pos_row = mm.sb("pos_row", [P, H, 13 * P])
                neg_row = mm.sb("neg_row", [P, H, 13 * P])
                for w0, n in ((0, 13), (13, 12)):
                    pr, nr = pos_row[:, :, 0:n * P], neg_row[:, :, 0:n * P]
                    attention_rows(nc, k, row_d, pr, nr, w0, n)
                    attention_sum(nc, d, k, pr, nr, w0, n)
        layer_norm(nc, k, "norm0", table=d.nodes)
        with ExitStack() as inner:
            mm = Core(nc, inner, "graph")
            xT = mm.sb("xT", [P, NP])
            aggT = mm.sb("aggT", [P, NP])
            y = mm.sb("y", [P, NP])
            turn(nc, k, k.x, xT, "turn_1")
            aggregate(nc, d.nodes, d.cntT, aggT, "agg1")
            mean_layer(nc, p, k, xT, aggT)
            layer_norm(nc, k, "norm1", table=d.nodes)
            turn(nc, k, k.x, xT, "turn_2")
            for layer in range(3):
                aggregate(nc, d.nodes, d.cnt, aggT, f"agg2{layer}", add=xT)
                mlp(nc, p, k, layer, aggT, xT, y, d.nodes if layer < 2 else None)
            add_to_x(nc, k, y, "add2")
            layer_norm(nc, k, "norm2", table=d.nodes)
            rel_hi_mid = mm.sb("rel_hi_mid", [P, D], BF16)
            rel_lo = mm.sb("rel_lo", [REL, D], BF16)
            qw = mm.sb("qw", [D, D])
            kw = mm.sb("kw", [D, D])
            relation_parts(nc, p, k, rel_hi_mid, rel_lo)
            relation_masks(nc, d, k)
            hop_in = mm.sem("hop_in")
            with nc.Block() as block:
                @block.sync
                def _(sp):
                    sp.dma_start(qw[:, :], p['L3_gnn_q_w']).then_inc(hop_in, 16)
                    sp.dma_start(kw[:, :], p['L3_gnn_k_w']).then_inc(hop_in, 16)
                    sp.wait_ge(hop_in, 32)
            turn(nc, k, k.x, xT, "turn_3")
            for hop in range(3):
                hop_left(nc, k, d, qw, xT)
                hop_edges(nc, d, k, kw, rel_hi_mid, rel_lo, d.nodes, y)
                if hop < 2:
                    turn(nc, k, y, xT, f"turn_4{hop}")
                add_to_x(nc, k, y, "add3", scale=4.0 if hop == 0 else 1.0)
        layer_norm(nc, k, "norm3", out=out)


INPUTS = ['x', 'src', 'dst', 'edge_type_64', 'L0_gnn_coeffs_t', 'L0_gnn_lin_weight', 'L0_gnn_lin_bias',
          'L0_gnn_att_src', 'L0_gnn_att_dst', 'L1_gnn_Wl', 'L1_gnn_bl', 'L1_gnn_Wr', 'L1_gnn_br', 'L2_gnn_W1',
          'L2_gnn_b1', 'L2_gnn_W2', 'L2_gnn_b2', 'L3_gnn_edge_emb', 'L3_gnn_q_w', 'L3_gnn_k_w']
DEBUG = {}


def kernel(**inputs):
    import numpy as np
    import concourse.bacc as bacc
    from concourse.bass_utils import run_bass_kernel_spmd as run

    nc = bacc.Bacc("TRN2", target_bir_lowering=False, num_devices=1)
    arrays, p = {}, {}
    for name in INPUTS:
        a = np.ascontiguousarray(inputs[name])
        arrays[f"in_{name}"] = a
        p[name] = nc.dram_tensor(f"in_{name}", a.shape, mybir.dt.from_np(a.dtype), kind="ExternalInput").ap()
    out = nc.dram_tensor("out_0", (N, D), F32, kind="ExternalOutput").ap()
    debug = {n: nc.dram_tensor(f"dbg_{n}", s, F32, kind="ExternalOutput").ap() for n, s in DEBUG.items()} or None
    build(nc, p, out, debug)
    r = run(nc, [arrays], core_ids=[0])
    return r.results[0]["out_0"]
```

```python
import concourse.bass as bass
from concourse import mybir
from contextlib import ExitStack, contextmanager

F32 = mybir.dt.float32
BF16 = mybir.dt.bfloat16
F16 = mybir.dt.float16
I32 = mybir.dt.int32
ALU = mybir.AluOpType
ACT = mybir.ActivationFunctionType
AX = mybir.AxisListType

P = 128
N, D, E = 3125, 128, 103125
W = -(-N // P)
NP = W * P
TAIL = N - (W - 1) * P
EP = 125
EC = E // EP
S = 512
J = S // P
NST = (E + W + W * (S - 1)) // S
CH = 400
NCH = NP // CH
MID = 1600
SHIFT = 9
H, C = 4, 32
BIG = 2.0 ** 100
REL = 64
SCAT_BUFS, SCAT_COLS = 3, 11


class Chain:

    def __init__(self, eng, sem):
        self.eng, self.sem, self.base, self.n = eng, sem, 0, 0

    def link(self, ins):
        ins.then_inc(self.sem, 1)
        self.n += 1
        self.eng.wait_ge(self.sem, self.base + self.n)

    @contextmanager
    def loop(self, start, end, links):
        before = self.base + self.n
        with self.eng.Fori(start, end) as i:
            self.base, self.n = i * links + (before - start * links), 0
            yield i
            assert self.n == links, self.n
        self.base, self.n = 0, before + (end - start) * links


def ring(eng, count, bufs, body, chain=None, links=0):
    for t in range(bufs):
        body(t, t, 0)
    full = count // bufs
    if full > 1:
        if chain:
            with chain.loop(1, full, links) as k:
                for b in range(bufs):
                    body(k * bufs + b, b, k)
        else:
            with eng.Fori(1, full) as k:
                for b in range(bufs):
                    body(k * bufs + b, b, k)
    for b in range(count - full * bufs):
        body(full * bufs + b, b, full)


def used(k):
    return not (isinstance(k, int) and k == 0)


class Core:
    stages = 0
    ended = []
    FEW = 45

    def __init__(self, nc, ctx, tag):
        Core.stages += 1
        self.nc, self.ctx, self.tag = nc, ctx, f"{tag}{Core.stages}"
        self.mine = []
        if len(nc.free_semaphores) < self.FEW:
            self.clear()
        ctx.callback(lambda: Core.ended.extend(self.mine))

    def sb(self, name, shape, dt=F32):
        return self.ctx.enter_context(self.nc.sbuf_tensor(f"{self.tag}_{name}", shape, dt))

    def ps(self, name, shape, dt=F32):
        return self.ctx.enter_context(self.nc.psum_tensor(f"{self.tag}_{name}", shape, dt))

    def sem(self, name, pool_dma=False):
        s = self.nc.alloc_semaphore(f"{self.tag}_{name}")
        if not pool_dma:
            self.mine.append(s)
        return s

    def clear(self):
        with self.nc.Block() as block:
            @block.sync
            def _(sp):
                for s in Core.ended:
                    sp.sem_clear(s)
        for s in Core.ended:
            self.nc.release_semaphore(s)
        Core.ended = []


class Step:

    def __init__(self, k, r, bufs):
        self.k, self.r, self.bufs = k, r, bufs
        self.t = k * bufs + r

    def lag(self, n):
        return Step(self.k, self.r - n, self.bufs)

    def slot(self, m):
        return self.r % m

    def uses(self, m):
        return self.k * (self.bufs // m) + self.r // m

    def exists(self, count):
        return not isinstance(self.k, int) or 0 <= self.t < count

    def at_least(self, n):
        return not isinstance(self.k, int) or self.t >= n


def pipeline(eng, count, lag, bufs, body, chain=None, links=0):
    full = count // bufs
    for i in range(2 * bufs):
        body(Step(i // bufs, i % bufs, bufs))
    with (chain.loop(2, full, links) if chain else eng.Fori(2, full)) as k:
        for r in range(bufs):
            body(Step(k, r, bufs))
    for i in range(full * bufs, count + lag):
        body(Step(i // bufs, i % bufs, bufs))


def since(eng, sem, step, back, per=1):
    if step.at_least(back):
        eng.wait_ge(sem, (step.t - back + 1) * per)


def build_constants(nc, k):
    with ExitStack() as ctx:
        m = Core(nc, ctx, "const")
        diff = m.sb("diff", [P, P], I32)
        node = m.sb("node", [P, P], I32)
        steps = m.sb("steps", [P, NST + 1], I32)
        part = m.sb("part", [P, 1], I32)
        iotas_written = m.sem("iotas_written")
        dve_step = m.sem("dve_step")
        block = ctx.enter_context(nc.Block())

        @block.gpsimd
        def _(pool):
            nc.gpsimd.iota(diff[:, :], [[1, P]], base=0, channel_multiplier=-1).then_inc(iotas_written, 1)
            nc.gpsimd.iota(node[:, :], [[1, P]], base=0, channel_multiplier=0).then_inc(iotas_written, 1)
            nc.gpsimd.iota(steps[:, :], [[1, NST + 1]], base=0, channel_multiplier=0).then_inc(iotas_written, 1)
            nc.gpsimd.iota(part[:, :], [[0, 1]], base=0, channel_multiplier=1).then_inc(iotas_written, 1)

        @block.vector
        def _(dve):
            c = Chain(dve, dve_step)
            dve.wait_ge(iotas_written, 4)
            nc.vector.tensor_scalar(k.ident[:, :], diff[:, :], 0, None, ALU.is_equal).then_inc(dve_step, 1)
            nc.vector.tensor_scalar(k.identb[:, :], diff[:, :], 0, None, ALU.is_equal).then_inc(dve_step, 1)
            nc.vector.tensor_scalar(k.ident_neg[:, :], diff[:, :], 0, -BIG, ALU.is_equal, ALU.mult).then_inc(dve_step, 1)
            nc.vector.tensor_scalar(k.tri[:, :], diff[:, :], 0, None, ALU.is_gt).then_inc(dve_step, 1)
            nc.vector.tensor_copy(k.node[:, :], node[:, :]).then_inc(dve_step, 1)
            nc.vector.tensor_copy(k.steps[:, :], steps[:, :]).then_inc(dve_step, 1)
            nc.vector.tensor_copy(k.part[:, :], part[:, :]).then_inc(dve_step, 1)
            nc.vector.memset(k.ones[:, :], 1.0).then_inc(dve_step, 1)


def sort_edges(nc, p, d, k):
    with ExitStack() as ctx:
        m = Core(nc, ctx, "sort")
        src = m.sb("src", [EP, EC], I32)
        dst = m.sb("dst", [EP, EC], I32)
        typ = m.sb("typ", [EP, EC], I32)
        tmp_i = m.sb("tmp_i", [EP, EC], I32)
        rec = m.sb("rec", [EP, EC, 4])
        win = m.sb("win", [EP, EC])
        mask = m.sb("mask", [EP, EC])
        run = m.sb("run", [EP, EC])
        zero = m.sb("zero", [EP, EC])
        pos = m.sb("pos", [EP, EC])
        pos_i = m.sb("pos_i", [EP, EC], I32)
        cur = m.sb("cur", [P, 1])
        off_a = m.sb("off_a", [P, 1])
        tot = m.sb("tot", [EP, W])
        nst = m.sb("nst", [P, W])
        nst_i = m.sb("nst_i", [P, W], I32)
        ends = m.sb("ends", [P, W])
        off = m.sb("off", [P, W])
        wst = m.sb("wst", [P, NST + 1])
        empty = m.sb("empty", [P, NST * J, 4])
        st_rec = [m.sb(f"st_rec{b}", [EP, SCAT_COLS, 4], I32) for b in range(SCAT_BUFS)]
        st_pos = [m.sb(f"st_pos{b}", [EP, SCAT_COLS], I32) for b in range(SCAT_BUFS)]
        before_ps = m.ps("before_ps", [P, W])
        total_ps = m.ps("total_ps", [P, W])
        edges_in = m.sem("edges_in")
        empties_set = m.sem("empties_set")
        empties_out = m.sem("empties_out")
        dve_step = m.sem("dve_step")
        totals_ready = m.sem("totals_ready")
        prefix_ready = m.sem("prefix_ready")
        staged = m.sem("staged")
        issue_step = m.sem("issue_step")
        scattered = [m.sem(f"scattered{b}", pool_dma=True) for b in range(SCAT_BUFS)]
        rounds = EC // (SCAT_BUFS * SCAT_COLS)
        block = ctx.enter_context(nc.Block())

        @block.sync
        def _(sp):
            for name, to in (("src", src), ("dst", dst), ("edge_type_64", typ)):
                sp.dma_start(to[:, :], p[name].rearrange("(p t) -> p t", p=EP)).then_inc(edges_in, 16)
            sp.wait_ge(empties_set, 2)
            sp.dma_start(d.slots.rearrange("(p t) f -> p t f", p=P), empty[:, :, :].bitcast(I32)).then_inc(empties_out, 16)
            sp.wait_ge(empties_out, 16)

        @block.gpsimd
        def _(pool):
            nc.gpsimd.memset(empty[:, :, :], 0.0).then_inc(empties_set, 1)
            pool.wait_ge(empties_set, 1)
            nc.gpsimd.memset(empty[:, :, 0:1], -1.0).then_inc(empties_set, 1)
            pool.wait_ge(empties_out, 16)

            def scatter(t, b, kk):
                pool.wait_ge(staged, (t + 1) * 2)
                pool.sem_inc(issue_step, 1)
                for j in range(SCAT_COLS):
                    pool.indirect_dma_start(d.slots, bass.IndirectOffsetOnAxis(ap=st_pos[b][:, j:j + 1], axis=0),
                                            st_rec[b][:, j, :], None).then_inc(scattered[b], 16)
            ring(pool, rounds * SCAT_BUFS, SCAT_BUFS, scatter)
            for b in range(SCAT_BUFS):
                pool.wait_ge(scattered[b], 16 * SCAT_COLS * rounds)

        @block.tensor
        def _(pe):
            pe.wait_ge(totals_ready, 1)
            nc.tensor.matmul(before_ps[0:EP, :], k.tri[0:EP, 0:EP], tot[:, :], start=True, stop=True).then_inc(prefix_ready, 1)
            nc.tensor.matmul(total_ps[:, :], k.ones[0:EP, :], tot[:, :], start=True, stop=True).then_inc(prefix_ready, 1)

        @block.vector
        def _(dve):
            c = Chain(dve, dve_step)
            c.link(nc.vector.memset(cur[:, :], 0.0))
            c.link(nc.vector.memset(zero[:, :], 0.0))
            c.link(nc.vector.memset(pos[:, :], 0.0))
            c.link(nc.vector.memset(wst[:, :], 0.0))
            dve.wait_ge(edges_in, 48)
            c.link(nc.vector.tensor_scalar(tmp_i[:, :], src[:, :], P - 1, None, ALU.bitwise_and))
            c.link(nc.vector.tensor_copy(rec[:, :, 0], tmp_i[:, :]))
            c.link(nc.vector.tensor_scalar(rec[:, :, 1], dst[:, :], -float(MID), None, ALU.add))
            c.link(nc.vector.tensor_copy(rec[:, :, 2], typ[:, :]))
            c.link(nc.vector.tensor_copy(rec[:, :, 3].bitcast(I32), dst[:, :]))
            c.link(nc.vector.tensor_scalar(tmp_i[:, :], src[:, :], 7, None, ALU.logical_shift_right))
            c.link(nc.vector.tensor_copy(win[:, :], tmp_i[:, :]))
            with c.loop(0, W, 3) as a:
                c.link(nc.vector.tensor_scalar(mask[:, :], win[:, :], cur[0:EP, :], None, ALU.is_equal))
                c.link(nc.vector.tensor_reduce(tot[:, bass.ds(a, 1)], mask[:, :], AX.X, ALU.add))
                c.link(nc.vector.tensor_scalar(cur[:, :], cur[:, :], 1.0, None, ALU.add))
            c.link(nc.vector.memset(cur[:, :], 0.0))
            nc.vector.memset(nst[:, :], 0.0).then_inc(totals_ready, 1)
            dve.wait_ge(prefix_ready, 2)
            c.link(nc.vector.tensor_scalar(nst_i[:, :], total_ps[:, :], 1.0, S - 1.0, ALU.max, ALU.add))
            c.link(nc.vector.tensor_scalar(nst_i[:, :], nst_i[:, :], SHIFT, None, ALU.logical_shift_right))
            c.link(nc.vector.tensor_copy(nst[:, :], nst_i[:, :]))
            c.link(nc.vector.tensor_tensor_scan(ends[:, :], nst[:, :], zero_row(k), 0.0, ALU.add, ALU.add))
            c.link(nc.vector.tensor_tensor(off[:, :], ends[:, :], nst[:, :], ALU.subtract))
            c.link(nc.vector.tensor_scalar(off[:, :], off[:, :], float(S), -1.0, ALU.mult, ALU.add))
            c.link(nc.vector.tensor_tensor(off[0:EP, :], off[0:EP, :], before_ps[0:EP, :], ALU.add))
            with c.loop(0, W, 6) as a:
                c.link(nc.vector.tensor_scalar(mask[:, :], win[:, :], cur[0:EP, :], None, ALU.is_equal))
                c.link(nc.vector.tensor_copy(off_a[0:EP, :], off[0:EP, bass.ds(a, 1)]))
                c.link(nc.vector.tensor_tensor_scan(run[:, :], mask[:, :], zero[:, :], off_a[0:EP, :], ALU.add, ALU.add))
                c.link(nc.vector.tensor_tensor(run[:, :], run[:, :], mask[:, :], ALU.mult))
                c.link(nc.vector.tensor_tensor(pos[:, :], pos[:, :], run[:, :], ALU.add))
                c.link(nc.vector.tensor_scalar(cur[:, :], cur[:, :], 1.0, None, ALU.add))
            c.link(nc.vector.tensor_copy(pos_i[:, :], pos[:, :]))

            def stage(t, b, kk):
                if used(kk):
                    dve.wait_ge(scattered[b], kk * 16 * SCAT_COLS)
                nc.vector.tensor_scalar(st_pos[b][:, :], pos_i[:, bass.ds(t * SCAT_COLS, SCAT_COLS)], 0, None,
                                        ALU.bitwise_or).then_inc(staged, 1)
                nc.vector.tensor_scalar(st_rec[b][:, :, :], rec[:, bass.ds(t * SCAT_COLS, SCAT_COLS), :].bitcast(I32), 0,
                                        None, ALU.bitwise_or).then_inc(staged, 1)
            ring(dve, rounds * SCAT_BUFS, SCAT_BUFS, stage)
            with c.loop(0, W, 2) as a:
                c.link(nc.vector.tensor_copy(off_a[:, :], ends[:, bass.ds(a, 1)]))
                c.link(nc.vector.scalar_tensor_tensor(wst[:, :], k.steps[:, :], off_a[:, :], wst[:, :], ALU.is_ge, ALU.add))
            c.link(nc.vector.tensor_copy(k.window_of[:, :], wst[:, 0:NST]))
            c.link(nc.vector.tensor_tensor(k.last_of[:, :], wst[:, 0:NST], wst[:, 1:NST + 1], ALU.not_equal))
            c.link(nc.vector.memset(k.cap[:, :], 0.0))
            c.link(nc.vector.tensor_tensor(k.cap[:, 1:NST], wst[:, 0:NST - 1], wst[:, 1:NST], ALU.is_equal))
            c.link(nc.vector.tensor_scalar(k.cap[:, :], k.cap[:, :], 2 * BIG, -BIG, ALU.mult, ALU.add))


def zero_row(k):
    return k.zeros[:, 0:W]


def count_pairs(nc, d, k):
    with ExitStack() as ctx:
        m = Core(nc, ctx, "count")
        tail_i = m.sb("tail_i", [P, NP], I32)
        tail = m.sb("tail", [P, NP], F16)
        iota_written = m.sem("iota_written")
        tail_set = m.sem("tail_set")
        rec = [m.sb(f"rec{b}", [P, J, 4]) for b in range(2)]
        head_hot = [m.sb(f"head_hot{b}", [P, J, P], BF16) for b in range(2)]
        tail_hot = [m.sb(f"tail_hot{b}", [P, J, NP], BF16) for b in range(2)]
        cum = [m.sb(f"cum{b}", [P, NP]) for b in range(2)]
        acc = m.ps("acc", [P, NCH, 512])
        rec_in = [m.sem(f"rec_in{b}") for b in range(2)]
        hot_ready = m.sem("hot_ready")
        counted = m.sem("counted")
        cleared = m.sem("cleared")
        copied = m.sem("copied")
        cum_out = [m.sem(f"cum_out{b}", pool_dma=True) for b in range(2)]
        block = ctx.enter_context(nc.Block())
        slots = d.slots.rearrange("(s p j) f -> s p (j f)", p=P, j=J)

        @block.sync
        def _(sp):
            def step(t, b, kk):
                if used(kk):
                    sp.wait_ge(hot_ready, (t - 1) * 2 * J)
                sp.dma_start(rec[b][:, :, :].rearrange("p j f -> p (j f)").bitcast(I32), slots[bass.ds(t, 1), :, :].rearrange("s p f -> p (s f)")).then_inc(rec_in[b], 16)
            ring(sp, NST, 2, step)

        @block.gpsimd
        def _(pool):
            nc.gpsimd.iota(tail_i[:, :], [[1, NP]], base=-MID, channel_multiplier=0).then_inc(iota_written, 1)

            def step(t, b, kk):
                w = pool.value_load(k.window_of[0:1, bass.ds(t, 1)], min_val=0, max_val=W)
                last = pool.value_load(k.last_of[0:1, bass.ds(t, 1)], min_val=0, max_val=1)
                pool.wait_ge(copied, (t + 1) * NCH)
                pool.sem_inc(k.issue, 1)
                pool.dma_start(d.cum[bass.ds(w, 1), :, :].rearrange("s p f -> p (s f)"), cum[b][:, :], cond=last).then_inc(cum_out[b], 16)
            ring(pool, NST, 2, step)
            for b in range(2):
                pool.wait_ge(cum_out[b], 16 * (NST // 2))

        @block.vector
        def _(dve):
            dve.wait_ge(iota_written, 1)
            nc.vector.tensor_copy(tail[:, :], tail_i[:, :]).then_inc(tail_set, 1)
            dve.wait_ge(tail_set, 1)

            def step(t, b, kk):
                dve.wait_ge(rec_in[b], (kk + 1) * 16)
                if used(kk):
                    dve.wait_ge(counted, (t - 1) * NCH)
                for j in range(J):
                    nc.vector.tensor_scalar(head_hot[b][:, j, :], k.node[:, :], rec[b][:, j, 0:1], None,
                                            ALU.is_equal).then_inc(hot_ready, 1)
                for j in range(J):
                    nc.vector.tensor_scalar(tail_hot[b][:, j, :], tail[:, :], rec[b][:, j, 1:2], None,
                                            ALU.is_equal).then_inc(hot_ready, 1)
            ring(dve, NST, 2, step)

        @block.tensor
        def _(pe):
            for c in range(NCH):
                nc.tensor.matmul(acc[:, c, 0:CH], k.zerosb[:, 0:P], k.zerosb[:, 0:CH], start=True, stop=False,
                                 skip_group_check=True).then_inc(cleared, 1)

            def step(t, b, kk):
                pe.wait_ge(hot_ready, (t + 1) * 2 * J)
                for c in range(NCH):
                    if used(kk) or b:
                        pe.wait_ge(copied, (t - 1) * NCH + c + 1)
                    for j in range(J):
                        mm = nc.tensor.matmul(acc[:, c, 0:CH], head_hot[b][:, j, :], tail_hot[b][:, j, c * CH:(c + 1) * CH],
                                              start=False, stop=False, skip_group_check=True)
                    mm.then_inc(counted, 1)
            ring(pe, NST, 2, step)

        @block.scalar
        def _(act):
            def step(t, b, kk):
                if used(kk):
                    act.wait_ge(cum_out[b], kk * 16)
                for c in range(NCH):
                    act.wait_ge(counted, t * NCH + c + 1)
                    nc.scalar.copy(cum[b][:, c * CH:(c + 1) * CH], acc[:, c, 0:CH]).then_inc(copied, 1)
            ring(act, NST, 2, step)


def split_counts(nc, d, k):
    B = 3
    G = -(-W // 4)
    with ExitStack() as ctx:
        m = Core(nc, ctx, "split")
        cum = [m.sb(f"cum{b}", [P, NP]) for b in range(B)]
        cnt = [m.sb(f"cnt{b}", [P, NP]) for b in range(B)]
        cntT = [m.sb(f"cntT{b}", [P, NP]) for b in range(B)]
        ps = m.ps("ps", [P, G, 512])
        cum_in = [m.sem(f"cum_in{b}") for b in range(B)]
        cnt_ready = m.sem("cnt_ready")
        turned = m.sem("turned")
        turned_copied = m.sem("turned_copied")
        degree_ready = m.sem("degree_ready")
        cnt_out = [m.sem(f"cnt_out{b}", pool_dma=True) for b in range(B)]
        cntT_out = [m.sem(f"cntT_out{b}", pool_dma=True) for b in range(B)]
        block = ctx.enter_context(nc.Block())
        cntT_cols = d.cntT.rearrange("j p (w n) -> p j w n", n=P)

        @block.sync
        def _(sp):
            def load(t, b, kk):
                if used(kk):
                    sp.wait_ge(cnt_ready, t - 1)
                sp.dma_start(cum[b][:, :], d.cum[bass.ds(t, 1), :, :].rearrange("s p f -> p (s f)")).then_inc(cum_in[b], 16)
            ring(sp, W, B, load)

        @block.gpsimd
        def _(pool):
            def store(t, b, kk):
                pool.wait_ge(cnt_ready, t + 1)
                pool.sem_inc(k.issue, 1)
                pool.dma_start(d.cnt[bass.ds(t, 1), :, :].rearrange("s p f -> p (s f)"), cnt[b][:, :]).then_inc(cnt_out[b], 16)
                pool.wait_ge(turned_copied, (t + 1) * G)
                pool.sem_inc(k.issue, 1)
                pool.dma_start(cntT_cols[:, :, bass.ds(t, 1), :].rearrange("p j w n -> p (j w) n"),
                               cntT[b][:, :].rearrange("p (j n) -> p j n", n=P)).then_inc(cntT_out[b], 16)
            ring(pool, W, B, store)
            for b in range(B):
                pool.wait_ge(cnt_out[b], 16 * ((W + B - 1 - b) // B))
                pool.wait_ge(cntT_out[b], 16 * ((W + B - 1 - b) // B))

        @block.vector
        def _(dve):
            def step(t, b, kk):
                dve.wait_ge(cum_in[b], (kk + 1) * 16)
                if used(kk):
                    dve.wait_ge(cnt_out[b], kk * 16)
                    dve.wait_ge(turned, (t - B + 1) * G)
                    dve.wait_ge(degree_ready, t - B + 1)
                if used(kk) or b:
                    nc.vector.tensor_tensor(cnt[b][:, :], cum[b][:, :], cum[(b - 1) % B][:, :], ALU.subtract).then_inc(cnt_ready, 1)
                else:
                    nc.vector.tensor_copy(cnt[b][:, :], cum[b][:, :]).then_inc(cnt_ready, 1)
                dve.wait_ge(cnt_ready, t + 1)
                nc.vector.tensor_reduce(k.degree[:, bass.ds(t, 1)], cnt[b][:, :], AX.X, ALU.add).then_inc(degree_ready, 1)
            ring(dve, W, B, step)

        @block.tensor
        def _(pe):
            def step(t, b, kk):
                pe.wait_ge(cnt_ready, t + 1)
                for g in range(G):
                    if used(kk) or b:
                        pe.wait_ge(turned_copied, (t - 1) * G + g + 1)
                    for j in range(4 * g, min(4 * g + 4, W)):
                        mm = nc.tensor.transpose(ps[:, g, (j % 4) * P:(j % 4 + 1) * P], cnt[b][:, j * P:(j + 1) * P], k.ident[:, :])
                    mm.then_inc(turned, 1)
            ring(pe, W, B, step)

        @block.scalar
        def _(act):
            def step(t, b, kk):
                if used(kk):
                    act.wait_ge(cntT_out[b], kk * 16)
                for g in range(G):
                    n = min(4, W - 4 * g) * P
                    act.wait_ge(turned, t * G + g + 1)
                    nc.scalar.copy(cntT[b][:, g * 512:g * 512 + n], ps[:, g, 0:n]).then_inc(turned_copied, 1)
            ring(act, W, B, step)


def bc(ap, shape):
    return ap.broadcast_to(shape)


def turn(nc, k, nodes, cols, tag):
    G = -(-W // 4)
    with ExitStack() as ctx:
        m = Core(nc, ctx, tag)
        ps = m.ps("ps", [P, G, 512])
        turned = m.sem("turned")
        block = ctx.enter_context(nc.Block())

        @block.tensor
        def _(pe):
            for w in range(W):
                mm = nc.tensor.transpose(ps[:, w // 4, (w % 4) * P:(w % 4 + 1) * P], nodes[:, w * P:(w + 1) * P], k.ident[:, :])
                if w % 4 == 3 or w == W - 1:
                    mm.then_inc(turned, 1)

        @block.scalar
        def _(act):
            for g in range(G):
                n = min(4, W - 4 * g) * P
                act.wait_ge(turned, g + 1)
                nc.scalar.copy(cols[:, g * 512:g * 512 + n], ps[:, g, 0:n])


def load_inputs(nc, p, k):
    with ExitStack() as ctx:
        m = Core(nc, ctx, "load")
        cleared = m.sem("cleared")
        x_in = m.sem("x_in")
        block = ctx.enter_context(nc.Block())

        @block.vector
        def _(dve):
            nc.vector.memset(k.x[:, :], 0.0).then_inc(cleared, 1)

        @block.sync
        def _(sp):
            sp.wait_ge(cleared, 1)
            x = k.x[:, :].rearrange("p (w d) -> p w d", d=D)
            sp.dma_start(x[:, 0:W - 1, :], p['x'][0:(W - 1) * P, :].rearrange("(w p) d -> p w d", p=P)).then_inc(x_in, 16)
            sp.dma_start(x[0:TAIL, W - 1, :], p['x'][(W - 1) * P:N, :]).then_inc(x_in, 16)
            sp.wait_ge(x_in, 32)


def attention_project(nc, p, d, k, xT, row_s, row_d):
    G = -(-W // 4)
    with ExitStack() as ctx:
        m = Core(nc, ctx, "proj")
        coef = m.sb("coef", [P, 3])
        lw = m.sb("lw", [P, 3, D])
        raw = {n: m.sb(n, [P, 3, D]) for n in ("bias", "att_src", "att_dst")}
        mixed = {n: m.sb(n + "_mix", [P, D]) for n in ("weight", "bias", "att_src", "att_dst")}
        names = ["weight", "bias", "att_src", "att_dst"]
        flipped = {n: m.sb(n + "_T", [P, D]) for n in names}
        ge = m.sb("ge", [P, H + 1])
        head_s = m.sb("head_s", [P, H, P])
        head_d = m.sb("head_d", [P, H, P])
        xt = m.sb("xt", [P, NP])
        xtT = m.sb("xtT", [P, NP])
        tmp = xT
        flag = m.sb("flag", [P, 1])
        lhs = m.sb("lhs", [P, W, k.LHS])
        ps = m.ps("ps", [P, NCH, 512])
        params_in = m.sem("params_in")
        mixes_ready = m.sem("mixes_ready")
        flips = m.sem("flips")
        flips_ready = m.sem("flips_ready")
        xt_summed = m.sem("xt_summed")
        xt_ready = m.sem("xt_ready")
        xtT_summed = m.sem("xtT_summed")
        xtT_ready = m.sem("xtT_ready")
        row_summed = m.sem("row_summed")
        row_ready = m.sem("row_ready")
        dve_step = m.sem("dve_step")
        lhs_ready = m.sem("lhs_ready")
        lhs_out = m.sem("lhs_out")
        block = ctx.enter_context(nc.Block())

        @block.sync
        def _(sp):
            sp.dma_start(coef[:, :], p['L0_gnn_coeffs_t'].partition_broadcast(P)).then_inc(params_in, 16)
            sp.dma_start(lw[:, :, :], p['L0_gnn_lin_weight'].rearrange("b o i -> o b i")).then_inc(params_in, 16)
            sp.dma_start(raw["bias"][:, :, :], p['L0_gnn_lin_bias'].partition_broadcast(P)).then_inc(params_in, 16)
            for n in ("att_src", "att_dst"):
                sp.dma_start(raw[n][:, :, :], p['L0_gnn_' + n].rearrange("b q h c -> (b q) (h c)").partition_broadcast(P)).then_inc(params_in, 16)
            sp.wait_ge(lhs_ready, 1)
            sp.dma_start(d.lhs.rearrange("w p f -> p w f"), lhs[:, :, :]).then_inc(lhs_out, 16)
            sp.wait_ge(lhs_out, 16)

        @block.tensor
        def _(pe):
            pe.wait_ge(mixes_ready, 1)
            for n, name in enumerate(names):
                mm = nc.tensor.transpose(ps[:, 7, n * P:(n + 1) * P], mixed[name][:, :], k.ident[:, :])
            mm.then_inc(flips, 1)
            pe.wait_ge(flips_ready, 1)
            for w in range(W):
                mm = nc.tensor.matmul(ps[:, w // 4, (w % 4) * P:(w % 4 + 1) * P], xT[:, w * P:(w + 1) * P],
                                      flipped["weight"][:, :], start=True, stop=True)
                if w % 4 == 3 or w == W - 1:
                    mm.then_inc(xt_summed, 1)
            for c in range(NCH):
                if c < G:
                    pe.wait_ge(xt_ready, c + 1)
                nc.tensor.matmul(ps[:, c, 0:CH], flipped["weight"][:, :], xT[:, c * CH:(c + 1) * CH], start=True,
                                 stop=True).then_inc(xtT_summed, 1)
            pe.wait_ge(xtT_ready, NCH)
            for r in range(2 * H):
                for c in range(NCH):
                    if r:
                        pe.wait_ge(row_ready, (r - 1) * NCH + c + 1)
                    nc.tensor.matmul(ps[:, c, 0:CH], (head_s if r < H else head_d)[:, r % H, :],
                                     xtT[:, c * CH:(c + 1) * CH], start=True, stop=True).then_inc(row_summed, 1)

        @block.scalar
        def _(act):
            act.wait_ge(flips_ready, 1)
            for c in range(NCH):
                act.wait_ge(xtT_summed, c + 1)
                nc.scalar.activation(xtT[:, c * CH:(c + 1) * CH], ps[:, c, 0:CH], ACT.Identity,
                                     bias=flipped["bias"][:, 0:1]).then_inc(xtT_ready, 1)
            for r in range(2 * H):
                for c in range(NCH):
                    act.wait_ge(row_summed, r * NCH + c + 1)
                    nc.scalar.copy((row_s if r < H else row_d)[:, r % H, c * CH:(c + 1) * CH], ps[:, c, 0:CH]).then_inc(row_ready, 1)

        @block.vector
        def _(dve):
            c = Chain(dve, dve_step)
            c.link(nc.vector.memset(lhs[:, :, :], 0.0))
            dve.wait_ge(params_in, 5 * 16)
            for name in names:
                r = lw if name == "weight" else raw[name]
                c.link(nc.vector.tensor_scalar(mixed[name][:, :], r[:, 0, :], coef[:, 0:1], None, ALU.mult))
                for b in (1, 2):
                    c.link(nc.vector.scalar_tensor_tensor(mixed[name][:, :], r[:, b, :], coef[:, b:b + 1],
                                                          mixed[name][:, :], ALU.mult, ALU.add))
            c.link(nc.vector.tensor_scalar(ge[:, :], k.steps[:, 0:H + 1], float(C), k.part[:, 0:1], ALU.mult, ALU.is_le))
            c.link(nc.vector.tensor_tensor(ge[:, 0:H], ge[:, 0:H], ge[:, 1:H + 1], ALU.subtract))
            nc.vector.tensor_copy(flag[:, :], ge[:, 0:1]).then_inc(mixes_ready, 1)
            dve.wait_ge(flips, 1)
            for n, name in enumerate(names):
                c.link(nc.vector.tensor_copy(flipped[name][:, :], ps[:, 7, n * P:(n + 1) * P]))
            for h in range(H):
                c.link(nc.vector.tensor_scalar(head_s[:, h, :], flipped["att_src"][:, :], ge[:, h:h + 1], None, ALU.mult))
                c.link(nc.vector.tensor_scalar(head_d[:, h, :], flipped["att_dst"][:, :], ge[:, h:h + 1], None, ALU.mult))
            nc.vector.tensor_copy(flag[:, :], ge[:, 0:1]).then_inc(flips_ready, 1)
            for g in range(G):
                n = min(4, W - 4 * g)
                dve.wait_ge(xt_summed, g + 1)
                nc.vector.tensor_tensor(xt[:, g * 512:g * 512 + n * P].rearrange("p (w f) -> p w f", f=P),
                                        ps[:, g, 0:n * P].rearrange("p (w f) -> p w f", f=P),
                                        bc(mixed["bias"][:, None, :], [P, n, P]), ALU.add).then_inc(xt_ready, 1)
            dve.wait_ge(xt_ready, G)
            dve.wait_ge(xtT_summed, NCH)
            xt3 = xt[:, :].rearrange("p (w f) -> p w f", f=P)
            tmp3 = tmp[:, :].rearrange("p (w f) -> p w f", f=P)
            for name, to in (("att_src", k.col_s), ("att_dst", k.col_d)):
                c.link(nc.vector.tensor_tensor(tmp3, xt3, bc(mixed[name][:, None, :], [P, W, P]), ALU.mult))
                c.link(nc.vector.tensor_reduce(to[:, :], tmp[:, :].rearrange("p (w c) -> p w c", c=C), AX.X, ALU.add))
            HW = C + 1
            for h in range(H):
                at = h * 3 * HW + h * HW if h < 3 else 9 * HW
                c.link(nc.vector.tensor_copy(lhs[:, :, at:at + C], xt3[:, :, h * C:(h + 1) * C]))
                c.link(nc.vector.memset(lhs[:, :, at + C:at + HW], 1.0))
            cs = k.col_s[:, :].rearrange("p (w h) -> p w h", h=H)
            c.link(nc.vector.tensor_copy(lhs[:, :, 10 * HW:10 * HW + H], cs))
            nc.vector.tensor_scalar(lhs[:, :, 10 * HW + H:10 * HW + 2 * H], cs, 0.2, None, ALU.mult).then_inc(lhs_ready, 1)


def attention_max(nc, d, k, row_s):
    with ExitStack() as ctx:
        m = Core(nc, ctx, "amax")
        cnt = [m.sb(f"cnt{b}", [P, NP]) for b in range(2)]
        masked = [m.sb(f"masked{b}", [P, NP]) for b in range(2)]
        spare = m.sb("spare", [P, H, NP], BF16)
        best = [m.sb(f"best{b}", [P, H]) for b in range(2)]
        go = m.sb("go", [P, 1])
        z = m.sb("z", [P, W * H])
        cnt_in = [m.sem(f"cnt_in{b}") for b in range(2)]
        masks_made = m.sem("masks_made")
        mask_seen = m.sem("mask_seen")
        maxima_found = m.sem("maxima_found")
        maxima_kept = m.sem("maxima_kept")
        dve_step = m.sem("dve_step")
        block = ctx.enter_context(nc.Block())

        @block.sync
        def _(sp):
            def load(t, b, kk):
                if used(kk):
                    sp.wait_ge(masks_made, t - 1)
                sp.dma_start(cnt[b][:, :], d.cntT[bass.ds(t, 1), :, :].rearrange("s p f -> p (s f)")).then_inc(cnt_in[b], 16)
            ring(sp, W, 2, load)

        @block.vector
        def _(dve):
            c = Chain(dve, dve_step)

            def keep(t, b):
                dve.wait_ge(maxima_found, (t + 1) * H)
                nc.vector.tensor_scalar(k.amax[:, bass.ds(t * H, H)], best[b][:, :], 0.0, None, ALU.add).then_inc(maxima_kept, 1)

            def step(t, b, kk):
                dve.wait_ge(cnt_in[b], (kk + 1) * 16)
                nc.vector.tensor_scalar(masked[b][:, :], cnt[b][:, :], 0.0, -BIG, ALU.is_equal, ALU.mult).then_inc(masks_made, 1)
                if used(kk) or b:
                    keep(t - 1, 1 - b)
                dve.wait_ge(masks_made, t + 1)
                nc.vector.tensor_copy(go[:, :], masked[b][:, 0:1]).then_inc(mask_seen, 1)
                for h in range(H):
                    nc.vector.tensor_tensor_reduce(spare[:, h, :], masked[b][:, :], row_s[:, h, :], 1.0, -3.0e38, ALU.add, ALU.max,
                                                   best[b][:, h:h + 1]).then_inc(maxima_found, 1)
            ring(dve, W, 2, step)
            keep(W - 1, (W - 1) % 2)
            dve.wait_ge(maxima_kept, W)
            c.link(nc.vector.tensor_tensor(z[:, :], k.amax[:, :], k.col_d[:, :], ALU.add))
            c.link(nc.vector.scalar_tensor_tensor(k.amax[:, :], z[:, :], 0.2, z[:, :], ALU.mult, ALU.max))


def attention_rows(nc, k, row_d, pos_row, neg_row, w0, n):
    with ExitStack() as ctx:
        m = Core(nc, ctx, "rows")
        ps = m.ps("ps", [P, 8, 512])
        spread = m.sem("spread")
        rows_made = m.sem("rows_made")
        block = ctx.enter_context(nc.Block())
        groups = [(h, g) for h in range(H) for g in range(0, n, 4)]

        @block.tensor
        def _(pe):
            for i, (h, g) in enumerate(groups):
                if i >= 8:
                    pe.wait_ge(rows_made, 2 * (i - 7))
                for j in range(g, min(g + 4, n)):
                    col = k.amax[:, (w0 + j) * H + h:(w0 + j) * H + h + 1]
                    mm = nc.tensor.matmul(ps[:, i % 8, (j - g) * P:(j - g + 1) * P], bc(col, [P, P]), k.ident[:, :],
                                          start=True, stop=True)
                mm.then_inc(spread, 1)

        @block.vector
        def _(dve):
            for i, (h, g) in enumerate(groups):
                q = min(4, n - g) * P
                dve.wait_ge(spread, i + 1)
                r = row_d[:, h, (w0 + g) * P:(w0 + g) * P + q]
                nc.vector.tensor_tensor(pos_row[:, h, g * P:g * P + q], r, ps[:, i % 8, 0:q], ALU.subtract).then_inc(rows_made, 1)
                nc.vector.scalar_tensor_tensor(neg_row[:, h, g * P:g * P + q], r, 0.2, ps[:, i % 8, 0:q], ALU.mult,
                                               ALU.subtract).then_inc(rows_made, 1)


def attention_sum(nc, d, k, pos_row, neg_row, w0, n):
    HW = C + 1
    NT = n * P
    QC = NT // 4
    with ExitStack() as ctx:
        m = Core(nc, ctx, "asum")
        cnt = [m.sb(f"cnt{b}", [P, NT]) for b in range(2)]
        lhs = [m.sb(f"lhs{b}", [P, k.LHS]) for b in range(2)]
        low = [m.sb(f"low{b}", [P, NT]) for b in range(2)]
        e = [m.sb(f"e{b}", [P, NT]) for b in range(2)]
        wt = [m.sb(f"wt{b}", [P, NT]) for b in range(3)]
        sums = m.sb("sums", [P, NT])
        sums3 = m.sb("sums3", [P, NT])
        o = m.sb("o", [P, n, H, HW])
        den = m.sb("den", [P, n * H])
        ps = m.ps("ps", [P, 8, 512])
        in_ = [m.sem(f"in{b}") for b in range(2)]
        low_ready = m.sem("low_ready")
        raised = m.sem("raised")
        act_bound = m.sem("act_bound")
        dve_bound = m.sem("dve_bound")
        exp_ready = m.sem("exp_ready")
        dve_weighted = m.sem("dve_weighted")
        pool_weighted = m.sem("pool_weighted")
        weight_used = m.sem("weight_used")
        sums_copied = m.sem("sums_copied")
        turned = m.sem("turned")
        o_copied = m.sem("o_copied")
        dve_step = m.sem("dve_step")
        block = ctx.enter_context(nc.Block())
        NG = -(-n // 3)

        @block.sync
        def _(sp):
            def load(t, b, kk):
                if used(kk):
                    sp.wait_ge(weight_used, (t - 1) * H)
                sp.dma_start(cnt[b][:, :], d.cnt[bass.ds(t, 1), :, w0 * P:w0 * P + NT].rearrange("s p f -> p (s f)")).then_inc(in_[b], 16)
                sp.dma_start(lhs[b][:, :], d.lhs[bass.ds(t, 1), :, :].rearrange("s p f -> p (s f)")).then_inc(in_[b], 16)
            ring(sp, W, 2, load)

        @block.scalar
        def _(act):
            def exp(t, h):
                x = e[h % 2][:, :]
                if h % 2 == 0:
                    act.wait_ge(raised, t * H + h + 1)
                    nc.scalar.activation(x, x, ACT.Relu, scale=-1.0).then_inc(act_bound, 1)
                    act.wait_ge(act_bound, t * 2 + h // 2 + 1)
                    nc.scalar.activation(x, x, ACT.Exp, scale=-1.0).then_inc(exp_ready, 1)
                else:
                    act.wait_ge(dve_bound, t * 2 + h // 2 + 1)
                    nc.scalar.activation(x, x, ACT.Exp).then_inc(exp_ready, 1)

            def step(t, b, kk):
                act.wait_ge(in_[b], (kk + 1) * 32)
                for h in range(H):
                    s = h % 2
                    if used(kk) or b or h >= 2:
                        act.wait_ge(raised, t * H + h - 1)
                    nc.scalar.activation(low[s][:, :], neg_row[:, h, :], ACT.Identity,
                                         bias=lhs[b][:, 10 * HW + H + h:10 * HW + H + h + 1]).then_inc(low_ready, 1)
                    if h:
                        exp(t, h - 1)
                    elif used(kk) or b:
                        exp(t - 1, H - 1)
            ring(act, W, 2, step)
            exp(W - 1, H - 1)
            act.wait_ge(weight_used, W * H)
            for c in range(4):
                nc.scalar.copy(sums[0:3 * HW, c * QC:(c + 1) * QC], ps[0:3 * HW, c, 0:QC]).then_inc(sums_copied, 1)
                nc.scalar.copy(sums3[0:HW, c * QC:(c + 1) * QC], ps[0:HW, 4 + c, 0:QC]).then_inc(sums_copied, 1)
            for g in range(NG):
                r = min(3, n - 3 * g)
                act.wait_ge(turned, g + 1)
                nc.scalar.copy(o[:, 3 * g:3 * g + r, :, :].rearrange("p w h c -> p (w h c)"), ps[:, g, 0:r * H * HW]).then_inc(o_copied, 1)

        @block.gpsimd
        def _(pool):
            def step(t, b, kk):
                if used(kk) or b:
                    pool.wait_ge(weight_used, t * H)
                pool.wait_ge(exp_ready, t * H + H)
                nc.gpsimd.tensor_tensor(wt[2][:, :], e[1][:, :], cnt[b][:, :], ALU.mult).then_inc(pool_weighted, 1)
            ring(pool, W, 2, step)

        @block.vector
        def _(dve):
            c = Chain(dve, dve_step)

            def weight(t, h, b, again):
                dve.wait_ge(exp_ready, t * H + h + 1)
                if again or h == 2:
                    dve.wait_ge(weight_used, t * H + h - 1)
                nc.vector.tensor_tensor(wt[h % 2][:, :], e[h % 2][:, :], cnt[b][:, :], ALU.mult).then_inc(dve_weighted, 1)

            def step(t, b, kk):
                again = used(kk) or b
                dve.wait_ge(in_[b], (kk + 1) * 32)
                for h in range(H):
                    s = h % 2
                    dve.wait_ge(low_ready, t * H + h + 1)
                    if h < 2 and again:
                        if h == 0:
                            dve.wait_ge(dve_weighted, t * 3)
                        else:
                            dve.wait_ge(pool_weighted, t)
                    if h >= 2:
                        dve.wait_ge(dve_weighted, t * 3 + h - 1)
                    nc.vector.scalar_tensor_tensor(e[s][:, :], pos_row[:, h, :], lhs[b][:, 10 * HW + h:10 * HW + h + 1],
                                                   low[s][:, :], ALU.add, ALU.max).then_inc(raised, 1)
                    if h % 2:
                        dve.wait_ge(raised, t * H + h + 1)
                        nc.vector.tensor_scalar(e[s][:, :], e[s][:, :], 1.0, None, ALU.min).then_inc(dve_bound, 1)
                    if h:
                        weight(t, h - 1, b, again)
            ring(dve, W, 2, step)
            dve.wait_ge(o_copied, NG)
            c.link(nc.vector.tensor_scalar(den[:, :], o[:, :, :, C].rearrange("p w h -> p (w h)"), 1e-16, None, ALU.add))
            c.link(nc.vector.reciprocal(den[:, :], den[:, :]))
            x = k.x[:, w0 * P:w0 * P + NT].rearrange("p (w c) -> p w c", c=C)
            o3 = o[:, :, :, :].rearrange("p w h c -> p (w h) c")[:, :, 0:C]
            c.link(nc.vector.tensor_tensor(o3, o3, bc(den[:, :, None], [P, n * H, C]), ALU.mult))
            c.link(nc.vector.tensor_tensor(x, x, o3, ALU.add))

        @block.tensor
        def _(pe):
            def step(t, b, kk):
                pe.wait_ge(in_[b], (kk + 1) * 32)
                first, last = isinstance(t, int) and t == 0, isinstance(t, int) and t == W - 1
                for h in range(H):
                    if h < 3:
                        pe.wait_ge(dve_weighted, t * 3 + h + 1)
                    else:
                        pe.wait_ge(pool_weighted, t + 1)
                    rows = 3 * HW if h < 3 else HW
                    at = h * 3 * HW
                    for c in range(4):
                        mm = nc.tensor.matmul(ps[0:rows, (0 if h < 3 else 4) + c, 0:QC], lhs[b][:, at:at + rows],
                                              wt[2 if h == 3 else h % 2][:, c * QC:(c + 1) * QC], start=first and h in (0, 3),
                                              stop=last and h in (2, 3), skip_group_check=True)
                    mm.then_inc(weight_used, 1)
            ring(pe, W, 2, step)
            pe.wait_ge(sums_copied, 8)
            for j in range(n):
                g, r = j // 3, (j % 3) * H * HW
                nc.tensor.transpose(ps[:, g, r:r + 3 * HW], sums[0:3 * HW, j * P:(j + 1) * P], k.ident[0:3 * HW, 0:3 * HW])
                mm = nc.tensor.transpose(ps[:, g, r + 3 * HW:r + 4 * HW], sums3[0:HW, j * P:(j + 1) * P], k.ident[0:HW, 0:HW])
                if j % 3 == 2 or j == n - 1:
                    mm.then_inc(turned, 1)


def layer_norm(nc, k, tag, table=None, out=None):
    with ExitStack() as ctx:
        m = Core(nc, ctx, tag)
        sq = m.sb("sq", [P, NP])
        s = m.sb("s", [P, W])
        v = m.sb("v", [P, W])
        dve_step = m.sem("dve_step")
        var_ready = m.sem("var_ready")
        root_ready = m.sem("root_ready")
        norm_ready = m.sem("norm_ready")
        stored = m.sem("stored")
        block = ctx.enter_context(nc.Block())
        x = k.x[:, :].rearrange("p (w f) -> p w f", f=D)

        @block.vector
        def _(dve):
            c = Chain(dve, dve_step)
            c.link(nc.vector.tensor_reduce(s[:, :], x, AX.X, ALU.add))
            c.link(nc.vector.tensor_scalar(s[:, :], s[:, :], 1.0 / D, None, ALU.mult))
            c.link(nc.vector.tensor_tensor(x, x, bc(s[:, :, None], [P, W, D]), ALU.subtract))
            c.link(nc.vector.tensor_tensor(sq[:, :], k.x[:, :], k.x[:, :], ALU.mult))
            c.link(nc.vector.tensor_reduce(v[:, :], sq[:, :].rearrange("p (w f) -> p w f", f=D), AX.X, ALU.add))
            nc.vector.tensor_scalar(v[:, :], v[:, :], 1.0 / D, 1e-5, ALU.mult, ALU.add).then_inc(var_ready, 1)
            dve.wait_ge(root_ready, 1)
            c.link(nc.vector.reciprocal(v[:, :], v[:, :]))
            nc.vector.tensor_tensor(x, x, bc(v[:, :, None], [P, W, D]), ALU.mult).then_inc(norm_ready, 1)

        @block.scalar
        def _(act):
            act.wait_ge(var_ready, 1)
            nc.scalar.activation(v[:, :], v[:, :], ACT.Sqrt).then_inc(root_ready, 1)

        @block.sync
        def _(sp):
            sp.wait_ge(norm_ready, 1)
            if table is not None:
                sp.dma_start(table.rearrange("w p f -> p w f"), x).then_inc(stored, 16)
                sp.wait_ge(stored, 16)
            if out is not None:
                sp.dma_start(out[0:(W - 1) * P, :].rearrange("(w p) d -> p w d", p=P), x[:, 0:W - 1, :]).then_inc(stored, 16)
                sp.dma_start(out[(W - 1) * P:N, :], x[0:TAIL, W - 1, :]).then_inc(stored, 16)
                sp.wait_ge(stored, 32)


def aggregate(nc, table, counts, total, tag, add=None):
    B = 3
    with ExitStack() as ctx:
        m = Core(nc, ctx, tag)
        rows = [m.sb(f"rows{b}", [P, D]) for b in range(B)]
        cnt = [m.sb(f"cnt{b}", [P, NP]) for b in range(B)]
        ps = m.ps("ps", [P, NCH, 512])
        in_ = [m.sem(f"in{b}") for b in range(B)]
        summed = m.sem("summed")
        block = ctx.enter_context(nc.Block())

        @block.sync
        def _(sp):
            def load(t, b, kk):
                if used(kk):
                    sp.wait_ge(summed, (t - B + 1) * NCH)
                sp.dma_start(rows[b][:, :], table[bass.ds(t, 1), :, :].rearrange("s p f -> p (s f)")).then_inc(in_[b], 16)
                sp.dma_start(cnt[b][:, :], counts[bass.ds(t, 1), :, :].rearrange("s p f -> p (s f)")).then_inc(in_[b], 16)
            ring(sp, W, B, load)

        @block.tensor
        def _(pe):
            def step(t, b, kk):
                pe.wait_ge(in_[b], (kk + 1) * 32)
                first, last = isinstance(t, int) and t == 0, isinstance(t, int) and t == W - 1
                for c in range(NCH):
                    nc.tensor.matmul(ps[:, c, 0:CH], rows[b][:, :], cnt[b][:, c * CH:(c + 1) * CH], start=first,
                                     stop=last, skip_group_check=True).then_inc(summed, 1)
            ring(pe, W, B, step)

        @block.vector
        def _(dve):
            for c in range(NCH):
                dve.wait_ge(summed, (W - 1) * NCH + c + 1)
                at = slice(c * CH, (c + 1) * CH)
                if add is None:
                    nc.vector.tensor_copy(total[:, at], ps[:, c, 0:CH])
                else:
                    nc.vector.tensor_tensor(total[:, at], ps[:, c, 0:CH], add[:, at], ALU.add)


def mean_layer(nc, p, k, xT, aggT):
    G = -(-W // 4)
    with ExitStack() as ctx:
        m = Core(nc, ctx, "mean")
        wl = m.sb("wl", [D, D])
        wr = m.sb("wr", [D, D])
        bl = m.sb("bl", [P, D])
        br = m.sb("br", [P, D])
        rdeg = m.sb("rdeg", [P, W])
        y = m.sb("y", [P, NP])
        sq = m.sb("sq", [P, NP])
        s = m.sb("s", [P, W])
        ps = m.ps("ps", [P, 8, 512])
        params_in = m.sem("params_in")
        rdeg_ready = m.sem("rdeg_ready")
        multiplied = m.sem("multiplied")
        mean_ready = m.sem("mean_ready")
        group_ready = m.sem("group_ready")
        squares_ready = m.sem("squares_ready")
        root_ready = m.sem("root_ready")
        dve_step = m.sem("dve_step")
        block = ctx.enter_context(nc.Block())

        @block.sync
        def _(sp):
            sp.dma_start(wl[:, :], p['L1_gnn_Wl']).then_inc(params_in, 16)
            sp.dma_start(wr[:, :], p['L1_gnn_Wr']).then_inc(params_in, 16)
            sp.dma_start(bl[:, :], p['L1_gnn_bl'].partition_broadcast(P)).then_inc(params_in, 16)
            sp.dma_start(br[:, :], p['L1_gnn_br'].partition_broadcast(P)).then_inc(params_in, 16)

        @block.tensor
        def _(pe):
            pe.wait_ge(params_in, 64)
            for g in range(G):
                if g >= 4:
                    pe.wait_ge(group_ready, g - 3)
                for w in range(4 * g, min(4 * g + 4, W)):
                    at = slice((w % 4) * P, (w % 4 + 1) * P)
                    nc.tensor.matmul(ps[:, 2 * (g % 4), at], xT[:, w * P:(w + 1) * P], wl[:, :], start=True, stop=True)
                    mm = nc.tensor.matmul(ps[:, 2 * (g % 4) + 1, at], aggT[:, w * P:(w + 1) * P], wr[:, :], start=True, stop=True)
                mm.then_inc(multiplied, 1)

        @block.scalar
        def _(act):
            act.wait_ge(rdeg_ready, 1)
            for w in range(W):
                g = w // 4
                if w % 4 == 0:
                    act.wait_ge(multiplied, g + 1)
                nc.scalar.activation(y[:, w * P:(w + 1) * P], ps[:, 2 * (g % 4) + 1, (w % 4) * P:(w % 4 + 1) * P],
                                     ACT.Copy, scale=rdeg[:, w:w + 1]).then_inc(mean_ready, 1)
            act.wait_ge(squares_ready, 1)
            nc.scalar.activation(s[:, :], s[:, :], ACT.Sqrt).then_inc(root_ready, 1)

        @block.vector
        def _(dve):
            c = Chain(dve, dve_step)
            c.link(nc.vector.tensor_scalar(rdeg[:, :], k.degree[:, :], 1.0, None, ALU.max))
            nc.vector.reciprocal(rdeg[:, :], rdeg[:, :]).then_inc(rdeg_ready, 1)
            dve.wait_ge(params_in, 64)
            c.link(nc.vector.tensor_tensor(bl[:, :], bl[:, :], br[:, :], ALU.add))
            for g in range(G):
                n = min(4, W - 4 * g) * P
                dve.wait_ge(mean_ready, min(4 * g + 4, W))
                nc.vector.tensor_tensor(y[:, g * 512:g * 512 + n], y[:, g * 512:g * 512 + n], ps[:, 2 * (g % 4), 0:n],
                                        ALU.add).then_inc(group_ready, 1)
            dve.wait_ge(group_ready, G)
            y3 = y[:, :].rearrange("p (w f) -> p w f", f=D)
            c.link(nc.vector.tensor_tensor(y3, y3, bc(bl[:, None, :], [P, W, D]), ALU.add))
            c.link(nc.vector.tensor_scalar(y[:, :], y[:, :], 0.0, None, ALU.max))
            c.link(nc.vector.tensor_tensor(sq[:, :], y[:, :], y[:, :], ALU.mult))
            nc.vector.tensor_reduce(s[:, :], sq[:, :].rearrange("p (w f) -> p w f", f=D), AX.X, ALU.add).then_inc(squares_ready, 1)
            dve.wait_ge(root_ready, 1)
            c.link(nc.vector.tensor_scalar(s[:, :], s[:, :], 1e-6, None, ALU.add))
            c.link(nc.vector.reciprocal(s[:, :], s[:, :]))
            c.link(nc.vector.tensor_tensor(y3, y3, bc(s[:, :, None], [P, W, D]), ALU.mult))
            c.link(nc.vector.tensor_tensor(k.x[:, :], k.x[:, :], y[:, :], ALU.add))


def mlp(nc, p, k, layer, aggT, outT, nodes, table):
    G = -(-W // 4)
    with ExitStack() as ctx:
        m = Core(nc, ctx, f"mlp{layer}")
        w1 = m.sb("w1", [D, D])
        w2 = m.sb("w2", [D, D])
        b1 = m.sb("b1", [D, 1])
        b2 = m.sb("b2", [D, 1])
        hT = m.sb("hT", [P, NP])
        ps = m.ps("ps", [P, NCH, 512])
        params_in = m.sem("params_in")
        hidden_summed = m.sem("hidden_summed")
        hidden_ready = m.sem("hidden_ready")
        out_summed = m.sem("out_summed")
        out_ready = m.sem("out_ready")
        turned = m.sem("turned")
        nodes_ready = m.sem("nodes_ready")
        stored = m.sem("stored")
        block = ctx.enter_context(nc.Block())

        @block.sync
        def _(sp):
            sp.dma_start(w1[:, :], p['L2_gnn_W1'][layer, :, :]).then_inc(params_in, 16)
            sp.dma_start(w2[:, :], p['L2_gnn_W2'][layer, :, :]).then_inc(params_in, 16)
            sp.dma_start(b1[:, :], p['L2_gnn_b1'][layer, :].rearrange("(d a) -> d a", a=1)).then_inc(params_in, 16)
            sp.dma_start(b2[:, :], p['L2_gnn_b2'][layer, :].rearrange("(d a) -> d a", a=1)).then_inc(params_in, 16)
            if table is not None:
                sp.wait_ge(nodes_ready, G)
                sp.dma_start(table.rearrange("w p f -> p w f"), nodes[:, :].rearrange("p (w f) -> p w f", f=D)).then_inc(stored, 16)
                sp.wait_ge(stored, 16)

        @block.tensor
        def _(pe):
            pe.wait_ge(params_in, 64)
            for c in range(NCH):
                nc.tensor.matmul(ps[:, c, 0:CH], w1[:, :], aggT[:, c * CH:(c + 1) * CH], start=True, stop=True).then_inc(hidden_summed, 1)
            for c in range(NCH):
                pe.wait_ge(hidden_ready, c + 1)
                nc.tensor.matmul(ps[:, c, 0:CH], w2[:, :], hT[:, c * CH:(c + 1) * CH], start=True, stop=True).then_inc(out_summed, 1)
            pe.wait_ge(out_ready, NCH)
            for w in range(W):
                mm = nc.tensor.transpose(ps[:, w // 4, (w % 4) * P:(w % 4 + 1) * P], outT[:, w * P:(w + 1) * P], k.ident[:, :])
                if w % 4 == 3 or w == W - 1:
                    mm.then_inc(turned, 1)

        @block.scalar
        def _(act):
            act.wait_ge(params_in, 64)
            for c in range(NCH):
                act.wait_ge(hidden_summed, c + 1)
                nc.scalar.activation(hT[:, c * CH:(c + 1) * CH], ps[:, c, 0:CH], ACT.Relu, bias=b1[:, :]).then_inc(hidden_ready, 1)
            for c in range(NCH):
                act.wait_ge(out_summed, c + 1)
                nc.scalar.activation(outT[:, c * CH:(c + 1) * CH], ps[:, c, 0:CH], ACT.Relu, bias=b2[:, :]).then_inc(out_ready, 1)
            for g in range(G):
                n = min(4, W - 4 * g) * P
                act.wait_ge(turned, g + 1)
                nc.scalar.copy(nodes[:, g * 512:g * 512 + n], ps[:, g, 0:n]).then_inc(nodes_ready, 1)


def add_to_x(nc, k, y, tag, scale=1.0):
    with nc.Block() as block:
        @block.vector
        def _(dve):
            nc.vector.scalar_tensor_tensor(k.x[:, :], k.x[:, :], scale, y[:, :], ALU.mult, ALU.add)


def hop_left(nc, k, d, qw, aggT):
    with ExitStack() as ctx:
        m = Core(nc, ctx, "left")
        leftT = m.sb("leftT", [P, NP])
        ps = m.ps("ps", [P, NCH, 512])
        summed = m.sem("summed")
        ready = m.sem("ready")
        stored = m.sem("stored")
        block = ctx.enter_context(nc.Block())

        @block.tensor
        def _(pe):
            for c in range(NCH):
                nc.tensor.matmul(ps[:, c, 0:CH], qw[:, :], aggT[:, c * CH:(c + 1) * CH], start=True, stop=True).then_inc(summed, 1)

        @block.scalar
        def _(act):
            for c in range(NCH):
                act.wait_ge(summed, c + 1)
                nc.scalar.copy(leftT[:, c * CH:(c + 1) * CH], ps[:, c, 0:CH]).then_inc(ready, 1)

        @block.sync
        def _(sp):
            sp.wait_ge(ready, NCH)
            sp.dma_start(d.left[0:W, :, :].rearrange("w f n -> f w n"), leftT[:, :].rearrange("f (w n) -> f w n", n=P)).then_inc(stored, 16)
            sp.dma_start(d.left[W, :, :], k.zeros[:, :]).then_inc(stored, 16)
            sp.wait_ge(stored, 32)


def relation_parts(nc, p, k, rel_hi_mid, rel_lo):
    with ExitStack() as ctx:
        m = Core(nc, ctx, "rel")
        t = m.sb("t", [P, D])
        hi = m.sb("hi", [P, D], BF16)
        r1 = m.sb("r1", [P, D])
        mid = m.sb("mid", [P, D], BF16)
        rel_in = m.sem("rel_in")
        dve_step = m.sem("dve_step")
        block = ctx.enter_context(nc.Block())

        @block.sync
        def _(sp):
            sp.dma_start(t[0:REL, :], p['L3_gnn_edge_emb']).then_inc(rel_in, 16)
            sp.dma_start(t[REL:P, :], p['L3_gnn_edge_emb']).then_inc(rel_in, 16)

        @block.vector
        def _(dve):
            c = Chain(dve, dve_step)
            dve.wait_ge(rel_in, 32)
            c.link(nc.vector.tensor_copy(hi[:, :], t[:, :]))
            c.link(nc.vector.tensor_tensor(r1[:, :], t[:, :], hi[:, :], ALU.subtract))
            c.link(nc.vector.tensor_copy(mid[:, :], r1[:, :]))
            c.link(nc.vector.tensor_copy(rel_hi_mid[0:REL, :], hi[0:REL, :]))
            c.link(nc.vector.tensor_copy(rel_hi_mid[REL:P, :], mid[REL:P, :]))
            c.link(nc.vector.tensor_tensor(r1[:, :], r1[:, :], mid[:, :], ALU.subtract))
            c.link(nc.vector.tensor_copy(rel_lo[:, :], r1[0:REL, :]))


def relation_masks(nc, d, k):
    B = 6
    with ExitStack() as ctx:
        m = Core(nc, ctx, "kinds")
        rec = [m.sb(f"rec{b}", [P, J, 4]) for b in range(B)]
        typ = m.sb("typ", [P, P], BF16)
        hot = [m.sb(f"hot{b}", [P, J, P], BF16) for b in range(B)]
        hotT = [m.sb(f"hotT{b}", [P, S], BF16) for b in range(B)]
        ps = m.ps("ps", [P, B, S])
        typ_ready = m.sem("typ_ready")
        rec_in = [m.sem(f"rec_in{b}") for b in range(B)]
        hot_ready = m.sem("hot_ready")
        turned = m.sem("turned")
        copied = m.sem("copied")
        stored = [m.sem(f"stored{b}") for b in range(B)]
        block = ctx.enter_context(nc.Block())
        slots = d.slots.rearrange("(s p j) f -> s p (j f)", p=P, j=J)

        @block.sync
        def _(sp):
            def load(s):
                since(sp, hot_ready, s, B, J)
                sp.dma_start(rec[s.slot(B)][:, :, :].rearrange("p j f -> p (j f)").bitcast(I32),
                             slots[bass.ds(s.t, 1), :, :].rearrange("s p f -> p (s f)")).then_inc(rec_in[s.slot(B)], 16)

            def store(s):
                sp.wait_ge(copied, s.t + 1)
                sp.dma_start(d.type_hots[bass.ds(s.t, 1), :, :].rearrange("s p f -> p (s f)"), hotT[s.slot(B)][:, :]).then_inc(stored[s.slot(B)], 16)

            def step(s):
                if s.exists(NST):
                    load(s)
                if s.lag(5).exists(NST):
                    store(s.lag(5))
            pipeline(sp, NST, 5, B, step)
            for b in range(B):
                sp.wait_ge(stored[b], 16 * ((NST + B - 1 - b) // B))

        @block.vector
        def _(dve):
            nc.vector.tensor_copy(typ[:, 0:REL], k.node[:, 0:REL]).then_inc(typ_ready, 1)
            nc.vector.tensor_copy(typ[:, REL:P], k.node[:, 0:REL]).then_inc(typ_ready, 1)
            dve.wait_ge(typ_ready, 2)

            def step(s):
                b = s.slot(B)
                dve.wait_ge(rec_in[b], (s.uses(B) + 1) * 16)
                since(dve, turned, s, B)
                for j in range(J):
                    nc.vector.tensor_scalar(hot[b][:, j, :], typ[:, :], rec[b][:, j, 2:3], None, ALU.is_equal).then_inc(hot_ready, 1)
            pipeline(dve, NST, 0, B, step)

        @block.tensor
        def _(pe):
            def step(s):
                b = s.slot(B)
                pe.wait_ge(hot_ready, (s.t + 1) * J)
                since(pe, copied, s, B)
                for j in range(J):
                    mm = nc.tensor.matmul(ps[:, b, j * P:(j + 1) * P], hot[b][:, j, :], k.identb[:, :], start=True, stop=True)
                mm.then_inc(turned, 1)
            pipeline(pe, NST, 0, B, step)

        @block.scalar
        def _(act):
            def step(s):
                b = s.slot(B)
                act.wait_ge(turned, s.t + 1)
                if s.at_least(B):
                    act.wait_ge(stored[b], s.uses(B) * 16)
                nc.scalar.copy(hotT[b][:, :], ps[:, b, :]).then_inc(copied, 1)
            pipeline(act, NST, 0, B, step)


def hop_edges(nc, d, k, kw, rel_hi_mid, rel_lo, table, result):
    MW = D + 1
    B = 6
    LAG = 4
    with ExitStack() as ctx:
        m = Core(nc, ctx, "hop")
        rec = [m.sb(f"rec{b}", [P, J, 4]) for b in range(6)]
        hotT = [m.sb(f"hotT{b}", [P, S], BF16) for b in range(6)]
        left = [m.sb(f"left{b}", [P, P]) for b in range(6)]
        tail_rows = [m.sb(f"tail_rows{b}", [P, J, D]) for b in range(3)]
        other = [m.sb(f"other{b}", [P, J, P], BF16) for b in range(3)]
        rt = [m.sb(f"rt{b}", [P, J, MW]) for b in range(6)]
        rtT = [m.sb(f"rtT{b}", [P, S]) for b in range(2)]
        right = [m.sb(f"right{b}", [P, S]) for b in range(2)]
        ex = [m.sb(f"ex{b}", [P, S]) for b in range(2)]
        exT = [m.sb(f"exT{b}", [P, S]) for b in range(2)]
        tile_max = [m.sb(f"tile_max{b}", [P, 1]) for b in range(2)]
        old_max = [m.sb(f"old_max{b}", [P, 1]) for b in range(2)]
        new_max = [m.sb(f"new_max{b}", [P, 1]) for b in range(2)]
        neg_max = [m.sb(f"neg_max{b}", [P, 1]) for b in range(2)]
        scale = [m.sb(f"scale{b}", [P, 1]) for b in range(3)]
        state = [m.sb(f"state{b}", [P, MW]) for b in range(3)]
        ps_rel = m.ps("ps_rel", [P, S])
        ps_rtT = m.ps("ps_rtT", [P, S])
        ps_right = m.ps("ps_right", [P, S])
        ps_logit = [m.ps(f"ps_logit{b}", [P, S]) for b in range(2)]
        ps_exT = m.ps("ps_exT", [P, S])
        ps_sum = [m.ps(f"ps_sum{b}", [P, S]) for b in range(2)]
        loads_in = [m.sem(f"loads_in{b}") for b in range(6)]
        rows_in = [m.sem(f"rows_in{b}", pool_dma=True) for b in range(3)]
        state_out = [m.sem(f"state_out{b}") for b in range(3)]
        issue = m.sem("issue")
        constants_set = m.sem("constants_set")
        other_ready = m.sem("other_ready")
        rel_ready = m.sem("rel_ready")
        rt_ready = m.sem("rt_ready")
        rt_turned = m.sem("rt_turned")
        rtT_ready = m.sem("rtT_ready")
        right_summed = m.sem("right_summed")
        right_ready = m.sem("right_ready")
        logits_ready = m.sem("logits_ready")
        tile_max_ready = m.sem("tile_max_ready")
        old_max_ready = m.sem("old_max_ready")
        new_max_ready = m.sem("new_max_ready")
        neg_max_ready = m.sem("neg_max_ready")
        ex_ready = m.sem("ex_ready")
        scale_ready = m.sem("scale_ready")
        ex_turned = m.sem("ex_turned")
        exT_ready = m.sem("exT_ready")
        messages_summed = m.sem("messages_summed")
        state_ready = m.sem("state_ready")
        block = ctx.enter_context(nc.Block())
        slots = d.slots.rearrange("(s p j) f -> s p (j f)", p=P, j=J)
        table_rows = table.rearrange("w p f -> (w p) f")

        @block.sync
        def _(sp):
            def load(s):
                b = s.slot(6)
                since(sp, other_ready, s, 6)
                since(sp, rt_ready, s, 6)
                sp.dma_start(rec[b][:, :, :].rearrange("p j f -> p (j f)").bitcast(I32),
                             slots[bass.ds(s.t, 1), :, :].rearrange("s p f -> p (s f)")).then_inc(loads_in[b], 16)
                since(sp, rel_ready, s, 6)
                sp.dma_start(hotT[b][:, :], d.type_hots[bass.ds(s.t, 1), :, :].rearrange("s p f -> p (s f)")).then_inc(loads_in[b], 16)
                since(sp, logits_ready, s, 6)
                w = sp.value_load(k.window_of[0:1, bass.ds(s.t, 1)], min_val=0, max_val=W)
                sp.dma_start(left[b][:, :], d.left[bass.ds(w, 1), :, :].rearrange("s p f -> p (s f)")).then_inc(loads_in[b], 16)

            def store(s):
                w = sp.value_load(k.window_of[0:1, bass.ds(s.t, 1)], min_val=0, max_val=W)
                last = sp.value_load(k.last_of[0:1, bass.ds(s.t, 1)], min_val=0, max_val=1)
                sp.wait_ge(state_ready, s.t + 1)
                sp.dma_start(d.state[bass.ds(w, 1), :, :].rearrange("s p f -> p (s f)"), state[s.slot(3)][:, :],
                             cond=last).then_inc(state_out[s.slot(3)], 16)

            def step(s):
                if s.exists(NST):
                    load(s)
                if s.lag(6).exists(NST):
                    store(s.lag(6))
            pipeline(sp, NST, 6, B, step)
            for b in range(3):
                sp.wait_ge(state_out[b], 16 * ((NST + 2 - b) // 3))

        @block.gpsimd
        def _(pool):
            def step(s):
                b = s.slot(3)
                since(pool, rt_ready, s, 3)
                pool.sem_inc(issue, 1)
                pool.wait_ge(loads_in[s.slot(6)], (s.uses(6) + 1) * 48)
                pool.sem_inc(issue, 1)
                for j in range(J):
                    pool.indirect_dma_start(tail_rows[b][:, j, :], None, table_rows,
                                            bass.IndirectOffsetOnAxis(ap=rec[s.slot(6)][:, j, 3:4].bitcast(I32), axis=0)).then_inc(rows_in[b], 16)
            pipeline(pool, NST, 0, B, step)

        @block.tensor
        def _(pe):
            def turn_products(s):
                pe.wait_ge(rt_ready, s.t + 1)
                since(pe, rtT_ready, s, 1)
                for j in range(J):
                    mm = nc.tensor.transpose(ps_rtT[:, j * P:(j + 1) * P], rt[s.slot(6)][:, j, 0:D], k.ident[:, :])
                mm.then_inc(rt_turned, 1)

            def turn_weights(s):
                pe.wait_ge(ex_ready, s.t + 1)
                since(pe, exT_ready, s, 1)
                for j in range(J):
                    mm = nc.tensor.transpose(ps_exT[:, j * P:(j + 1) * P], ex[s.slot(2)][:, j * P:(j + 1) * P], k.ident[:, :])
                mm.then_inc(ex_turned, 1)

            def relations(s):
                pe.wait_ge(loads_in[s.slot(6)], (s.uses(6) + 1) * 48)
                since(pe, rt_ready, s, 1)
                hot = hotT[s.slot(6)]
                for j in range(J):
                    at = slice(j * P, (j + 1) * P)
                    nc.tensor.matmul(ps_rel[:, at], hot[:, at], rel_hi_mid[:, :], start=True, stop=False)
                    mm = nc.tensor.matmul(ps_rel[:, at], hot[0:REL, at], rel_lo[:, :], start=False, stop=True)
                mm.then_inc(rel_ready, 1)

            def rights(s):
                pe.wait_ge(rtT_ready, s.t + 1)
                since(pe, right_ready, s, 1)
                nc.tensor.matmul(ps_right[:, :], kw[:, :], rtT[s.slot(2)][:, :], start=True, stop=True).then_inc(right_summed, 1)

            def messages(s):
                pe.wait_ge(exT_ready, s.t + 1)
                since(pe, state_ready, s, 2)
                for j in range(J):
                    mm = nc.tensor.matmul(ps_sum[s.slot(2)][:, 0:MW], exT[s.slot(2)][:, j * P:(j + 1) * P],
                                          rt[s.slot(6)][:, j, :], start=(j == 0), stop=(j == J - 1))
                mm.then_inc(messages_summed, 1)

            def logits(s):
                pe.wait_ge(right_ready, s.t + 1)
                since(pe, ex_ready, s, 2)
                ps = ps_logit[s.slot(2)]
                nc.tensor.matmul(ps[:, :], left[s.slot(6)][:, :], right[s.slot(2)][:, :], start=True, stop=False,
                                 skip_group_check=True)
                pe.wait_ge(other_ready, s.t + 1)
                for j in range(J):
                    mm = nc.tensor.matmul(ps[:, j * P:(j + 1) * P], other[s.slot(3)][:, j, :], k.ident_neg[:, :], start=False,
                                          stop=(j == J - 1), skip_group_check=True)
                mm.then_inc(logits_ready, 1)

            def step(s):
                if s.lag(1).exists(NST):
                    turn_products(s.lag(1))
                if s.lag(4).exists(NST):
                    turn_weights(s.lag(4))
                if s.exists(NST):
                    relations(s)
                if s.lag(1).exists(NST):
                    rights(s.lag(1))
                if s.lag(4).exists(NST):
                    messages(s.lag(4))
                if s.lag(2).exists(NST):
                    logits(s.lag(2))
            pipeline(pe, NST, LAG, B, step)

        @block.scalar
        def _(act):
            def products(s):
                act.wait_ge(rt_turned, s.t + 1)
                since(act, right_summed, s, 2)
                nc.scalar.copy(rtT[s.slot(2)][:, :], ps_rtT[:, :]).then_inc(rtT_ready, 1)

            def weights(s):
                act.wait_ge(ex_turned, s.t + 1)
                since(act, messages_summed, s, 2)
                nc.scalar.copy(exT[s.slot(2)][:, :], ps_exT[:, :]).then_inc(exT_ready, 1)

            def exponentials(s):
                act.wait_ge(neg_max_ready, s.t + 1)
                since(act, ex_turned, s, 2)
                nc.scalar.activation(ex[s.slot(2)][:, :], ps_logit[s.slot(2)][:, :], ACT.Exp,
                                     bias=neg_max[s.slot(2)][:, :]).then_inc(ex_ready, 1)
                act.wait_ge(old_max_ready, s.t + 1)
                since(act, state_ready, s, 3)
                nc.scalar.activation(scale[s.slot(3)][:, :], old_max[s.slot(2)][:, :], ACT.Exp,
                                     bias=neg_max[s.slot(2)][:, :]).then_inc(scale_ready, 1)

            def tanh(s):
                act.wait_ge(right_summed, s.t + 1)
                since(act, logits_ready, s, 2)
                nc.scalar.activation(right[s.slot(2)][:, :], ps_right[:, :], ACT.Tanh).then_inc(right_ready, 1)

            def step(s):
                if s.lag(1).exists(NST):
                    products(s.lag(1))
                if s.lag(4).exists(NST):
                    weights(s.lag(4))
                if s.lag(3).exists(NST):
                    exponentials(s.lag(3))
                if s.lag(1).exists(NST):
                    tanh(s.lag(1))
            pipeline(act, NST, LAG, B, step)

        @block.vector
        def _(dve):
            for b in range(6):
                nc.vector.memset(rt[b][:, :, D:MW], 1.0).then_inc(constants_set, 1)
            nc.vector.memset(state[2][:, :], 0.0).then_inc(constants_set, 1)
            nc.vector.memset(new_max[1][:, :], -BIG).then_inc(constants_set, 1)
            dve.wait_ge(constants_set, 8)

            def maxima(s):
                b = s.slot(2)
                dve.wait_ge(logits_ready, s.t + 1)
                nc.vector.tensor_reduce(tile_max[b][:, :], ps_logit[b][:, :], AX.X, ALU.max).then_inc(tile_max_ready, 1)
                since(dve, scale_ready, s, 2)
                since(dve, new_max_ready, s, 1)
                cap = k.cap[:, bass.ds(s.t, 1)]
                nc.vector.tensor_tensor(old_max[b][:, :], new_max[1 - b][:, :], cap, ALU.min).then_inc(old_max_ready, 1)
                dve.wait_ge(tile_max_ready, s.t + 1)
                nc.vector.scalar_tensor_tensor(new_max[b][:, :], new_max[1 - b][:, :], cap, tile_max[b][:, :], ALU.min,
                                               ALU.max).then_inc(new_max_ready, 1)
                dve.wait_ge(new_max_ready, s.t + 1)
                nc.vector.tensor_scalar(neg_max[b][:, :], new_max[b][:, :], -1.0, BIG / 2, ALU.mult, ALU.min).then_inc(neg_max_ready, 1)

            def products(s):
                dve.wait_ge(rows_in[s.slot(3)], (s.uses(3) + 1) * 16 * J)
                dve.wait_ge(rel_ready, s.t + 1)
                since(dve, messages_summed, s, 6)
                nc.vector.tensor_tensor(rt[s.slot(6)][:, :, 0:D], tail_rows[s.slot(3)][:, :, :],
                                        ps_rel[:, :].rearrange("p (j f) -> p j f", f=D), ALU.mult).then_inc(rt_ready, 1)

            def states(s):
                b = s.slot(3)
                dve.wait_ge(messages_summed, s.t + 1)
                dve.wait_ge(scale_ready, s.t + 1)
                since(dve, state_ready, s, 1)
                if s.at_least(3):
                    dve.wait_ge(state_out[b], s.uses(3) * 16)
                nc.vector.scalar_tensor_tensor(state[b][:, :], state[(b - 1) % 3][:, :], scale[b][:, :], ps_sum[s.slot(2)][:, 0:MW],
                                               ALU.mult, ALU.add).then_inc(state_ready, 1)

            def masks(s):
                dve.wait_ge(loads_in[s.slot(6)], (s.uses(6) + 1) * 48)
                since(dve, logits_ready, s, 3)
                nc.vector.tensor_tensor(other[s.slot(3)][:, :, :], bc(k.node[:, None, :], [P, J, P]),
                                        bc(rec[s.slot(6)][:, :, 0:1], [P, J, P]), ALU.not_equal).then_inc(other_ready, 1)

            def step(s):
                if s.lag(3).exists(NST):
                    maxima(s.lag(3))
                if s.exists(NST):
                    products(s)
                    masks(s)
                if s.lag(4).exists(NST):
                    states(s.lag(4))
            pipeline(dve, NST, LAG, B, step)

    with ExitStack() as ctx:
        m = Core(nc, ctx, "hop_end")
        st = m.sb("st", [P, W, MW])
        r = m.sb("r", [P, W])
        cn = m.sb("cn", [P, W])
        sq = m.sb("sq", [P, NP])
        st_in = m.sem("st_in")
        dve_step = m.sem("dve_step")
        squares_ready = m.sem("squares_ready")
        root_ready = m.sem("root_ready")
        unit_ready = m.sem("unit_ready")
        stored = m.sem("stored")
        block = ctx.enter_context(nc.Block())
        y3 = result[:, :].rearrange("p (w f) -> p w f", f=D)

        @block.sync
        def _(sp):
            sp.dma_start(st[:, :, :], d.state[0:W, :, :].rearrange("w p f -> p w f")).then_inc(st_in, 16)
            sp.wait_ge(unit_ready, 1)
            sp.dma_start(table.rearrange("w p f -> p w f"), y3).then_inc(stored, 16)
            sp.wait_ge(stored, 16)

        @block.scalar
        def _(act):
            act.wait_ge(squares_ready, 1)
            nc.scalar.activation(r[:, :], r[:, :], ACT.Sqrt).then_inc(root_ready, 1)

        @block.vector
        def _(dve):
            c = Chain(dve, dve_step)
            dve.wait_ge(st_in, 16)
            c.link(nc.vector.tensor_scalar(r[:, :], st[:, :, D], 1e-30, None, ALU.max))
            c.link(nc.vector.tensor_scalar(cn[:, :], k.degree[:, :], 1.0, None, ALU.max))
            c.link(nc.vector.tensor_tensor(r[:, :], r[:, :], cn[:, :], ALU.mult))
            c.link(nc.vector.reciprocal(r[:, :], r[:, :]))
            c.link(nc.vector.tensor_tensor(y3, st[:, :, 0:D], bc(r[:, :, None], [P, W, D]), ALU.mult))
            c.link(nc.vector.tensor_tensor(sq[:, :], result[:, :], result[:, :], ALU.mult))
            nc.vector.tensor_reduce(r[:, :], sq[:, :].rearrange("p (w f) -> p w f", f=D), AX.X, ALU.add).then_inc(squares_ready, 1)
            dve.wait_ge(root_ready, 1)
            c.link(nc.vector.tensor_scalar(r[:, :], r[:, :], 1e-12, None, ALU.max))
            c.link(nc.vector.reciprocal(r[:, :], r[:, :]))
            nc.vector.tensor_tensor(y3, y3, bc(r[:, :, None], [P, W, D]), ALU.mult).then_inc(unit_ready, 1)


class Space:
    pass


def build(nc, p, out, debug=None):
    Core.ended = []
    with ExitStack() as ctx:
        m = Core(nc, ctx, "all")
        k, d = Space(), Space()
        k.ident = m.sb("ident", [P, P])
        k.identb = m.sb("identb", [P, P], BF16)
        k.ident_neg = m.sb("ident_neg", [P, P], BF16)
        k.tri = m.sb("tri", [P, P])
        k.node = m.sb("node", [P, P], BF16)
        k.steps = m.sb("steps", [P, NST + 1])
        k.part = m.sb("part", [P, 1])
        k.ones = m.sb("ones", [P, P])
        k.zeros = m.sb("zeros", [P, P])
        k.zerosb = m.sb("zerosb", [P, CH], BF16)
        k.window_of = m.sb("window_of", [P, NST], I32)
        k.last_of = m.sb("last_of", [P, NST], I32)
        k.cap = m.sb("cap", [P, NST])
        k.degree = m.sb("degree", [P, W])
        k.issue = m.sem("issue")
        d.slots = nc.dram_tensor("slots", (NST * S, 4), I32).ap()
        d.cum = nc.dram_tensor("cum", (W + 1, P, NP), F32).ap()
        d.cnt = nc.dram_tensor("cnt", (W, P, NP), F32).ap()
        d.cntT = nc.dram_tensor("cntT", (W, P, NP), F32).ap()
        zeros_set = m.sem("zeros_set")
        with nc.Block() as block:
            @block.vector
            def _(dve):
                nc.vector.memset(k.zeros[:, :], 0.0).then_inc(zeros_set, 1)
                nc.vector.memset(k.zerosb[:, :], 0.0).then_inc(zeros_set, 1)
        build_constants(nc, k)
        sort_edges(nc, p, d, k)
        count_pairs(nc, d, k)
        split_counts(nc, d, k)
        k.x = m.sb("x", [P, NP])
        k.LHS = 10 * (C + 1) + 2 * H
        k.col_s = m.sb("col_s", [P, W * H])
        k.col_d = m.sb("col_d", [P, W * H])
        k.amax = m.sb("amax", [P, W * H])
        d.lhs = nc.dram_tensor("lhs", (W, P, k.LHS), F32).ap()
        d.nodes = nc.dram_tensor("nodes", (W, P, D), F32).ap()
        d.left = nc.dram_tensor("left", (W + 1, P, P), F32).ap()
        d.type_hots = nc.dram_tensor("types", (NST, P, S), BF16).ap()
        d.state = nc.dram_tensor("state", (W + 1, P, D + 1), F32).ap()
        load_inputs(nc, p, k)
        with ExitStack() as inner:
            mm = Core(nc, inner, "att")
            row_d = mm.sb("row_d", [P, H, NP])
            with ExitStack() as deep:
                mm = Core(nc, deep, "att")
                row_s = mm.sb("row_s", [P, H, NP])
                with ExitStack() as deeper:
                    xT = Core(nc, deeper, "att").sb("xT", [P, NP])
                    turn(nc, k, k.x, xT, "turn_x")
                    attention_project(nc, p, d, k, xT, row_s, row_d)
                attention_max(nc, d, k, row_s)
            with ExitStack() as deep:
                mm = Core(nc, deep, "att")
                pos_row = mm.sb("pos_row", [P, H, 13 * P])
                neg_row = mm.sb("neg_row", [P, H, 13 * P])
                for w0, n in ((0, 13), (13, 12)):
                    pr, nr = pos_row[:, :, 0:n * P], neg_row[:, :, 0:n * P]
                    attention_rows(nc, k, row_d, pr, nr, w0, n)
                    attention_sum(nc, d, k, pr, nr, w0, n)
        layer_norm(nc, k, "norm0", table=d.nodes)
        with ExitStack() as inner:
            mm = Core(nc, inner, "graph")
            xT = mm.sb("xT", [P, NP])
            aggT = mm.sb("aggT", [P, NP])
            y = mm.sb("y", [P, NP])
            turn(nc, k, k.x, xT, "turn_1")
            aggregate(nc, d.nodes, d.cntT, aggT, "agg1")
            mean_layer(nc, p, k, xT, aggT)
            layer_norm(nc, k, "norm1", table=d.nodes)
            turn(nc, k, k.x, xT, "turn_2")
            for layer in range(3):
                aggregate(nc, d.nodes, d.cnt, aggT, f"agg2{layer}", add=xT)
                mlp(nc, p, k, layer, aggT, xT, y, d.nodes if layer < 2 else None)
            add_to_x(nc, k, y, "add2")
            layer_norm(nc, k, "norm2", table=d.nodes)
            rel_hi_mid = mm.sb("rel_hi_mid", [P, D], BF16)
            rel_lo = mm.sb("rel_lo", [REL, D], BF16)
            qw = mm.sb("qw", [D, D])
            kw = mm.sb("kw", [D, D])
            relation_parts(nc, p, k, rel_hi_mid, rel_lo)
            relation_masks(nc, d, k)
            hop_in = mm.sem("hop_in")
            with nc.Block() as block:
                @block.sync
                def _(sp):
                    sp.dma_start(qw[:, :], p['L3_gnn_q_w']).then_inc(hop_in, 16)
                    sp.dma_start(kw[:, :], p['L3_gnn_k_w']).then_inc(hop_in, 16)
                    sp.wait_ge(hop_in, 32)
            turn(nc, k, k.x, xT, "turn_3")
            for hop in range(3):
                hop_left(nc, k, d, qw, xT)
                hop_edges(nc, d, k, kw, rel_hi_mid, rel_lo, d.nodes, y)
                if hop < 2:
                    turn(nc, k, y, xT, f"turn_4{hop}")
                add_to_x(nc, k, y, "add3", scale=4.0 if hop == 0 else 1.0)
        layer_norm(nc, k, "norm3", out=out)


INPUTS = ['x', 'src', 'dst', 'edge_type_64', 'L0_gnn_coeffs_t', 'L0_gnn_lin_weight', 'L0_gnn_lin_bias',
          'L0_gnn_att_src', 'L0_gnn_att_dst', 'L1_gnn_Wl', 'L1_gnn_bl', 'L1_gnn_Wr', 'L1_gnn_br', 'L2_gnn_W1',
          'L2_gnn_b1', 'L2_gnn_W2', 'L2_gnn_b2', 'L3_gnn_edge_emb', 'L3_gnn_q_w', 'L3_gnn_k_w']
DEBUG = {}


def kernel(**inputs):
    import numpy as np
    import concourse.bacc as bacc
    from concourse.bass_utils import run_bass_kernel_spmd as run

    nc = bacc.Bacc("TRN2", target_bir_lowering=False, num_devices=1)
    arrays, p = {}, {}
    for name in INPUTS:
        a = np.ascontiguousarray(inputs[name])
        arrays[f"in_{name}"] = a
        p[name] = nc.dram_tensor(f"in_{name}", a.shape, mybir.dt.from_np(a.dtype), kind="ExternalInput").ap()
    out = nc.dram_tensor("out_0", (N, D), F32, kind="ExternalOutput").ap()
    debug = {n: nc.dram_tensor(f"dbg_{n}", s, F32, kind="ExternalOutput").ap() for n, s in DEBUG.items()} or None
    build(nc, p, out, debug)
    r = run(nc, [arrays], core_ids=[0])
    return r.results[0]["out_0"]
```

```python
import concourse.bass as bass
from concourse import mybir
from contextlib import ExitStack, contextmanager

F32 = mybir.dt.float32
BF16 = mybir.dt.bfloat16
F16 = mybir.dt.float16
I32 = mybir.dt.int32
ALU = mybir.AluOpType
ACT = mybir.ActivationFunctionType
AX = mybir.AxisListType

P = 128
N, D, E = 3125, 128, 103125
W = -(-N // P)
NP = W * P
TAIL = N - (W - 1) * P
EP = 125
EC = E // EP
S = 512
J = S // P
NST = (E + W + W * (S - 1)) // S
CH = 400
NCH = NP // CH
CCH = -(-N // NCH)
NC = NCH * CCH
MID = 1600
SHIFT = 9
H, C = 4, 32
BIG = 2.0 ** 100
REL = 64
KINDS, K = 2, 3
SCAT_BUFS, SCAT_COLS = 3, 11


class Chain:

    def __init__(self, eng, sem):
        self.eng, self.sem, self.base, self.n = eng, sem, 0, 0

    def add(self, ins):
        ins.then_inc(self.sem, 1)
        self.n += 1

    def link(self, ins):
        self.add(ins)
        self.eng.wait_ge(self.sem, self.base + self.n)

    @contextmanager
    def loop(self, start, end, links):
        before = self.base + self.n
        with self.eng.Fori(start, end) as i:
            self.base, self.n = i * links + (before - start * links), 0
            yield i
            assert self.n == links, self.n
        self.base, self.n = 0, before + (end - start) * links


def ring(eng, count, bufs, body, chain=None, links=0):
    for t in range(bufs):
        body(t, t, 0)
    full = count // bufs
    if full > 1:
        if chain:
            with chain.loop(1, full, links) as k:
                for b in range(bufs):
                    body(k * bufs + b, b, k)
        else:
            with eng.Fori(1, full) as k:
                for b in range(bufs):
                    body(k * bufs + b, b, k)
    for b in range(count - full * bufs):
        body(full * bufs + b, b, full)


def used(k):
    return not (isinstance(k, int) and k == 0)


class Core:
    stages = 0
    ended = []
    FEW = 45

    def __init__(self, nc, ctx, tag):
        Core.stages += 1
        self.nc, self.ctx, self.tag = nc, ctx, f"{tag}{Core.stages}"
        self.mine = []
        if len(nc.free_semaphores) < self.FEW:
            self.clear()
        ctx.callback(lambda: Core.ended.extend(self.mine))

    def sb(self, name, shape, dt=F32):
        return self.ctx.enter_context(self.nc.sbuf_tensor(f"{self.tag}_{name}", shape, dt))

    def ps(self, name, shape, dt=F32):
        return self.ctx.enter_context(self.nc.psum_tensor(f"{self.tag}_{name}", shape, dt))

    def sem(self, name, pool_dma=False):
        s = self.nc.alloc_semaphore(f"{self.tag}_{name}")
        if not pool_dma:
            self.mine.append(s)
        return s

    def clear(self):
        with self.nc.Block() as block:
            @block.sync
            def _(sp):
                for s in Core.ended:
                    sp.sem_clear(s)
        for s in Core.ended:
            self.nc.release_semaphore(s)
        Core.ended = []


class Step:

    def __init__(self, k, r, bufs):
        self.k, self.r, self.bufs = k, r, bufs
        self.t = k * bufs + r

    def lag(self, n):
        return Step(self.k, self.r - n, self.bufs)

    def slot(self, m):
        return self.r % m

    def uses(self, m):
        return self.k * (self.bufs // m) + self.r // m

    def exists(self, count):
        return not isinstance(self.k, int) or 0 <= self.t < count

    def at_least(self, n):
        return not isinstance(self.k, int) or self.t >= n


def pipeline(eng, count, lag, bufs, body, chain=None, links=0):
    full = count // bufs
    for i in range(2 * bufs):
        body(Step(i // bufs, i % bufs, bufs))
    with (chain.loop(2, full, links) if chain else eng.Fori(2, full)) as k:
        for r in range(bufs):
            body(Step(k, r, bufs))
    for i in range(full * bufs, count + lag):
        body(Step(i // bufs, i % bufs, bufs))


def since(eng, sem, step, back, per=1):
    if step.at_least(back):
        eng.wait_ge(sem, (step.t - back + 1) * per)


def build_constants(nc, k):
    with ExitStack() as ctx:
        m = Core(nc, ctx, "const")
        diff = m.sb("diff", [P, P], I32)
        node = m.sb("node", [P, P], I32)
        steps = m.sb("steps", [P, NST + 1], I32)
        part = m.sb("part", [P, 1], I32)
        iotas_written = m.sem("iotas_written")
        dve_step = m.sem("dve_step")
        block = ctx.enter_context(nc.Block())

        @block.gpsimd
        def _(pool):
            nc.gpsimd.iota(diff[:, :], [[1, P]], base=0, channel_multiplier=-1).then_inc(iotas_written, 1)
            nc.gpsimd.iota(node[:, :], [[1, P]], base=0, channel_multiplier=0).then_inc(iotas_written, 1)
            nc.gpsimd.iota(steps[:, :], [[1, NST + 1]], base=0, channel_multiplier=0).then_inc(iotas_written, 1)
            nc.gpsimd.iota(part[:, :], [[0, 1]], base=0, channel_multiplier=1).then_inc(iotas_written, 1)

        @block.vector
        def _(dve):
            c = Chain(dve, dve_step)
            dve.wait_ge(iotas_written, 4)
            nc.vector.tensor_scalar(k.ident[:, :], diff[:, :], 0, None, ALU.is_equal).then_inc(dve_step, 1)
            nc.vector.tensor_scalar(k.identb[:, :], diff[:, :], 0, None, ALU.is_equal).then_inc(dve_step, 1)
            nc.vector.tensor_scalar(k.ident_neg[:, :], diff[:, :], 0, -BIG, ALU.is_equal, ALU.mult).then_inc(dve_step, 1)
            nc.vector.tensor_scalar(k.tri[:, :], diff[:, :], 0, None, ALU.is_gt).then_inc(dve_step, 1)
            nc.vector.tensor_copy(k.node[:, :], node[:, :]).then_inc(dve_step, 1)
            nc.vector.tensor_copy(k.steps[:, :], steps[:, :]).then_inc(dve_step, 1)
            nc.vector.tensor_copy(k.typ[:, 0:REL], node[:, 0:REL]).then_inc(dve_step, 1)
            nc.vector.tensor_copy(k.typ[:, REL:P], node[:, 0:REL]).then_inc(dve_step, 1)
            nc.vector.tensor_copy(k.part[:, :], part[:, :]).then_inc(dve_step, 1)
            nc.vector.memset(k.ones[:, :], 1.0).then_inc(dve_step, 1)


def sort_edges(nc, p, d, k):
    with ExitStack() as ctx:
        m = Core(nc, ctx, "sort")
        src = m.sb("src", [EP, EC], I32)
        dst = m.sb("dst", [EP, EC], I32)
        typ = m.sb("typ", [EP, EC], I32)
        tmp_i = m.sb("tmp_i", [EP, EC], I32)
        rec = m.sb("rec", [EP, EC, 4])
        win = m.sb("win", [EP, EC], BF16)
        mask = [m.sb(f"mask{b}", [EP, EC], BF16) for b in range(2)]
        run = m.sb("run", [EP, EC])
        placed = [m.sb(f"placed{b}", [EP, EC]) for b in range(2)]
        zero = m.sb("zero", [EP, EC], BF16)
        pos = m.sb("pos", [EP, EC])
        pos_i = m.sb("pos_i", [EP, EC], I32)
        cur = m.sb("cur", [P, 1])
        off_a = m.sb("off_a", [P, 1])
        tot = m.sb("tot", [EP, W])
        nst = m.sb("nst", [P, W])
        nst_i = m.sb("nst_i", [P, W], I32)
        ends = m.sb("ends", [P, W])
        off = m.sb("off", [P, W])
        wst = m.sb("wst", [P, NST + 1])
        empty = m.sb("empty", [P, NST * J, 4])
        st_rec = [m.sb(f"st_rec{b}", [EP, SCAT_COLS, 4], I32) for b in range(SCAT_BUFS)]
        st_pos = [m.sb(f"st_pos{b}", [EP, SCAT_COLS], I32) for b in range(SCAT_BUFS)]
        before_ps = m.ps("before_ps", [P, W])
        total_ps = m.ps("total_ps", [P, W])
        edges_in = m.sem("edges_in")
        empties_set = m.sem("empties_set")
        empties_out = m.sem("empties_out")
        dve_step = m.sem("dve_step")
        totals_ready = m.sem("totals_ready")
        prefix_ready = m.sem("prefix_ready")
        placed_ready = m.sem("placed_ready")
        placed_added = m.sem("placed_added")
        staged = m.sem("staged")
        issue_step = m.sem("issue_step")
        scattered = [m.sem(f"scattered{b}", pool_dma=True) for b in range(SCAT_BUFS)]
        rounds = EC // (SCAT_BUFS * SCAT_COLS)
        block = ctx.enter_context(nc.Block())

        @block.sync
        def _(sp):
            for name, to in (("src", src), ("dst", dst), ("edge_type_64", typ)):
                sp.dma_start(to[:, :], p[name].rearrange("(p t) -> p t", p=EP)).then_inc(edges_in, 16)
            sp.wait_ge(empties_set, 2)
            sp.dma_start(d.slots.rearrange("(p t) f -> p t f", p=P), empty[:, :, :].bitcast(I32)).then_inc(empties_out, 16)
            sp.wait_ge(empties_out, 16)

        @block.gpsimd
        def _(pool):
            nc.gpsimd.memset(empty[:, :, :], 0.0).then_inc(empties_set, 1)
            pool.wait_ge(empties_set, 1)
            nc.gpsimd.memset(empty[:, :, 0:1], -1.0).then_inc(empties_set, 1)

            def add(t, b, kk):
                pool.wait_ge(placed_ready, t + 1)
                if used(kk) or b:
                    pool.wait_ge(placed_added, t)
                nc.gpsimd.tensor_tensor(pos[:, :], pos[:, :], placed[b][:, :], ALU.add).then_inc(placed_added, 1)
            ring(pool, W, 2, add)
            pool.wait_ge(empties_out, 16)

            def scatter(t, b, kk):
                pool.wait_ge(staged, (t + 1) * 2)
                pool.sem_inc(issue_step, 1)
                for j in range(SCAT_COLS):
                    pool.indirect_dma_start(d.slots, bass.IndirectOffsetOnAxis(ap=st_pos[b][:, j:j + 1], axis=0),
                                            st_rec[b][:, j, :], None).then_inc(scattered[b], 16)
            ring(pool, rounds * SCAT_BUFS, SCAT_BUFS, scatter)
            for b in range(SCAT_BUFS):
                pool.wait_ge(scattered[b], 16 * SCAT_COLS * rounds)

        @block.tensor
        def _(pe):
            pe.wait_ge(totals_ready, 1)
            nc.tensor.matmul(before_ps[0:EP, :], k.tri[0:EP, 0:EP], tot[:, :], start=True, stop=True).then_inc(prefix_ready, 1)
            nc.tensor.matmul(total_ps[:, :], k.ones[0:EP, :], tot[:, :], start=True, stop=True).then_inc(prefix_ready, 1)

        @block.vector
        def _(dve):
            c = Chain(dve, dve_step)
            c.link(nc.vector.memset(cur[:, :], 0.0))
            c.link(nc.vector.memset(zero[:, :], 0.0))
            c.link(nc.vector.memset(pos[:, :], 0.0))
            c.link(nc.vector.memset(wst[:, :], 0.0))
            dve.wait_ge(edges_in, 48)
            c.link(nc.vector.tensor_scalar(tmp_i[:, :], src[:, :], P - 1, None, ALU.bitwise_and))
            c.link(nc.vector.tensor_copy(rec[:, :, 0], tmp_i[:, :]))
            c.link(nc.vector.tensor_scalar(rec[:, :, 1], dst[:, :], -float(MID), None, ALU.add))
            c.link(nc.vector.tensor_copy(rec[:, :, 2], typ[:, :]))
            c.link(nc.vector.tensor_copy(rec[:, :, 3].bitcast(I32), dst[:, :]))
            c.link(nc.vector.tensor_scalar(tmp_i[:, :], src[:, :], 7, None, ALU.logical_shift_right))
            c.link(nc.vector.tensor_copy(win[:, :], tmp_i[:, :]))
            with c.loop(0, W, 2) as a:
                c.link(nc.vector.tensor_scalar(mask[0][:, :], win[:, :], cur[0:EP, :], 0.0, ALU.is_equal, ALU.add,
                                               accum_out=tot[:, bass.ds(a, 1)]))
                c.link(nc.vector.tensor_scalar(cur[:, :], cur[:, :], 1.0, None, ALU.add))
            c.link(nc.vector.memset(cur[:, :], 0.0))
            nc.vector.memset(nst[:, :], 0.0).then_inc(totals_ready, 1)
            dve.wait_ge(prefix_ready, 2)
            c.link(nc.vector.tensor_scalar(nst_i[:, :], total_ps[:, :], 1.0, S - 1.0, ALU.max, ALU.add))
            c.link(nc.vector.tensor_scalar(nst_i[:, :], nst_i[:, :], SHIFT, None, ALU.logical_shift_right))
            c.link(nc.vector.tensor_copy(nst[:, :], nst_i[:, :]))
            c.link(nc.vector.tensor_tensor_scan(ends[:, :], nst[:, :], zero_row(k), 0.0, ALU.add, ALU.add))
            c.link(nc.vector.tensor_tensor(off[:, :], ends[:, :], nst[:, :], ALU.subtract))
            c.link(nc.vector.tensor_scalar(off[:, :], off[:, :], float(S), -1.0, ALU.mult, ALU.add))
            c.link(nc.vector.tensor_tensor(off[0:EP, :], off[0:EP, :], before_ps[0:EP, :], ALU.add))
            def place(t, b, kk):
                c.add(nc.vector.tensor_scalar(mask[b][:, :], win[:, :], cur[0:EP, :], None, ALU.is_equal))
                c.link(nc.vector.tensor_copy(off_a[0:EP, :], off[0:EP, bass.ds(t, 1)]))
                c.add(nc.vector.tensor_scalar(cur[:, :], cur[:, :], 1.0, None, ALU.add))
                c.link(nc.vector.tensor_tensor_scan(run[:, :], mask[b][:, :], zero[:, :], off_a[0:EP, :], ALU.add, ALU.add))
                if used(kk):
                    dve.wait_ge(placed_added, t - 1)
                nc.vector.tensor_tensor(placed[b][:, :], run[:, :], mask[b][:, :], ALU.mult).then_inc(placed_ready, 1)
            ring(dve, W, 2, place, c, 8)
            dve.wait_ge(placed_added, W)
            c.link(nc.vector.tensor_copy(pos_i[:, :], pos[:, :]))

            def stage(t, b, kk):
                if used(kk):
                    dve.wait_ge(scattered[b], kk * 16 * SCAT_COLS)
                nc.vector.tensor_scalar(st_pos[b][:, :], pos_i[:, bass.ds(t * SCAT_COLS, SCAT_COLS)], 0, None,
                                        ALU.bitwise_or).then_inc(staged, 1)
                nc.vector.tensor_scalar(st_rec[b][:, :, :], rec[:, bass.ds(t * SCAT_COLS, SCAT_COLS), :].bitcast(I32), 0,
                                        None, ALU.bitwise_or).then_inc(staged, 1)
            ring(dve, rounds * SCAT_BUFS, SCAT_BUFS, stage)
            with c.loop(0, W, 2) as a:
                c.link(nc.vector.tensor_copy(off_a[:, :], ends[:, bass.ds(a, 1)]))
                c.link(nc.vector.scalar_tensor_tensor(wst[:, :], k.steps[:, :], off_a[:, :], wst[:, :], ALU.is_ge, ALU.add))
            c.link(nc.vector.tensor_copy(k.window_of[:, :], wst[:, 0:NST]))
            c.link(nc.vector.tensor_tensor(k.last_of[:, :], wst[:, 0:NST], wst[:, 1:NST + 1], ALU.not_equal))
            c.link(nc.vector.memset(k.cap[:, :], 0.0))
            c.link(nc.vector.tensor_tensor(k.cap[:, 1:NST], wst[:, 0:NST - 1], wst[:, 1:NST], ALU.is_equal))
            c.link(nc.vector.tensor_scalar(k.cap[:, :], k.cap[:, :], 2 * BIG, -BIG, ALU.mult, ALU.add))


def zero_row(k):
    return k.zeros[:, 0:W]


def count_pairs(nc, d, k):
    with ExitStack() as ctx:
        m = Core(nc, ctx, "count")
        tail_i = m.sb("tail_i", [P, NC], I32)
        tail = m.sb("tail", [P, NC], F16)
        iota_written = m.sem("iota_written")
        tail_set = m.sem("tail_set")
        rec = [m.sb(f"rec{b}", [P, J, 4]) for b in range(2)]
        head_hot = [m.sb(f"head_hot{b}", [P, J, P], BF16) for b in range(2)]
        tail_hot = [m.sb(f"tail_hot{b}", [P, J, NC], BF16) for b in range(2)]
        cum = [m.sb(f"cum{b}", [P, NC]) for b in range(2)]
        acc = m.ps("acc", [P, NCH, 512])
        rec_in = [m.sem(f"rec_in{b}") for b in range(2)]
        hot_ready = m.sem("hot_ready")
        counted = m.sem("counted")
        cleared = m.sem("cleared")
        copied = m.sem("copied")
        cum_out = [m.sem(f"cum_out{b}", pool_dma=True) for b in range(2)]
        block = ctx.enter_context(nc.Block())
        slots = d.slots.rearrange("(s p j) f -> s p (j f)", p=P, j=J)

        @block.sync
        def _(sp):
            def step(t, b, kk):
                if used(kk):
                    sp.wait_ge(hot_ready, (t - 1) * 2 * J)
                sp.dma_start(rec[b][:, :, :].rearrange("p j f -> p (j f)").bitcast(I32), slots[bass.ds(t, 1), :, :].rearrange("s p f -> p (s f)")).then_inc(rec_in[b], 16)
            ring(sp, NST, 2, step)

        @block.gpsimd
        def _(pool):
            nc.gpsimd.iota(tail_i[:, :], [[1, NC]], base=-MID, channel_multiplier=0).then_inc(iota_written, 1)

            def step(t, b, kk):
                w = pool.value_load(k.window_of[0:1, bass.ds(t, 1)], min_val=0, max_val=W)
                last = pool.value_load(k.last_of[0:1, bass.ds(t, 1)], min_val=0, max_val=1)
                pool.wait_ge(copied, (t + 1) * NCH)
                pool.sem_inc(k.issue, 1)
                pool.dma_start(d.cum[bass.ds(w, 1), :, :].rearrange("s p f -> p (s f)"), cum[b][:, :], cond=last).then_inc(cum_out[b], 16)
            ring(pool, NST, 2, step)
            for b in range(2):
                pool.wait_ge(cum_out[b], 16 * (NST // 2))

        @block.vector
        def _(dve):
            dve.wait_ge(iota_written, 1)
            nc.vector.tensor_copy(tail[:, :], tail_i[:, :]).then_inc(tail_set, 1)
            dve.wait_ge(tail_set, 1)

            def step(t, b, kk):
                dve.wait_ge(rec_in[b], (kk + 1) * 16)
                if used(kk):
                    dve.wait_ge(counted, (t - 1) * NCH)
                for j in range(J):
                    nc.vector.tensor_scalar(head_hot[b][:, j, :], k.node[:, :], rec[b][:, j, 0:1], None,
                                            ALU.is_equal).then_inc(hot_ready, 1)
                for j in range(J):
                    nc.vector.tensor_scalar(tail_hot[b][:, j, :], tail[:, :], rec[b][:, j, 1:2], None,
                                            ALU.is_equal).then_inc(hot_ready, 1)
            ring(dve, NST, 2, step)

        @block.tensor
        def _(pe):
            for c in range(NCH):
                nc.tensor.matmul(acc[:, c, 0:CCH], k.zerosb[:, 0:P], k.zerosb[:, 0:CCH], start=True, stop=False,
                                 skip_group_check=True).then_inc(cleared, 1)

            def step(t, b, kk):
                pe.wait_ge(hot_ready, (t + 1) * 2 * J)
                for c in range(NCH):
                    if used(kk) or b:
                        pe.wait_ge(copied, (t - 1) * NCH + c + 1)
                    for j in range(J):
                        mm = nc.tensor.matmul(acc[:, c, 0:CCH], head_hot[b][:, j, :], tail_hot[b][:, j, c * CCH:(c + 1) * CCH],
                                              start=False, stop=False, skip_group_check=True)
                    mm.then_inc(counted, 1)
            ring(pe, NST, 2, step)

        @block.scalar
        def _(act):
            def step(t, b, kk):
                if used(kk):
                    act.wait_ge(cum_out[b], kk * 16)
                for c in range(NCH):
                    act.wait_ge(counted, t * NCH + c + 1)
                    nc.scalar.copy(cum[b][:, c * CCH:(c + 1) * CCH], acc[:, c, 0:CCH]).then_inc(copied, 1)
            ring(act, NST, 2, step)


def split_counts(nc, d, k):
    B = 3
    G = -(-W // 4)
    with ExitStack() as ctx:
        m = Core(nc, ctx, "split")
        cum = [m.sb(f"cum{b}", [P, NC]) for b in range(B)]
        cnt = [m.sb(f"cnt{b}", [P, NP]) for b in range(B)]
        cntT = [m.sb(f"cntT{b}", [P, NP]) for b in range(B)]
        ps = m.ps("ps", [P, G, 512])
        cum_in = [m.sem(f"cum_in{b}") for b in range(B)]
        padding_set = m.sem("padding_set")
        cnt_ready = m.sem("cnt_ready")
        turned = m.sem("turned")
        turned_copied = m.sem("turned_copied")
        degree_ready = m.sem("degree_ready")
        cnt_out = [m.sem(f"cnt_out{b}", pool_dma=True) for b in range(B)]
        cntT_out = [m.sem(f"cntT_out{b}", pool_dma=True) for b in range(B)]
        block = ctx.enter_context(nc.Block())
        cntT_cols = d.cntT.rearrange("j p (w n) -> p j w n", n=P)

        @block.sync
        def _(sp):
            def load(t, b, kk):
                if used(kk):
                    sp.wait_ge(cnt_ready, t - 1)
                sp.dma_start(cum[b][:, :], d.cum[bass.ds(t, 1), :, :].rearrange("s p f -> p (s f)")).then_inc(cum_in[b], 16)
            ring(sp, W, B, load)

        @block.gpsimd
        def _(pool):
            def store(t, b, kk):
                pool.wait_ge(cnt_ready, t + 1)
                pool.sem_inc(k.issue, 1)
                pool.dma_start(d.cnt[bass.ds(t, 1), :, :].rearrange("s p f -> p (s f)"), cnt[b][:, 0:NC]).then_inc(cnt_out[b], 16)
                pool.wait_ge(turned_copied, (t + 1) * G)
                pool.sem_inc(k.issue, 1)
                pool.dma_start(cntT_cols[:, :, bass.ds(t, 1), :].rearrange("p j w n -> p (j w) n"),
                               cntT[b][:, :].rearrange("p (j n) -> p j n", n=P)).then_inc(cntT_out[b], 16)
            ring(pool, W, B, store)
            for b in range(B):
                pool.wait_ge(cnt_out[b], 16 * ((W + B - 1 - b) // B))
                pool.wait_ge(cntT_out[b], 16 * ((W + B - 1 - b) // B))

        @block.vector
        def _(dve):
            for b in range(B):
                nc.vector.memset(cnt[b][:, NC:NP], 0.0).then_inc(padding_set, 1)

            def step(t, b, kk):
                dve.wait_ge(cum_in[b], (kk + 1) * 16)
                if used(kk):
                    dve.wait_ge(cnt_out[b], kk * 16)
                    dve.wait_ge(turned, (t - B + 1) * G)
                    dve.wait_ge(degree_ready, t - B + 1)
                if used(kk) or b:
                    nc.vector.tensor_tensor(cnt[b][:, 0:NC], cum[b][:, :], cum[(b - 1) % B][:, :], ALU.subtract).then_inc(cnt_ready, 1)
                else:
                    nc.vector.tensor_copy(cnt[b][:, 0:NC], cum[b][:, :]).then_inc(cnt_ready, 1)
                dve.wait_ge(cnt_ready, t + 1)
                nc.vector.tensor_reduce(k.degree[:, bass.ds(t, 1)], cnt[b][:, 0:NC], AX.X, ALU.add).then_inc(degree_ready, 1)
            ring(dve, W, B, step)

        @block.tensor
        def _(pe):
            pe.wait_ge(padding_set, B)

            def step(t, b, kk):
                pe.wait_ge(cnt_ready, t + 1)
                for g in range(G):
                    if used(kk) or b:
                        pe.wait_ge(turned_copied, (t - 1) * G + g + 1)
                    for j in range(4 * g, min(4 * g + 4, W)):
                        mm = nc.tensor.transpose(ps[:, g, (j % 4) * P:(j % 4 + 1) * P], cnt[b][:, j * P:(j + 1) * P], k.ident[:, :])
                    mm.then_inc(turned, 1)
            ring(pe, W, B, step)

        @block.scalar
        def _(act):
            def step(t, b, kk):
                if used(kk):
                    act.wait_ge(cntT_out[b], kk * 16)
                for g in range(G):
                    n = min(4, W - 4 * g) * P
                    act.wait_ge(turned, t * G + g + 1)
                    nc.scalar.copy(cntT[b][:, g * 512:g * 512 + n], ps[:, g, 0:n]).then_inc(turned_copied, 1)
            ring(act, W, B, step)


def bc(ap, shape):
    return ap.broadcast_to(shape)


def turn(nc, k, nodes, cols, tag):
    G = -(-W // 4)
    with ExitStack() as ctx:
        m = Core(nc, ctx, tag)
        ps = m.ps("ps", [P, G, 512])
        turned = m.sem("turned")
        block = ctx.enter_context(nc.Block())

        @block.tensor
        def _(pe):
            for w in range(W):
                mm = nc.tensor.transpose(ps[:, w // 4, (w % 4) * P:(w % 4 + 1) * P], nodes[:, w * P:(w + 1) * P], k.ident[:, :])
                if w % 4 == 3 or w == W - 1:
                    mm.then_inc(turned, 1)

        @block.scalar
        def _(act):
            for g in range(G):
                n = min(4, W - 4 * g) * P
                act.wait_ge(turned, g + 1)
                nc.scalar.copy(cols[:, g * 512:g * 512 + n], ps[:, g, 0:n])


def load_inputs(nc, p, k):
    with ExitStack() as ctx:
        m = Core(nc, ctx, "load")
        cleared = m.sem("cleared")
        x_in = m.sem("x_in")
        block = ctx.enter_context(nc.Block())

        @block.vector
        def _(dve):
            nc.vector.memset(k.x[:, :], 0.0).then_inc(cleared, 1)

        @block.sync
        def _(sp):
            sp.wait_ge(cleared, 1)
            x = k.x[:, :].rearrange("p (w d) -> p w d", d=D)
            sp.dma_start(x[:, 0:W - 1, :], p['x'][0:(W - 1) * P, :].rearrange("(w p) d -> p w d", p=P)).then_inc(x_in, 16)
            sp.dma_start(x[0:TAIL, W - 1, :], p['x'][(W - 1) * P:N, :]).then_inc(x_in, 16)
            sp.wait_ge(x_in, 32)


def attention_project(nc, p, d, k, xT, row_s, row_d):
    G = -(-W // 4)
    with ExitStack() as ctx:
        m = Core(nc, ctx, "proj")
        coef = m.sb("coef", [P, 3])
        lw = m.sb("lw", [P, 3, D])
        raw = {n: m.sb(n, [P, 3, D]) for n in ("bias", "att_src", "att_dst")}
        mixed = {n: m.sb(n + "_mix", [P, D]) for n in ("weight", "bias", "att_src", "att_dst")}
        names = ["weight", "bias", "att_src", "att_dst"]
        flipped = {n: m.sb(n + "_T", [P, D]) for n in names}
        ge = m.sb("ge", [P, H + 1])
        head_s = m.sb("head_s", [P, H, P])
        head_d = m.sb("head_d", [P, H, P])
        xt = m.sb("xt", [P, NP])
        xtT = m.sb("xtT", [P, NP])
        tmp = xT
        flag = m.sb("flag", [P, 1])
        lhs = m.sb("lhs", [P, W, k.LHS])
        ps = m.ps("ps", [P, NCH, 512])
        params_in = m.sem("params_in")
        mixes_ready = m.sem("mixes_ready")
        flips = m.sem("flips")
        flips_ready = m.sem("flips_ready")
        xt_summed = m.sem("xt_summed")
        xt_ready = m.sem("xt_ready")
        xtT_summed = m.sem("xtT_summed")
        xtT_ready = m.sem("xtT_ready")
        row_summed = m.sem("row_summed")
        row_ready = m.sem("row_ready")
        dve_step = m.sem("dve_step")
        lhs_ready = m.sem("lhs_ready")
        lhs_out = m.sem("lhs_out")
        block = ctx.enter_context(nc.Block())

        @block.sync
        def _(sp):
            sp.dma_start(coef[:, :], p['L0_gnn_coeffs_t'].partition_broadcast(P)).then_inc(params_in, 16)
            sp.dma_start(lw[:, :, :], p['L0_gnn_lin_weight'].rearrange("b o i -> o b i")).then_inc(params_in, 16)
            sp.dma_start(raw["bias"][:, :, :], p['L0_gnn_lin_bias'].partition_broadcast(P)).then_inc(params_in, 16)
            for n in ("att_src", "att_dst"):
                sp.dma_start(raw[n][:, :, :], p['L0_gnn_' + n].rearrange("b q h c -> (b q) (h c)").partition_broadcast(P)).then_inc(params_in, 16)
            sp.wait_ge(lhs_ready, 1)
            sp.dma_start(d.lhs.rearrange("w p f -> p w f"), lhs[:, :, :]).then_inc(lhs_out, 16)
            sp.wait_ge(lhs_out, 16)

        @block.tensor
        def _(pe):
            pe.wait_ge(mixes_ready, 1)
            for n, name in enumerate(names):
                mm = nc.tensor.transpose(ps[:, 7, n * P:(n + 1) * P], mixed[name][:, :], k.ident[:, :])
            mm.then_inc(flips, 1)
            pe.wait_ge(flips_ready, 1)
            for w in range(W):
                mm = nc.tensor.matmul(ps[:, w // 4, (w % 4) * P:(w % 4 + 1) * P], xT[:, w * P:(w + 1) * P],
                                      flipped["weight"][:, :], start=True, stop=True)
                if w % 4 == 3 or w == W - 1:
                    mm.then_inc(xt_summed, 1)
            for c in range(NCH):
                if c < G:
                    pe.wait_ge(xt_ready, c + 1)
                nc.tensor.matmul(ps[:, c, 0:CH], flipped["weight"][:, :], xT[:, c * CH:(c + 1) * CH], start=True,
                                 stop=True).then_inc(xtT_summed, 1)
            pe.wait_ge(xtT_ready, NCH)
            for r in range(2 * H):
                for c in range(NCH):
                    if r:
                        pe.wait_ge(row_ready, (r - 1) * NCH + c + 1)
                    nc.tensor.matmul(ps[:, c, 0:CH], (head_s if r < H else head_d)[:, r % H, :],
                                     xtT[:, c * CH:(c + 1) * CH], start=True, stop=True).then_inc(row_summed, 1)

        @block.scalar
        def _(act):
            act.wait_ge(flips_ready, 1)
            for c in range(NCH):
                act.wait_ge(xtT_summed, c + 1)
                nc.scalar.activation(xtT[:, c * CH:(c + 1) * CH], ps[:, c, 0:CH], ACT.Identity,
                                     bias=flipped["bias"][:, 0:1]).then_inc(xtT_ready, 1)
            for r in range(2 * H):
                for c in range(NCH):
                    act.wait_ge(row_summed, r * NCH + c + 1)
                    nc.scalar.copy((row_s if r < H else row_d)[:, r % H, c * CH:(c + 1) * CH], ps[:, c, 0:CH]).then_inc(row_ready, 1)

        @block.vector
        def _(dve):
            c = Chain(dve, dve_step)
            c.link(nc.vector.memset(lhs[:, :, :], 0.0))
            dve.wait_ge(params_in, 5 * 16)
            for name in names:
                r = lw if name == "weight" else raw[name]
                c.link(nc.vector.tensor_scalar(mixed[name][:, :], r[:, 0, :], coef[:, 0:1], None, ALU.mult))
                for b in (1, 2):
                    c.link(nc.vector.scalar_tensor_tensor(mixed[name][:, :], r[:, b, :], coef[:, b:b + 1],
                                                          mixed[name][:, :], ALU.mult, ALU.add))
            c.link(nc.vector.tensor_scalar(ge[:, :], k.steps[:, 0:H + 1], float(C), k.part[:, 0:1], ALU.mult, ALU.is_le))
            c.link(nc.vector.tensor_tensor(ge[:, 0:H], ge[:, 0:H], ge[:, 1:H + 1], ALU.subtract))
            nc.vector.tensor_copy(flag[:, :], ge[:, 0:1]).then_inc(mixes_ready, 1)
            dve.wait_ge(flips, 1)
            for n, name in enumerate(names):
                c.link(nc.vector.tensor_copy(flipped[name][:, :], ps[:, 7, n * P:(n + 1) * P]))
            for h in range(H):
                c.link(nc.vector.tensor_scalar(head_s[:, h, :], flipped["att_src"][:, :], ge[:, h:h + 1], None, ALU.mult))
                c.link(nc.vector.tensor_scalar(head_d[:, h, :], flipped["att_dst"][:, :], ge[:, h:h + 1], None, ALU.mult))
            nc.vector.tensor_copy(flag[:, :], ge[:, 0:1]).then_inc(flips_ready, 1)
            for g in range(G):
                n = min(4, W - 4 * g)
                dve.wait_ge(xt_summed, g + 1)
                nc.vector.tensor_tensor(xt[:, g * 512:g * 512 + n * P].rearrange("p (w f) -> p w f", f=P),
                                        ps[:, g, 0:n * P].rearrange("p (w f) -> p w f", f=P),
                                        bc(mixed["bias"][:, None, :], [P, n, P]), ALU.add).then_inc(xt_ready, 1)
            dve.wait_ge(xt_ready, G)
            dve.wait_ge(xtT_summed, NCH)
            xt3 = xt[:, :].rearrange("p (w f) -> p w f", f=P)
            tmp3 = tmp[:, :].rearrange("p (w f) -> p w f", f=P)
            for name, to in (("att_src", k.col_s), ("att_dst", k.col_d)):
                c.link(nc.vector.tensor_tensor(tmp3, xt3, bc(mixed[name][:, None, :], [P, W, P]), ALU.mult))
                c.link(nc.vector.tensor_reduce(to[:, :], tmp[:, :].rearrange("p (w c) -> p w c", c=C), AX.X, ALU.add))
            HW = C + 1
            for h in range(H):
                at = h * 3 * HW + h * HW if h < 3 else 9 * HW
                c.link(nc.vector.tensor_copy(lhs[:, :, at:at + C], xt3[:, :, h * C:(h + 1) * C]))
                c.link(nc.vector.memset(lhs[:, :, at + C:at + HW], 1.0))
            cs = k.col_s[:, :].rearrange("p (w h) -> p w h", h=H)
            c.link(nc.vector.tensor_copy(lhs[:, :, 10 * HW:10 * HW + H], cs))
            nc.vector.tensor_scalar(lhs[:, :, 10 * HW + H:10 * HW + 2 * H], cs, 0.2, None, ALU.mult).then_inc(lhs_ready, 1)


def attention_max(nc, d, k, row_s):
    with ExitStack() as ctx:
        m = Core(nc, ctx, "amax")
        cnt = [m.sb(f"cnt{b}", [P, N]) for b in range(2)]
        masked = [m.sb(f"masked{b}", [P, N]) for b in range(2)]
        spare = m.sb("spare", [P, H, N], BF16)
        best = [m.sb(f"best{b}", [P, H]) for b in range(2)]
        go = m.sb("go", [P, 1])
        big = m.sb("big", [P, 1])
        z = m.sb("z", [P, W * H])
        rec = [m.sb(f"rec{q}", [P, K * J, 4]) for q in range(KINDS)]
        hot = [m.sb(f"hot{i}", [P, K * J, P], BF16) for i in range(2)]
        hotT = [m.sb(f"hotT{i}", [P, K, S], BF16) for i in range(2)]
        ps_turn = [m.ps(f"ps_turn{i}", [P, S]) for i in range(K)]
        rec_in = [m.sem(f"rec_in{q}") for q in range(KINDS)]
        hot_out = [m.sem(f"hot_out{i}") for i in range(2)]
        hot_ready = m.sem("hot_ready")
        hot_turned = m.sem("hot_turned")
        hot_copied = m.sem("hot_copied")
        cnt_in = [m.sem(f"cnt_in{b}") for b in range(2)]
        masks_made = m.sem("masks_made")
        mask_seen = m.sem("mask_seen")
        big_set = m.sem("big_set")
        maxima_found = m.sem("maxima_found")
        maxima_kept = m.sem("maxima_kept")
        dve_step = m.sem("dve_step")
        block = ctx.enter_context(nc.Block())
        slots = d.slots.rearrange("(s p j) f -> s p (j f)", p=P, j=J)

        @block.sync
        def _(sp):
            def store(t, b):
                for q in range(KINDS):
                    u = (b * KINDS + q) % 2
                    sp.wait_ge(hot_copied, (t * KINDS + q + 1) * K)
                    sp.dma_start(d.type_hots[bass.ds((t * KINDS + q) * K, K), :, :].rearrange("s p f -> p s f"),
                                 hotT[u][:, :, :]).then_inc(hot_out[u], 16)

            def load(t, b, kk):
                if used(kk):
                    sp.wait_ge(masks_made, t - 1)
                sp.dma_start(cnt[b][:, :], d.cntT[bass.ds(t, 1), :, 0:N].rearrange("s p f -> p (s f)")).then_inc(cnt_in[b], 16)
                for q in range(KINDS):
                    if used(kk) or b:
                        sp.wait_ge(hot_ready, (t - 1) * KINDS + q + 1)
                    sp.dma_start(rec[q][:, :, :].rearrange("p (k j) f -> p k (j f)", j=J).bitcast(I32),
                                 slots[bass.ds((t * KINDS + q) * K, K), :, :].rearrange("s p f -> p s f")).then_inc(rec_in[q], 16)
                if used(kk) or b:
                    store(t - 1, 1 - b)
            ring(sp, W, 2, load)
            store(W - 1, (W - 1) % 2)
            for u in range(2):
                sp.wait_ge(hot_out[u], 16 * ((W * KINDS + 1 - u) // 2))

        @block.gpsimd
        def _(pool):
            def make(t, b, kk):
                for q in range(KINDS):
                    pool.wait_ge(rec_in[q], (t + 1) * 16)
                    if used(kk) or b * KINDS + q >= 2:
                        pool.wait_ge(hot_turned, (t * KINDS + q - 1) * K)
                    pool.sem_inc(k.issue, 1)
                    for i in range(K * J):
                        make_hot = nc.gpsimd.tensor_scalar(hot[(b * KINDS + q) % 2][:, i, :], k.typ[:, :], rec[q][:, i, 2:3], None,
                                                           ALU.is_equal)
                    make_hot.then_inc(hot_ready, 1)
            ring(pool, W, 2, make)

        @block.tensor
        def _(pe):
            def turn_hots(t, b, kk):
                for q in range(KINDS):
                    pe.wait_ge(hot_ready, t * KINDS + q + 1)
                    for i in range(K):
                        if used(kk) or b or q:
                            pe.wait_ge(hot_copied, (t * KINDS + q - 1) * K + i + 1)
                        for j in range(J):
                            mm = nc.tensor.matmul(ps_turn[i][:, j * P:(j + 1) * P], hot[(b * KINDS + q) % 2][:, i * J + j, :], k.identb[:, :],
                                                  start=True, stop=True)
                        mm.then_inc(hot_turned, 1)
            ring(pe, W, 2, turn_hots)

        @block.scalar
        def _(act):
            act.wait_ge(big_set, 1)

            def mask(t, b, kk):
                act.wait_ge(cnt_in[b], (kk + 1) * 16)
                if used(kk):
                    act.wait_ge(maxima_found, (t - 1) * H)
                nc.scalar.activation(masked[b][:, :], cnt[b][:, :], ACT.Relu, bias=big[:, :], scale=-BIG).then_inc(masks_made, 1)
                for q in range(KINDS):
                    for i in range(K):
                        act.wait_ge(hot_turned, (t * KINDS + q) * K + i + 1)
                        g = b * KINDS + q
                        if (used(kk) or g >= 2) and i == 0:
                            act.wait_ge(hot_out[g % 2], (kk * KINDS + g // 2) * 16)
                        nc.scalar.copy(hotT[g % 2][:, i, :], ps_turn[i][:, :]).then_inc(hot_copied, 1)
            ring(act, W, 2, mask)

        @block.vector
        def _(dve):
            c = Chain(dve, dve_step)
            nc.vector.memset(big[:, :], BIG).then_inc(big_set, 1)

            def keep(t, b):
                dve.wait_ge(maxima_found, (t + 1) * H)
                nc.vector.tensor_scalar(k.amax[:, bass.ds(t * H, H)], best[b][:, :], 0.0, None, ALU.add).then_inc(maxima_kept, 1)

            def step(t, b, kk):
                if used(kk) or b:
                    keep(t - 1, 1 - b)
                dve.wait_ge(masks_made, t + 1)
                nc.vector.tensor_copy(go[:, :], masked[b][:, 0:1]).then_inc(mask_seen, 1)
                for h in range(H):
                    nc.vector.tensor_tensor_reduce(spare[:, h, :], row_s[:, h, 0:N], masked[b][:, :], 1.0, -3.0e38, ALU.subtract, ALU.max,
                                                   best[b][:, h:h + 1]).then_inc(maxima_found, 1)
            ring(dve, W, 2, step)
            keep(W - 1, (W - 1) % 2)
            dve.wait_ge(maxima_kept, W)
            c.link(nc.vector.tensor_tensor(z[:, :], k.amax[:, :], k.col_d[:, :], ALU.add))
            c.link(nc.vector.scalar_tensor_tensor(k.amax[:, :], z[:, :], 0.2, z[:, :], ALU.mult, ALU.max))


def attention_rows(nc, k, row_d, pos_row, neg_row, w0, n):
    with ExitStack() as ctx:
        m = Core(nc, ctx, "rows")
        ps = m.ps("ps", [P, 8, 512])
        spread = m.sem("spread")
        rows_made = m.sem("rows_made")
        block = ctx.enter_context(nc.Block())
        groups = [(h, g) for h in range(H) for g in range(0, n, 4)]

        @block.tensor
        def _(pe):
            for i, (h, g) in enumerate(groups):
                if i >= 8:
                    pe.wait_ge(rows_made, 2 * (i - 7))
                for j in range(g, min(g + 4, n)):
                    col = k.amax[:, (w0 + j) * H + h:(w0 + j) * H + h + 1]
                    mm = nc.tensor.matmul(ps[:, i % 8, (j - g) * P:(j - g + 1) * P], bc(col, [P, P]), k.ident[:, :],
                                          start=True, stop=True)
                mm.then_inc(spread, 1)

        @block.vector
        def _(dve):
            for i, (h, g) in enumerate(groups):
                q = min(4, n - g) * P
                dve.wait_ge(spread, i + 1)
                r = row_d[:, h, (w0 + g) * P:(w0 + g) * P + q]
                nc.vector.tensor_tensor(pos_row[:, h, g * P:g * P + q], r, ps[:, i % 8, 0:q], ALU.subtract).then_inc(rows_made, 1)
                nc.vector.scalar_tensor_tensor(neg_row[:, h, g * P:g * P + q], r, 0.2, ps[:, i % 8, 0:q], ALU.mult,
                                               ALU.subtract).then_inc(rows_made, 1)


def attention_sum(nc, d, k, pos_row, neg_row, w0, n):
    HW = C + 1
    B = 3
    NT = n * P
    QC = -(-min(NT, N - w0 * P) // 4)
    NQ = 4 * QC
    with ExitStack() as ctx:
        m = Core(nc, ctx, "asum")
        cnt = [m.sb(f"cnt{b}", [P, NQ]) for b in range(B)]
        lhs = [m.sb(f"lhs{b}", [P, k.LHS]) for b in range(B)]
        low = [m.sb(f"low{b}", [P, NQ]) for b in range(2)]
        e_all = m.sb("e_all", [P, H * NT])
        e = [e_all[:, h * NT:(h + 1) * NT] for h in range(H)]
        wt = [m.sb(f"wt{b}", [P, NQ]) for b in range(3)]
        sums, sums3 = e[0], e[1]
        o = e_all[:, 2 * NT:2 * NT + n * H * HW].rearrange("p (w h c) -> p w h c", h=H, c=HW)
        den = m.sb("den", [P, n * H])
        ps = m.ps("ps", [P, 8, 512])
        in_ = [m.sem(f"in{b}") for b in range(B)]
        low_ready = m.sem("low_ready")
        raised = m.sem("raised")
        act_bound = m.sem("act_bound")
        dve_bound = m.sem("dve_bound")
        exp_ready = m.sem("exp_ready")
        dve_weighted = m.sem("dve_weighted")
        pool_weighted = m.sem("pool_weighted")
        weight_used = m.sem("weight_used")
        sums_copied = m.sem("sums_copied")
        turned = m.sem("turned")
        o_copied = m.sem("o_copied")
        padding_set = m.sem("padding_set")
        dve_step = m.sem("dve_step")
        block = ctx.enter_context(nc.Block())
        NG = -(-n // 3)

        @block.sync
        def _(sp):
            def load(t, b, kk):
                if used(kk):
                    sp.wait_ge(weight_used, (t - B + 1) * H)
                sp.dma_start(cnt[b][:, :], d.cnt[bass.ds(t, 1), :, w0 * P:w0 * P + NQ].rearrange("s p f -> p (s f)")).then_inc(in_[b], 16)
                sp.dma_start(lhs[b][:, :], d.lhs[bass.ds(t, 1), :, :].rearrange("s p f -> p (s f)")).then_inc(in_[b], 16)
            ring(sp, W, B, load)

        @block.scalar
        def _(act):
            def exp(t, h):
                x = e[h][:, 0:NQ]
                if h == 0:
                    act.wait_ge(raised, t * H + h + 1)
                    nc.scalar.activation(x, x, ACT.Relu, scale=-1.0).then_inc(act_bound, 1)
                    act.wait_ge(act_bound, t + 1)
                    nc.scalar.activation(x, x, ACT.Exp, scale=-1.0).then_inc(exp_ready, 1)
                else:
                    act.wait_ge(dve_bound, t * (H - 1) + h)
                    nc.scalar.activation(x, x, ACT.Exp).then_inc(exp_ready, 1)

            def lower(t, h, b, again):
                if again:
                    act.wait_ge(raised, t * H + h - 1)
                nc.scalar.activation(low[h % 2][:, :], neg_row[:, h, 0:NQ], ACT.Identity,
                                     bias=lhs[b][:, 10 * HW + H + h:10 * HW + H + h + 1]).then_inc(low_ready, 1)

            act.wait_ge(in_[0], 32)
            lower(0, 0, 0, False)

            def step(t, b, kk):
                again = used(kk) or b
                for h in range(H):
                    if h < H - 1:
                        lower(t, h + 1, b, again or h)
                    elif not isinstance(t, int) or t < W - 1:
                        act.wait_ge(in_[(b + 1) % B], (kk + 1 + (b + 1) // B) * 32)
                        lower(t + 1, 0, (b + 1) % B, True)
                    if h:
                        exp(t, h - 1)
                    elif again:
                        exp(t - 1, H - 1)
            ring(act, W, B, step)
            exp(W - 1, H - 1)
            act.wait_ge(weight_used, W * H)
            for c in range(4):
                nc.scalar.copy(sums[0:3 * HW, c * QC:(c + 1) * QC], ps[0:3 * HW, c, 0:QC]).then_inc(sums_copied, 1)
                nc.scalar.copy(sums3[0:HW, c * QC:(c + 1) * QC], ps[0:HW, 4 + c, 0:QC]).then_inc(sums_copied, 1)
            for g in range(NG):
                r = min(3, n - 3 * g)
                act.wait_ge(turned, g + 1)
                nc.scalar.copy(o[:, 3 * g:3 * g + r, :, :].rearrange("p w h c -> p (w h c)"), ps[:, g, 0:r * H * HW]).then_inc(o_copied, 1)

        @block.gpsimd
        def _(pool):
            def step(t, b, kk):
                for h in (1, 3):
                    if used(kk) or b or h == 3:
                        pool.wait_ge(weight_used, t * H + h - 1)
                    pool.wait_ge(exp_ready, t * H + h + 1)
                    nc.gpsimd.tensor_tensor(wt[2][:, :], e[h][:, 0:NQ], cnt[b][:, :], ALU.mult).then_inc(pool_weighted, 1)
            ring(pool, W, B, step)

        @block.vector
        def _(dve):
            c = Chain(dve, dve_step)
            if NQ < NT:
                for part in (sums, sums3):
                    nc.vector.memset(part[:, NQ:NT], 0.0).then_inc(padding_set, 1)

            def weight(t, h, b, again):
                dve.wait_ge(exp_ready, t * H + h + 1)
                if again:
                    dve.wait_ge(weight_used, (t - 1) * H + h + 1)
                nc.vector.tensor_tensor(wt[h // 2][:, :], e[h][:, 0:NQ], cnt[b][:, :], ALU.mult).then_inc(dve_weighted, 1)

            def step(t, b, kk):
                again = used(kk) or b
                dve.wait_ge(in_[b], (kk + 1) * 32)
                for h in range(H):
                    dve.wait_ge(low_ready, t * H + h + 1)
                    if again:
                        dve.wait_ge(pool_weighted if h % 2 else dve_weighted, (t - 1) * 2 + h // 2 + 1)
                    nc.vector.scalar_tensor_tensor(e[h][:, 0:NQ], pos_row[:, h, 0:NQ], lhs[b][:, 10 * HW + h:10 * HW + h + 1],
                                                   low[h % 2][:, :], ALU.add, ALU.max).then_inc(raised, 1)
                    if h:
                        dve.wait_ge(raised, t * H + h + 1)
                        nc.vector.tensor_scalar(e[h][:, 0:NQ], e[h][:, 0:NQ], 1.0, None, ALU.min).then_inc(dve_bound, 1)
                    if h == 2:
                        weight(t, 0, b, again)
                    elif h == 0 and again:
                        weight(t - 1, 2, (b - 1) % B, used(kk) or b > 1)
            ring(dve, W, B, step)
            weight(W - 1, 2, (W - 1) % B, True)
            dve.wait_ge(o_copied, NG)
            c.link(nc.vector.tensor_scalar(den[:, :], o[:, :, :, C].rearrange("p w h -> p (w h)"), 1e-16, None, ALU.add))
            c.link(nc.vector.reciprocal(den[:, :], den[:, :]))
            x = k.x[:, w0 * P:w0 * P + NT].rearrange("p (w c) -> p w c", c=C)
            o3 = o[:, :, :, :].rearrange("p w h c -> p (w h) c")[:, :, 0:C]
            c.link(nc.vector.tensor_tensor(o3, o3, bc(den[:, :, None], [P, n * H, C]), ALU.mult))
            c.link(nc.vector.tensor_tensor(x, x, o3, ALU.add))

        @block.tensor
        def _(pe):
            def step(t, b, kk):
                pe.wait_ge(in_[b], (kk + 1) * 32)
                first, last = isinstance(t, int) and t == 0, isinstance(t, int) and t == W - 1
                for h in range(H):
                    pe.wait_ge(pool_weighted if h % 2 else dve_weighted, t * 2 + h // 2 + 1)
                    rows = 3 * HW if h < 3 else HW
                    at = h * 3 * HW
                    for c in range(4):
                        mm = nc.tensor.matmul(ps[0:rows, (0 if h < 3 else 4) + c, 0:QC], lhs[b][:, at:at + rows],
                                              wt[2 if h % 2 else h // 2][:, c * QC:(c + 1) * QC], start=first and h in (0, 3),
                                              stop=last and h in (2, 3), skip_group_check=True)
                    mm.then_inc(weight_used, 1)
            ring(pe, W, B, step)
            pe.wait_ge(sums_copied, 8)
            if NQ < NT:
                pe.wait_ge(padding_set, 2)
            for j in range(n):
                g, r = j // 3, (j % 3) * H * HW
                nc.tensor.transpose(ps[:, g, r:r + 3 * HW], sums[0:3 * HW, j * P:(j + 1) * P], k.ident[0:3 * HW, 0:3 * HW])
                mm = nc.tensor.transpose(ps[:, g, r + 3 * HW:r + 4 * HW], sums3[0:HW, j * P:(j + 1) * P], k.ident[0:HW, 0:HW])
                if j % 3 == 2 or j == n - 1:
                    mm.then_inc(turned, 1)


def layer_norm(nc, k, tag, table=None, out=None):
    with ExitStack() as ctx:
        m = Core(nc, ctx, tag)
        sq = m.sb("sq", [P, NP])
        s = m.sb("s", [P, W])
        v = m.sb("v", [P, W])
        dve_step = m.sem("dve_step")
        var_ready = m.sem("var_ready")
        root_ready = m.sem("root_ready")
        norm_ready = m.sem("norm_ready")
        stored = m.sem("stored")
        block = ctx.enter_context(nc.Block())
        x = k.x[:, :].rearrange("p (w f) -> p w f", f=D)

        @block.vector
        def _(dve):
            c = Chain(dve, dve_step)
            c.link(nc.vector.tensor_reduce(s[:, :], x, AX.X, ALU.add))
            c.link(nc.vector.tensor_scalar(s[:, :], s[:, :], 1.0 / D, None, ALU.mult))
            c.link(nc.vector.tensor_tensor(x, x, bc(s[:, :, None], [P, W, D]), ALU.subtract))
            c.link(nc.vector.tensor_tensor(sq[:, :], k.x[:, :], k.x[:, :], ALU.mult))
            c.link(nc.vector.tensor_reduce(v[:, :], sq[:, :].rearrange("p (w f) -> p w f", f=D), AX.X, ALU.add))
            nc.vector.tensor_scalar(v[:, :], v[:, :], 1.0 / D, 1e-5, ALU.mult, ALU.add).then_inc(var_ready, 1)
            dve.wait_ge(root_ready, 1)
            c.link(nc.vector.reciprocal(v[:, :], v[:, :]))
            nc.vector.tensor_tensor(x, x, bc(v[:, :, None], [P, W, D]), ALU.mult).then_inc(norm_ready, 1)

        @block.scalar
        def _(act):
            act.wait_ge(var_ready, 1)
            nc.scalar.activation(v[:, :], v[:, :], ACT.Sqrt).then_inc(root_ready, 1)

        @block.sync
        def _(sp):
            sp.wait_ge(norm_ready, 1)
            if table is not None:
                sp.dma_start(table.rearrange("w p f -> p w f"), x).then_inc(stored, 16)
                sp.wait_ge(stored, 16)
            if out is not None:
                sp.dma_start(out[0:(W - 1) * P, :].rearrange("(w p) d -> p w d", p=P), x[:, 0:W - 1, :]).then_inc(stored, 16)
                sp.dma_start(out[(W - 1) * P:N, :], x[0:TAIL, W - 1, :]).then_inc(stored, 16)
                sp.wait_ge(stored, 32)


def aggregate(nc, d, k, table, counts, total, tag, add=None, first=None):
    B = 3
    G = 7
    chunks = [slice(c * 512, min((c + 1) * 512, N)) for c in range(G)]
    kinds = first is not None
    with ExitStack() as ctx:
        m = Core(nc, ctx, tag)
        rows = [m.sb(f"rows{b}", [P, D]) for b in range(B)]
        cnt = [m.sb(f"cnt{b}", [P, N]) for b in range(B)]
        rec = [m.sb(f"rec{b}", [P, K, J, 4]) for b in range(B)]
        hot = [m.sb(f"hot{b}", [P, K, J, P], BF16) for b in range(B)]
        hotT = [m.sb(f"hotT{b}", [P, K, S], BF16) for b in range(B)]
        ps = m.ps("ps", [P, G, 512])
        ps_turn = m.ps("ps_turn", [P, S])
        in_ = [m.sem(f"in{b}") for b in range(B)]
        rec_in = [m.sem(f"rec_in{b}") for b in range(B)]
        stored = [m.sem(f"stored{b}") for b in range(B)]
        hot_ready = m.sem("hot_ready")
        turned = m.sem("turned")
        copied = m.sem("copied")
        summed = m.sem("summed")
        block = ctx.enter_context(nc.Block())
        slots = d.slots.rearrange("(s p j) f -> s p (j f)", p=P, j=J)

        @block.sync
        def _(sp):
            def store(t, b):
                sp.wait_ge(copied, (t + 1) * K)
                sp.dma_start(d.type_hots[bass.ds(t * K + first, K), :, :].rearrange("s p f -> p s f"), hotT[b][:, :, :]).then_inc(stored[b], 16)

            def load(t, b, kk):
                if used(kk):
                    sp.wait_ge(summed, (t - B + 1) * G)
                sp.dma_start(rows[b][:, :], table[bass.ds(t, 1), :, :].rearrange("s p f -> p (s f)")).then_inc(in_[b], 16)
                sp.dma_start(cnt[b][:, :], counts[bass.ds(t, 1), :, 0:N].rearrange("s p f -> p (s f)")).then_inc(in_[b], 16)
                if kinds:
                    if used(kk):
                        sp.wait_ge(hot_ready, (t - B + 1) * K * J)
                    sp.dma_start(rec[b][:, :, :, :].rearrange("p k j f -> p k (j f)").bitcast(I32),
                                 slots[bass.ds(t * K + first, K), :, :].rearrange("s p f -> p s f")).then_inc(rec_in[b], 16)
                    if used(kk) or b == 2:
                        store(t - 2, (b - 2) % B)
            ring(sp, W, B, load)
            if kinds:
                store(W - 2, (W - 2) % B)
                store(W - 1, (W - 1) % B)
                for b in range(B):
                    sp.wait_ge(stored[b], 16 * ((W + B - 1 - b) // B))

        @block.tensor
        def _(pe):
            def step(t, b, kk):
                pe.wait_ge(in_[b], (kk + 1) * 32)
                start, stop = isinstance(t, int) and t == 0, isinstance(t, int) and t == W - 1
                for c, at in enumerate(chunks):
                    nc.tensor.matmul(ps[:, c, 0:at.stop - at.start], rows[b][:, :], cnt[b][:, at], start=start,
                                     stop=stop, skip_group_check=True).then_inc(summed, 1)
                    if kinds and c in (1, 3, 5):
                        q = c // 2
                        pe.wait_ge(hot_ready, (t * K + q + 1) * J)
                        if used(kk) or b or q:
                            pe.wait_ge(copied, t * K + q)
                        for j in range(J):
                            mm = nc.tensor.matmul(ps_turn[:, j * P:(j + 1) * P], hot[b][:, q, j, :], k.identb[:, :], start=True, stop=True)
                        mm.then_inc(turned, 1)
            ring(pe, W, B, step)

        @block.scalar
        def _(act):
            def step(t, b, kk):
                for q in range(K):
                    act.wait_ge(turned, t * K + q + 1)
                    if used(kk) and q == 0:
                        act.wait_ge(stored[b], kk * 16)
                    nc.scalar.copy(hotT[b][:, q, :], ps_turn[:, :]).then_inc(copied, 1)
            if kinds:
                ring(act, W, B, step)

        @block.vector
        def _(dve):
            def step(t, b, kk):
                dve.wait_ge(rec_in[b], (kk + 1) * 16)
                if used(kk):
                    dve.wait_ge(turned, (t - B + 1) * K)
                for q in range(K):
                    for j in range(J):
                        nc.vector.tensor_scalar(hot[b][:, q, j, :], k.typ[:, :], rec[b][:, q, j, 2:3], None, ALU.is_equal).then_inc(hot_ready, 1)
            if kinds:
                ring(dve, W, B, step)
            nc.vector.memset(total[:, N:NP], 0.0)
            for c, at in enumerate(chunks):
                n = at.stop - at.start
                dve.wait_ge(summed, (W - 1) * G + c + 1)
                if add is None:
                    nc.vector.tensor_copy(total[:, at], ps[:, c, 0:n])
                else:
                    nc.vector.tensor_tensor(total[:, at], ps[:, c, 0:n], add[:, at], ALU.add)


def mean_layer(nc, p, k, xT, aggT):
    G = -(-W // 4)
    with ExitStack() as ctx:
        m = Core(nc, ctx, "mean")
        wl = m.sb("wl", [D, D])
        wr = m.sb("wr", [D, D])
        bl = m.sb("bl", [P, D])
        br = m.sb("br", [P, D])
        rdeg = m.sb("rdeg", [P, W])
        y = m.sb("y", [P, NP])
        sq = m.sb("sq", [P, NP])
        s = m.sb("s", [P, W])
        ps = m.ps("ps", [P, 8, 512])
        params_in = m.sem("params_in")
        rdeg_ready = m.sem("rdeg_ready")
        multiplied = m.sem("multiplied")
        mean_ready = m.sem("mean_ready")
        group_ready = m.sem("group_ready")
        squares_ready = m.sem("squares_ready")
        root_ready = m.sem("root_ready")
        dve_step = m.sem("dve_step")
        block = ctx.enter_context(nc.Block())

        @block.sync
        def _(sp):
            sp.dma_start(wl[:, :], p['L1_gnn_Wl']).then_inc(params_in, 16)
            sp.dma_start(wr[:, :], p['L1_gnn_Wr']).then_inc(params_in, 16)
            sp.dma_start(bl[:, :], p['L1_gnn_bl'].partition_broadcast(P)).then_inc(params_in, 16)
            sp.dma_start(br[:, :], p['L1_gnn_br'].partition_broadcast(P)).then_inc(params_in, 16)

        @block.tensor
        def _(pe):
            pe.wait_ge(params_in, 64)
            for g in range(G):
                if g >= 4:
                    pe.wait_ge(group_ready, g - 3)
                for w in range(4 * g, min(4 * g + 4, W)):
                    at = slice((w % 4) * P, (w % 4 + 1) * P)
                    nc.tensor.matmul(ps[:, 2 * (g % 4), at], xT[:, w * P:(w + 1) * P], wl[:, :], start=True, stop=True)
                    mm = nc.tensor.matmul(ps[:, 2 * (g % 4) + 1, at], aggT[:, w * P:(w + 1) * P], wr[:, :], start=True, stop=True)
                mm.then_inc(multiplied, 1)

        @block.scalar
        def _(act):
            act.wait_ge(rdeg_ready, 1)
            for w in range(W):
                g = w // 4
                if w % 4 == 0:
                    act.wait_ge(multiplied, g + 1)
                nc.scalar.activation(y[:, w * P:(w + 1) * P], ps[:, 2 * (g % 4) + 1, (w % 4) * P:(w % 4 + 1) * P],
                                     ACT.Copy, scale=rdeg[:, w:w + 1]).then_inc(mean_ready, 1)
            act.wait_ge(squares_ready, 1)
            nc.scalar.activation(s[:, :], s[:, :], ACT.Sqrt).then_inc(root_ready, 1)

        @block.vector
        def _(dve):
            c = Chain(dve, dve_step)
            c.link(nc.vector.tensor_scalar(rdeg[:, :], k.degree[:, :], 1.0, None, ALU.max))
            nc.vector.reciprocal(rdeg[:, :], rdeg[:, :]).then_inc(rdeg_ready, 1)
            dve.wait_ge(params_in, 64)
            c.link(nc.vector.tensor_tensor(bl[:, :], bl[:, :], br[:, :], ALU.add))
            for g in range(G):
                n = min(4, W - 4 * g) * P
                dve.wait_ge(mean_ready, min(4 * g + 4, W))
                nc.vector.tensor_tensor(y[:, g * 512:g * 512 + n], y[:, g * 512:g * 512 + n], ps[:, 2 * (g % 4), 0:n],
                                        ALU.add).then_inc(group_ready, 1)
            dve.wait_ge(group_ready, G)
            y3 = y[:, :].rearrange("p (w f) -> p w f", f=D)
            c.link(nc.vector.tensor_tensor(y3, y3, bc(bl[:, None, :], [P, W, D]), ALU.add))
            c.link(nc.vector.tensor_scalar(y[:, :], y[:, :], 0.0, None, ALU.max))
            c.link(nc.vector.tensor_tensor(sq[:, :], y[:, :], y[:, :], ALU.mult))
            nc.vector.tensor_reduce(s[:, :], sq[:, :].rearrange("p (w f) -> p w f", f=D), AX.X, ALU.add).then_inc(squares_ready, 1)
            dve.wait_ge(root_ready, 1)
            c.link(nc.vector.tensor_scalar(s[:, :], s[:, :], 1e-6, None, ALU.add))
            c.link(nc.vector.reciprocal(s[:, :], s[:, :]))
            c.link(nc.vector.tensor_tensor(y3, y3, bc(s[:, :, None], [P, W, D]), ALU.mult))
            c.link(nc.vector.tensor_tensor(k.x[:, :], k.x[:, :], y[:, :], ALU.add))


def mlp(nc, p, k, layer, aggT, outT, nodes, table):
    G = -(-W // 4)
    with ExitStack() as ctx:
        m = Core(nc, ctx, f"mlp{layer}")
        w1 = m.sb("w1", [D, D])
        w2 = m.sb("w2", [D, D])
        b1 = m.sb("b1", [D, 1])
        b2 = m.sb("b2", [D, 1])
        hT = m.sb("hT", [P, NP])
        ps = m.ps("ps", [P, NCH, 512])
        params_in = m.sem("params_in")
        hidden_summed = m.sem("hidden_summed")
        hidden_ready = m.sem("hidden_ready")
        out_summed = m.sem("out_summed")
        out_ready = m.sem("out_ready")
        turned = m.sem("turned")
        nodes_ready = m.sem("nodes_ready")
        stored = m.sem("stored")
        block = ctx.enter_context(nc.Block())

        @block.sync
        def _(sp):
            sp.dma_start(w1[:, :], p['L2_gnn_W1'][layer, :, :]).then_inc(params_in, 16)
            sp.dma_start(w2[:, :], p['L2_gnn_W2'][layer, :, :]).then_inc(params_in, 16)
            sp.dma_start(b1[:, :], p['L2_gnn_b1'][layer, :].rearrange("(d a) -> d a", a=1)).then_inc(params_in, 16)
            sp.dma_start(b2[:, :], p['L2_gnn_b2'][layer, :].rearrange("(d a) -> d a", a=1)).then_inc(params_in, 16)
            if table is not None:
                sp.wait_ge(nodes_ready, G)
                sp.dma_start(table.rearrange("w p f -> p w f"), nodes[:, :].rearrange("p (w f) -> p w f", f=D)).then_inc(stored, 16)
                sp.wait_ge(stored, 16)

        @block.tensor
        def _(pe):
            pe.wait_ge(params_in, 64)
            for c in range(NCH):
                nc.tensor.matmul(ps[:, c, 0:CH], w1[:, :], aggT[:, c * CH:(c + 1) * CH], start=True, stop=True).then_inc(hidden_summed, 1)
            for c in range(NCH):
                pe.wait_ge(hidden_ready, c + 1)
                nc.tensor.matmul(ps[:, c, 0:CH], w2[:, :], hT[:, c * CH:(c + 1) * CH], start=True, stop=True).then_inc(out_summed, 1)
            pe.wait_ge(out_ready, NCH)
            for w in range(W):
                mm = nc.tensor.transpose(ps[:, w // 4, (w % 4) * P:(w % 4 + 1) * P], outT[:, w * P:(w + 1) * P], k.ident[:, :])
                if w % 4 == 3 or w == W - 1:
                    mm.then_inc(turned, 1)

        @block.scalar
        def _(act):
            act.wait_ge(params_in, 64)
            for c in range(NCH):
                act.wait_ge(hidden_summed, c + 1)
                nc.scalar.activation(hT[:, c * CH:(c + 1) * CH], ps[:, c, 0:CH], ACT.Relu, bias=b1[:, :]).then_inc(hidden_ready, 1)
            for c in range(NCH):
                act.wait_ge(out_summed, c + 1)
                nc.scalar.activation(outT[:, c * CH:(c + 1) * CH], ps[:, c, 0:CH], ACT.Relu, bias=b2[:, :]).then_inc(out_ready, 1)
            for g in range(G):
                n = min(4, W - 4 * g) * P
                act.wait_ge(turned, g + 1)
                nc.scalar.copy(nodes[:, g * 512:g * 512 + n], ps[:, g, 0:n]).then_inc(nodes_ready, 1)


def add_to_x(nc, k, y, tag, scale=1.0):
    with nc.Block() as block:
        @block.vector
        def _(dve):
            nc.vector.scalar_tensor_tensor(k.x[:, :], k.x[:, :], scale, y[:, :], ALU.mult, ALU.add)


def hop_left(nc, k, d, qw, nodes, aggT, table, scale):
    G = -(-W // 4)
    with ExitStack() as ctx:
        m = Core(nc, ctx, "left")
        leftT = m.sb("leftT", [P, NP])
        ps = m.ps("ps", [P, G, 512])
        turned = m.sem("turned")
        turned_copied = m.sem("turned_copied")
        summed = m.sem("summed")
        ready = m.sem("ready")
        stored = m.sem("stored")
        block = ctx.enter_context(nc.Block())
        groups = [slice(g * 512, min((g + 1) * 512, NP)) for g in range(G)]

        @block.tensor
        def _(pe):
            for g in range(G):
                for w in range(4 * g, min(4 * g + 4, W)):
                    mm = nc.tensor.transpose(ps[:, g, (w % 4) * P:(w % 4 + 1) * P], nodes[:, w * P:(w + 1) * P], k.ident[:, :])
                mm.then_inc(turned, 1)
            for g, at in enumerate(groups):
                pe.wait_ge(turned_copied, g + 1)
                nc.tensor.matmul(ps[:, g, 0:at.stop - at.start], qw[:, :], aggT[:, at], start=True, stop=True).then_inc(summed, 1)

        @block.scalar
        def _(act):
            for g, at in enumerate(groups):
                act.wait_ge(turned, g + 1)
                nc.scalar.copy(aggT[:, at], ps[:, g, 0:at.stop - at.start]).then_inc(turned_copied, 1)

        @block.vector
        def _(dve):
            if scale is not None:
                nc.vector.scalar_tensor_tensor(k.x[:, :], k.x[:, :], scale, nodes[:, :], ALU.mult, ALU.add)
            for g, at in enumerate(groups):
                dve.wait_ge(summed, g + 1)
                nc.vector.tensor_copy(leftT[:, at], ps[:, g, 0:at.stop - at.start]).then_inc(ready, 1)

        @block.sync
        def _(sp):
            sp.dma_start(d.left[W, :, :], k.zeros[:, :]).then_inc(stored, 16)
            if scale is not None:
                sp.dma_start(table.rearrange("w p f -> p w f"), nodes[:, :].rearrange("p (w f) -> p w f", f=D)).then_inc(stored, 16)
            for w0, w1 in ((0, 12), (12, W)):
                sp.wait_ge(ready, -(-w1 // 4))
                sp.dma_start(d.left[w0:w1, :, :].rearrange("w f n -> f w n"),
                             leftT[:, w0 * P:w1 * P].rearrange("f (w n) -> f w n", n=P)).then_inc(stored, 16)
            sp.wait_ge(stored, 64 if scale is not None else 48)


def relation_parts(nc, p, k, rel_hi_mid, rel_lo):
    with ExitStack() as ctx:
        m = Core(nc, ctx, "rel")
        t = m.sb("t", [P, D])
        hi = m.sb("hi", [P, D], BF16)
        r1 = m.sb("r1", [P, D])
        mid = m.sb("mid", [P, D], BF16)
        rel_in = m.sem("rel_in")
        dve_step = m.sem("dve_step")
        block = ctx.enter_context(nc.Block())

        @block.sync
        def _(sp):
            sp.dma_start(t[0:REL, :], p['L3_gnn_edge_emb']).then_inc(rel_in, 16)
            sp.dma_start(t[REL:P, :], p['L3_gnn_edge_emb']).then_inc(rel_in, 16)

        @block.vector
        def _(dve):
            c = Chain(dve, dve_step)
            dve.wait_ge(rel_in, 32)
            c.link(nc.vector.tensor_copy(hi[:, :], t[:, :]))
            c.link(nc.vector.tensor_tensor(r1[:, :], t[:, :], hi[:, :], ALU.subtract))
            c.link(nc.vector.tensor_copy(mid[:, :], r1[:, :]))
            c.link(nc.vector.tensor_copy(rel_hi_mid[0:REL, :], hi[0:REL, :]))
            c.link(nc.vector.tensor_copy(rel_hi_mid[REL:P, :], mid[REL:P, :]))
            c.link(nc.vector.tensor_tensor(r1[:, :], r1[:, :], mid[:, :], ALU.subtract))
            c.link(nc.vector.tensor_copy(rel_lo[:, :], r1[0:REL, :]))


def relation_hots(nc, d, k, u):
    with ExitStack() as ctx:
        m = Core(nc, ctx, "kinds")
        rec = m.sb("rec", [P, J, 4])
        hot = m.sb("hot", [P, J, P], BF16)
        hotT = m.sb("hotT", [P, S], BF16)
        ps = m.ps("ps", [P, S])
        rec_in = m.sem("rec_in")
        hot_ready = m.sem("hot_ready")
        turned = m.sem("turned")
        copied = m.sem("copied")
        stored = m.sem("stored")
        block = ctx.enter_context(nc.Block())
        slots = d.slots.rearrange("(s p j) f -> s p (j f)", p=P, j=J)

        @block.sync
        def _(sp):
            sp.dma_start(rec[:, :, :].rearrange("p j f -> p (j f)").bitcast(I32), slots[u, :, :]).then_inc(rec_in, 16)
            sp.wait_ge(copied, 1)
            sp.dma_start(d.type_hots[u, :, :], hotT[:, :]).then_inc(stored, 16)
            sp.wait_ge(stored, 16)

        @block.vector
        def _(dve):
            dve.wait_ge(rec_in, 16)
            for j in range(J):
                nc.vector.tensor_scalar(hot[:, j, :], k.typ[:, :], rec[:, j, 2:3], None, ALU.is_equal).then_inc(hot_ready, 1)

        @block.tensor
        def _(pe):
            pe.wait_ge(hot_ready, J)
            for j in range(J):
                mm = nc.tensor.matmul(ps[:, j * P:(j + 1) * P], hot[:, j, :], k.identb[:, :], start=True, stop=True)
            mm.then_inc(turned, 1)

        @block.scalar
        def _(act):
            act.wait_ge(turned, 1)
            nc.scalar.copy(hotT[:, :], ps[:, :]).then_inc(copied, 1)


def hop_edges(nc, d, k, kw, rel_hi_mid, rel_lo, table, result):
    MW = D + 1
    B = 6
    LAG = 4
    with ExitStack() as ctx:
        m = Core(nc, ctx, "hop")
        rec = [m.sb(f"rec{b}", [P, J, 4]) for b in range(6)]
        hotT = [m.sb(f"hotT{b}", [P, S], BF16) for b in range(6)]
        left = [m.sb(f"left{b}", [P, P]) for b in range(6)]
        tail_rows = [m.sb(f"tail_rows{b}", [P, J, D]) for b in range(6)]
        other = [m.sb(f"other{b}", [P, J, P], BF16) for b in range(3)]
        rt = [m.sb(f"rt{b}", [P, J, MW]) for b in range(6)]
        rtT = [m.sb(f"rtT{b}", [P, S]) for b in range(2)]
        right = [m.sb(f"right{b}", [P, S]) for b in range(2)]
        ex = [m.sb(f"ex{b}", [P, S]) for b in range(2)]
        exT = [m.sb(f"exT{b}", [P, S]) for b in range(2)]
        tile_max = [m.sb(f"tile_max{b}", [P, 1]) for b in range(2)]
        old_max = [m.sb(f"old_max{b}", [P, 1]) for b in range(2)]
        new_max = [m.sb(f"new_max{b}", [P, 1]) for b in range(2)]
        neg_max = [m.sb(f"neg_max{b}", [P, 1]) for b in range(2)]
        scale = [m.sb(f"scale{b}", [P, 1]) for b in range(3)]
        state = [m.sb(f"state{b}", [P, MW]) for b in range(3)]
        ps_rel = m.ps("ps_rel", [P, S])
        ps_rtT = m.ps("ps_rtT", [P, S])
        ps_right = m.ps("ps_right", [P, S])
        ps_logit = [m.ps(f"ps_logit{b}", [P, S]) for b in range(2)]
        ps_exT = m.ps("ps_exT", [P, S])
        ps_sum = [m.ps(f"ps_sum{b}", [P, S]) for b in range(2)]
        loads_in = [m.sem(f"loads_in{b}") for b in range(6)]
        rows_in = [m.sem(f"rows_in{b}", pool_dma=True) for b in range(6)]
        state_out = [m.sem(f"state_out{b}") for b in range(3)]
        issue = m.sem("issue")
        constants_set = m.sem("constants_set")
        other_ready = m.sem("other_ready")
        rel_ready = m.sem("rel_ready")
        rt_ready = m.sem("rt_ready")
        rt_turned = m.sem("rt_turned")
        rtT_ready = m.sem("rtT_ready")
        right_summed = m.sem("right_summed")
        right_ready = m.sem("right_ready")
        logits_ready = m.sem("logits_ready")
        tile_max_ready = m.sem("tile_max_ready")
        old_max_ready = m.sem("old_max_ready")
        new_max_ready = m.sem("new_max_ready")
        neg_max_ready = m.sem("neg_max_ready")
        ex_ready = m.sem("ex_ready")
        scale_ready = m.sem("scale_ready")
        ex_turned = m.sem("ex_turned")
        exT_ready = m.sem("exT_ready")
        messages_summed = m.sem("messages_summed")
        state_ready = m.sem("state_ready")
        block = ctx.enter_context(nc.Block())
        slots = d.slots.rearrange("(s p j) f -> s p (j f)", p=P, j=J)
        table_rows = table.rearrange("w p f -> (w p) f")

        @block.sync
        def _(sp):
            def load(s):
                b = s.slot(6)
                since(sp, other_ready, s, 6)
                since(sp, rt_ready, s, 6)
                sp.dma_start(rec[b][:, :, :].rearrange("p j f -> p (j f)").bitcast(I32),
                             slots[bass.ds(s.t, 1), :, :].rearrange("s p f -> p (s f)")).then_inc(loads_in[b], 16)
                since(sp, rel_ready, s, 6)
                sp.dma_start(hotT[b][:, :], d.type_hots[bass.ds(s.t, 1), :, :].rearrange("s p f -> p (s f)")).then_inc(loads_in[b], 16)
                since(sp, logits_ready, s, 6)
                w = sp.value_load(k.window_of[0:1, bass.ds(s.t, 1)], min_val=0, max_val=W)
                sp.dma_start(left[b][:, :], d.left[bass.ds(w, 1), :, :].rearrange("s p f -> p (s f)")).then_inc(loads_in[b], 16)

            def store(s):
                w = sp.value_load(k.window_of[0:1, bass.ds(s.t, 1)], min_val=0, max_val=W)
                last = sp.value_load(k.last_of[0:1, bass.ds(s.t, 1)], min_val=0, max_val=1)
                sp.wait_ge(state_ready, s.t + 1)
                sp.dma_start(d.state[bass.ds(w, 1), :, :].rearrange("s p f -> p (s f)"), state[s.slot(3)][:, :],
                             cond=last).then_inc(state_out[s.slot(3)], 16)

            def step(s):
                if s.exists(NST):
                    load(s)
                if s.lag(6).exists(NST):
                    store(s.lag(6))
            pipeline(sp, NST, 6, B, step)
            for b in range(3):
                sp.wait_ge(state_out[b], 16 * ((NST + 2 - b) // 3))

        @block.gpsimd
        def _(pool):
            def step(s):
                b = s.slot(6)
                pool.wait_ge(loads_in[b], (s.uses(6) + 1) * 48)
                pool.sem_inc(issue, 1)
                for j in range(J):
                    pool.indirect_dma_start(tail_rows[b][:, j, :], None, table_rows,
                                            bass.IndirectOffsetOnAxis(ap=rec[b][:, j, 3:4].bitcast(I32), axis=0)).then_inc(rows_in[b], 16)
            pipeline(pool, NST, 0, B, step)

        @block.tensor
        def _(pe):
            def turn_products(s):
                pe.wait_ge(rt_ready, s.t + 1)
                since(pe, rtT_ready, s, 1)
                for j in range(J):
                    mm = nc.tensor.transpose(ps_rtT[:, j * P:(j + 1) * P], rt[s.slot(6)][:, j, 0:D], k.ident[:, :])
                mm.then_inc(rt_turned, 1)

            def turn_weights(s):
                pe.wait_ge(ex_ready, s.t + 1)
                since(pe, exT_ready, s, 1)
                for j in range(J):
                    mm = nc.tensor.transpose(ps_exT[:, j * P:(j + 1) * P], ex[s.slot(2)][:, j * P:(j + 1) * P], k.ident[:, :])
                mm.then_inc(ex_turned, 1)

            def relations(s):
                pe.wait_ge(loads_in[s.slot(6)], (s.uses(6) + 1) * 48)
                since(pe, rt_ready, s, 1)
                hot = hotT[s.slot(6)]
                for j in range(J):
                    at = slice(j * P, (j + 1) * P)
                    nc.tensor.matmul(ps_rel[:, at], hot[:, at], rel_hi_mid[:, :], start=True, stop=False)
                    mm = nc.tensor.matmul(ps_rel[:, at], hot[0:REL, at], rel_lo[:, :], start=False, stop=True)
                mm.then_inc(rel_ready, 1)

            def rights(s):
                pe.wait_ge(rtT_ready, s.t + 1)
                since(pe, right_ready, s, 1)
                nc.tensor.matmul(ps_right[:, :], kw[:, :], rtT[s.slot(2)][:, :], start=True, stop=True).then_inc(right_summed, 1)

            def messages(s):
                pe.wait_ge(exT_ready, s.t + 1)
                since(pe, state_ready, s, 2)
                for j in range(J):
                    mm = nc.tensor.matmul(ps_sum[s.slot(2)][:, 0:MW], exT[s.slot(2)][:, j * P:(j + 1) * P],
                                          rt[s.slot(6)][:, j, :], start=(j == 0), stop=(j == J - 1))
                mm.then_inc(messages_summed, 1)

            def logits(s):
                pe.wait_ge(right_ready, s.t + 1)
                since(pe, ex_ready, s, 2)
                ps = ps_logit[s.slot(2)]
                nc.tensor.matmul(ps[:, :], left[s.slot(6)][:, :], right[s.slot(2)][:, :], start=True, stop=False,
                                 skip_group_check=True)
                pe.wait_ge(other_ready, s.t + 1)
                for j in range(J):
                    mm = nc.tensor.matmul(ps[:, j * P:(j + 1) * P], other[s.slot(3)][:, j, :], k.ident_neg[:, :], start=False,
                                          stop=(j == J - 1), skip_group_check=True)
                mm.then_inc(logits_ready, 1)

            def step(s):
                if s.lag(1).exists(NST):
                    turn_products(s.lag(1))
                if s.lag(4).exists(NST):
                    turn_weights(s.lag(4))
                if s.exists(NST):
                    relations(s)
                if s.lag(1).exists(NST):
                    rights(s.lag(1))
                if s.lag(4).exists(NST):
                    messages(s.lag(4))
                if s.lag(2).exists(NST):
                    logits(s.lag(2))
            pipeline(pe, NST, LAG, B, step)

        @block.scalar
        def _(act):
            def products(s):
                act.wait_ge(rt_turned, s.t + 1)
                since(act, right_summed, s, 2)
                nc.scalar.copy(rtT[s.slot(2)][:, :], ps_rtT[:, :]).then_inc(rtT_ready, 1)

            def weights(s):
                act.wait_ge(ex_turned, s.t + 1)
                since(act, messages_summed, s, 2)
                nc.scalar.copy(exT[s.slot(2)][:, :], ps_exT[:, :]).then_inc(exT_ready, 1)

            def exponentials(s):
                act.wait_ge(neg_max_ready, s.t + 1)
                since(act, ex_turned, s, 2)
                nc.scalar.activation(ex[s.slot(2)][:, :], ps_logit[s.slot(2)][:, :], ACT.Exp,
                                     bias=neg_max[s.slot(2)][:, :]).then_inc(ex_ready, 1)
                act.wait_ge(old_max_ready, s.t + 1)
                since(act, state_ready, s, 3)
                nc.scalar.activation(scale[s.slot(3)][:, :], old_max[s.slot(2)][:, :], ACT.Exp,
                                     bias=neg_max[s.slot(2)][:, :]).then_inc(scale_ready, 1)

            def tanh(s):
                act.wait_ge(right_summed, s.t + 1)
                since(act, logits_ready, s, 2)
                nc.scalar.activation(right[s.slot(2)][:, :], ps_right[:, :], ACT.Tanh).then_inc(right_ready, 1)

            def step(s):
                if s.lag(1).exists(NST):
                    products(s.lag(1))
                if s.lag(4).exists(NST):
                    weights(s.lag(4))
                if s.lag(3).exists(NST):
                    exponentials(s.lag(3))
                if s.lag(1).exists(NST):
                    tanh(s.lag(1))
            pipeline(act, NST, LAG, B, step)

        @block.vector
        def _(dve):
            for b in range(6):
                nc.vector.memset(rt[b][:, :, D:MW], 1.0).then_inc(constants_set, 1)
            nc.vector.memset(state[2][:, :], 0.0).then_inc(constants_set, 1)
            nc.vector.memset(new_max[1][:, :], -BIG).then_inc(constants_set, 1)
            dve.wait_ge(constants_set, 8)

            def maxima(s):
                b = s.slot(2)
                dve.wait_ge(logits_ready, s.t + 1)
                nc.vector.tensor_reduce(tile_max[b][:, :], ps_logit[b][:, :], AX.X, ALU.max).then_inc(tile_max_ready, 1)
                since(dve, scale_ready, s, 2)
                since(dve, new_max_ready, s, 1)
                cap = k.cap[:, bass.ds(s.t, 1)]
                nc.vector.tensor_tensor(old_max[b][:, :], new_max[1 - b][:, :], cap, ALU.min).then_inc(old_max_ready, 1)
                dve.wait_ge(tile_max_ready, s.t + 1)
                nc.vector.scalar_tensor_tensor(new_max[b][:, :], new_max[1 - b][:, :], cap, tile_max[b][:, :], ALU.min,
                                               ALU.max).then_inc(new_max_ready, 1)
                dve.wait_ge(new_max_ready, s.t + 1)
                nc.vector.tensor_scalar(neg_max[b][:, :], new_max[b][:, :], -1.0, BIG / 2, ALU.mult, ALU.min).then_inc(neg_max_ready, 1)

            def products(s):
                dve.wait_ge(rows_in[s.slot(6)], (s.uses(6) + 1) * 16 * J)
                dve.wait_ge(rel_ready, s.t + 1)
                since(dve, messages_summed, s, 6)
                nc.vector.tensor_tensor(rt[s.slot(6)][:, :, 0:D], tail_rows[s.slot(6)][:, :, :],
                                        ps_rel[:, :].rearrange("p (j f) -> p j f", f=D), ALU.mult).then_inc(rt_ready, 1)

            def states(s):
                b = s.slot(3)
                dve.wait_ge(messages_summed, s.t + 1)
                dve.wait_ge(scale_ready, s.t + 1)
                since(dve, state_ready, s, 1)
                if s.at_least(3):
                    dve.wait_ge(state_out[b], s.uses(3) * 16)
                nc.vector.scalar_tensor_tensor(state[b][:, :], state[(b - 1) % 3][:, :], scale[b][:, :], ps_sum[s.slot(2)][:, 0:MW],
                                               ALU.mult, ALU.add).then_inc(state_ready, 1)

            def masks(s):
                dve.wait_ge(loads_in[s.slot(6)], (s.uses(6) + 1) * 48)
                since(dve, logits_ready, s, 3)
                nc.vector.tensor_tensor(other[s.slot(3)][:, :, :], bc(k.node[:, None, :], [P, J, P]),
                                        bc(rec[s.slot(6)][:, :, 0:1], [P, J, P]), ALU.not_equal).then_inc(other_ready, 1)

            def step(s):
                if s.lag(3).exists(NST):
                    maxima(s.lag(3))
                if s.exists(NST):
                    products(s)
                    masks(s)
                if s.lag(4).exists(NST):
                    states(s.lag(4))
            pipeline(dve, NST, LAG, B, step)

    with ExitStack() as ctx:
        m = Core(nc, ctx, "hop_end")
        st = m.sb("st", [P, W, MW])
        r = m.sb("r", [P, W])
        cn = m.sb("cn", [P, W])
        sq = m.sb("sq", [P, NP])
        st_in = m.sem("st_in")
        dve_step = m.sem("dve_step")
        squares_ready = m.sem("squares_ready")
        root_ready = m.sem("root_ready")
        block = ctx.enter_context(nc.Block())
        y3 = result[:, :].rearrange("p (w f) -> p w f", f=D)

        @block.sync
        def _(sp):
            sp.dma_start(st[:, :, :], d.state[0:W, :, :].rearrange("w p f -> p w f")).then_inc(st_in, 16)

        @block.scalar
        def _(act):
            act.wait_ge(squares_ready, 1)
            nc.scalar.activation(r[:, :], r[:, :], ACT.Sqrt).then_inc(root_ready, 1)

        @block.vector
        def _(dve):
            c = Chain(dve, dve_step)
            dve.wait_ge(st_in, 16)
            c.link(nc.vector.tensor_scalar(r[:, :], st[:, :, D], 1e-30, None, ALU.max))
            c.link(nc.vector.tensor_scalar(cn[:, :], k.degree[:, :], 1.0, None, ALU.max))
            c.link(nc.vector.tensor_tensor(r[:, :], r[:, :], cn[:, :], ALU.mult))
            c.link(nc.vector.reciprocal(r[:, :], r[:, :]))
            c.link(nc.vector.tensor_tensor(y3, st[:, :, 0:D], bc(r[:, :, None], [P, W, D]), ALU.mult))
            c.link(nc.vector.tensor_tensor(sq[:, :], result[:, :], result[:, :], ALU.mult))
            nc.vector.tensor_reduce(r[:, :], sq[:, :].rearrange("p (w f) -> p w f", f=D), AX.X, ALU.add).then_inc(squares_ready, 1)
            dve.wait_ge(root_ready, 1)
            c.link(nc.vector.tensor_scalar(r[:, :], r[:, :], 1e-12, None, ALU.max))
            c.link(nc.vector.reciprocal(r[:, :], r[:, :]))
            nc.vector.tensor_tensor(y3, y3, bc(r[:, :, None], [P, W, D]), ALU.mult)


class Space:
    pass


def build(nc, p, out, debug=None):
    Core.ended = []
    with ExitStack() as ctx:
        m = Core(nc, ctx, "all")
        k, d = Space(), Space()
        k.ident = m.sb("ident", [P, P])
        k.identb = m.sb("identb", [P, P], BF16)
        k.ident_neg = m.sb("ident_neg", [P, P], BF16)
        k.tri = m.sb("tri", [P, P])
        k.node = m.sb("node", [P, P], BF16)
        k.typ = m.sb("typ", [P, P], BF16)
        k.steps = m.sb("steps", [P, NST + 1])
        k.part = m.sb("part", [P, 1])
        k.ones = m.sb("ones", [P, P])
        k.zeros = m.sb("zeros", [P, P])
        k.zerosb = m.sb("zerosb", [P, CH], BF16)
        k.window_of = m.sb("window_of", [P, NST], I32)
        k.last_of = m.sb("last_of", [P, NST], I32)
        k.cap = m.sb("cap", [P, NST])
        k.degree = m.sb("degree", [P, W])
        k.issue = m.sem("issue")
        d.slots = nc.dram_tensor("slots", (NST * S, 4), I32).ap()
        d.cum = nc.dram_tensor("cum", (W + 1, P, NC), F32).ap()
        d.cnt = nc.dram_tensor("cnt", (W, P, NC), F32).ap()
        d.cntT = nc.dram_tensor("cntT", (W, P, NP), F32).ap()
        zeros_set = m.sem("zeros_set")
        with nc.Block() as block:
            @block.vector
            def _(dve):
                nc.vector.memset(k.zeros[:, :], 0.0).then_inc(zeros_set, 1)
                nc.vector.memset(k.zerosb[:, :], 0.0).then_inc(zeros_set, 1)
        build_constants(nc, k)
        sort_edges(nc, p, d, k)
        count_pairs(nc, d, k)
        split_counts(nc, d, k)
        k.x = m.sb("x", [P, NP])
        k.LHS = 10 * (C + 1) + 2 * H
        k.col_s = m.sb("col_s", [P, W * H])
        k.col_d = m.sb("col_d", [P, W * H])
        k.amax = m.sb("amax", [P, W * H])
        d.lhs = nc.dram_tensor("lhs", (W, P, k.LHS), F32).ap()
        d.nodes = nc.dram_tensor("nodes", (W, P, D), F32).ap()
        d.left = nc.dram_tensor("left", (W + 1, P, P), F32).ap()
        d.type_hots = nc.dram_tensor("types", (NST, P, S), BF16).ap()
        d.state = nc.dram_tensor("state", (W + 1, P, D + 1), F32).ap()
        load_inputs(nc, p, k)
        with ExitStack() as inner:
            mm = Core(nc, inner, "att")
            row_d = mm.sb("row_d", [P, H, NP])
            with ExitStack() as deep:
                mm = Core(nc, deep, "att")
                row_s = mm.sb("row_s", [P, H, NP])
                with ExitStack() as deeper:
                    xT = Core(nc, deeper, "att").sb("xT", [P, NP])
                    turn(nc, k, k.x, xT, "turn_x")
                    attention_project(nc, p, d, k, xT, row_s, row_d)
                attention_max(nc, d, k, row_s)
            with ExitStack() as deep:
                mm = Core(nc, deep, "att")
                pos_row = mm.sb("pos_row", [P, H, 13 * P])
                neg_row = mm.sb("neg_row", [P, H, 13 * P])
                for w0, n in ((0, 13), (13, 12)):
                    pr, nr = pos_row[:, :, 0:n * P], neg_row[:, :, 0:n * P]
                    attention_rows(nc, k, row_d, pr, nr, w0, n)
                    attention_sum(nc, d, k, pr, nr, w0, n)
        layer_norm(nc, k, "norm0", table=d.nodes)
        with ExitStack() as inner:
            mm = Core(nc, inner, "graph")
            xT = mm.sb("xT", [P, NP])
            aggT = mm.sb("aggT", [P, NP])
            y = mm.sb("y", [P, NP])
            turn(nc, k, k.x, xT, "turn_1")
            aggregate(nc, d, k, d.nodes, d.cntT, aggT, "agg1", first=KINDS * K * W)
            mean_layer(nc, p, k, xT, aggT)
            layer_norm(nc, k, "norm1", table=d.nodes)
            turn(nc, k, k.x, xT, "turn_2")
            for layer in range(3):
                aggregate(nc, d, k, d.nodes, d.cnt, aggT, f"agg2{layer}", add=xT)
                mlp(nc, p, k, layer, aggT, xT, y, d.nodes if layer < 2 else None)
            add_to_x(nc, k, y, "add2")
            layer_norm(nc, k, "norm2", table=d.nodes)
            rel_hi_mid = mm.sb("rel_hi_mid", [P, D], BF16)
            rel_lo = mm.sb("rel_lo", [REL, D], BF16)
            qw = mm.sb("qw", [D, D])
            kw = mm.sb("kw", [D, D])
            relation_parts(nc, p, k, rel_hi_mid, rel_lo)
            for u in range((KINDS + 1) * K * W, NST):
                relation_hots(nc, d, k, u)
            hop_in = mm.sem("hop_in")
            with nc.Block() as block:
                @block.sync
                def _(sp):
                    sp.dma_start(qw[:, :], p['L3_gnn_q_w']).then_inc(hop_in, 16)
                    sp.dma_start(kw[:, :], p['L3_gnn_k_w']).then_inc(hop_in, 16)
                    sp.wait_ge(hop_in, 32)
            for hop in range(3):
                hop_left(nc, k, d, qw, y if hop else k.x, xT, d.nodes, (None, 4.0, 1.0)[hop])
                hop_edges(nc, d, k, kw, rel_hi_mid, rel_lo, d.nodes, y)
            add_to_x(nc, k, y, "add3")
        layer_norm(nc, k, "norm3", out=out)


INPUTS = ['x', 'src', 'dst', 'edge_type_64', 'L0_gnn_coeffs_t', 'L0_gnn_lin_weight', 'L0_gnn_lin_bias',
          'L0_gnn_att_src', 'L0_gnn_att_dst', 'L1_gnn_Wl', 'L1_gnn_bl', 'L1_gnn_Wr', 'L1_gnn_br', 'L2_gnn_W1',
          'L2_gnn_b1', 'L2_gnn_W2', 'L2_gnn_b2', 'L3_gnn_edge_emb', 'L3_gnn_q_w', 'L3_gnn_k_w']
DEBUG = {}


def kernel(**inputs):
    import numpy as np
    import concourse.bacc as bacc
    from concourse.bass_utils import run_bass_kernel_spmd as run

    nc = bacc.Bacc("TRN2", target_bir_lowering=False, num_devices=1)
    arrays, p = {}, {}
    for name in INPUTS:
        a = np.ascontiguousarray(inputs[name])
        arrays[f"in_{name}"] = a
        p[name] = nc.dram_tensor(f"in_{name}", a.shape, mybir.dt.from_np(a.dtype), kind="ExternalInput").ap()
    out = nc.dram_tensor("out_0", (N, D), F32, kind="ExternalOutput").ap()
    debug = {n: nc.dram_tensor(f"dbg_{n}", s, F32, kind="ExternalOutput").ap() for n, s in DEBUG.items()} or None
    build(nc, p, out, debug)
    r = run(nc, [arrays], core_ids=[0])
    return r.results[0]["out_0"]
```
